# Optimizing a Trainium2 kernel written in Bass

```python
import numpy as np
import jax
import jax.numpy as jnp

def _softmax(x, axis=-1):
    return jax.nn.softmax(x, axis=axis)

def _gelu(x):
    return jax.nn.gelu(x, approximate=True)

def _silu(x):
    return jax.nn.silu(x)

def _sigmoid(x):
    return jax.nn.sigmoid(x)

def _layernorm(x, axis=-1, eps=1e-05):
    m = jnp.mean(x, axis=axis, keepdims=True)
    v = jnp.var(x, axis=axis, keepdims=True)
    return (x - m) / jnp.sqrt(v + eps)

def _scatter_add(tgt, idx, src, axis=0):
    return tgt.at[idx].add(src)

def _segment_sum(src, seg, n):
    return jax.ops.segment_sum(src, seg, n)
kernel_name = 'mk_gps_d2_gnn_r32_0ab80f'

def setup_inputs(seed: int=0):
    np.random.seed(seed)
    _w = jnp.asarray

    def _rec_inputs():
        import jax
        import jax.numpy as jnp
        _gk = jax.random.key(seed)
        x = -0.0003713 + 1 * jax.random.normal(jax.random.fold_in(_gk, 1), (3125, 256), jnp.float32)
        src = jax.random.randint(jax.random.fold_in(_gk, 2), (50000,), 0, 3125, jnp.int32)
        dst = jax.random.randint(jax.random.fold_in(_gk, 3), (50000,), 0, 3125, jnp.int32)
        _o = jnp.argsort(dst, stable=True)
        src = src[_o]
        dst = dst[_o]
        return (x, src, dst)
    x, src, dst = _rec_inputs()

    def _L0_gnn_setup():
        import jax, jax.numpy as jnp
        import numpy as np
        N_NODES = 50000
        key = jax.random.key(seed)
        k1, k2, k3 = jax.random.split(key, 3)
        x = jax.random.normal(k1, (N_NODES, 256), dtype=jnp.float32)
        W = jax.random.normal(k2, (256, 256), dtype=jnp.float32) * (1.0 / np.sqrt(256))
        edge_index = jax.random.randint(k3, (2, 50000), 0, N_NODES, dtype=jnp.int64)
        return {'x': x, 'W': W, 'edge_index': edge_index}
    _L0_gnn_all = _L0_gnn_setup()
    _L0_gnn_in = {k: v for k, v in _L0_gnn_all.items() if k in ('W',)}
    del _L0_gnn_all

    def _L0_mix_setup():
        import jax, jax.numpy as jnp
        import numpy as np
        B, N, C = (8, 256, 256)
        HEADS, DH, KR = (8, 32, 4)
        INNER = HEADS * DH
        FF = 4 * C
        EPS = 1e-05

        def layernorm(x, g, b):
            mu = jnp.mean(x, axis=-1, keepdims=True)
            var = jnp.mean((x - mu) ** 2, axis=-1, keepdims=True)
            return (x - mu) * jax.lax.rsqrt(var + EPS) * g + b
        key = jax.random.key(seed)
        ks = jax.random.split(key, 16)
        s = 0.02
        return {'x': jax.random.normal(ks[0], (B, N, C), jnp.float32), 'ln1_g': jnp.ones((C,), jnp.float32), 'ln1_b': jnp.zeros((C,), jnp.float32), 'Wx': jax.random.normal(ks[1], (C, INNER), jnp.float32) * s, 'bx': jnp.zeros((INNER,), jnp.float32), 'Wq': jax.random.normal(ks[2], (DH, KR), jnp.float32) * s, 'Wk': jax.random.normal(ks[3], (DH, KR), jnp.float32) * s, 'Wv': jax.random.normal(ks[4], (DH, DH), jnp.float32) * s, 'Wo': jax.random.normal(ks[5], (INNER, C), jnp.float32) * s, 'bo': jnp.zeros((C,), jnp.float32), 'ln2_g': jnp.ones((C,), jnp.float32), 'ln2_b': jnp.zeros((C,), jnp.float32), 'W1': jax.random.normal(ks[6], (C, FF), jnp.float32) * s, 'b1': jnp.zeros((FF,), jnp.float32), 'W2': jax.random.normal(ks[7], (FF, C), jnp.float32) * s, 'b2': jnp.zeros((C,), jnp.float32)}
    _L0_mix_all = _L0_mix_setup()
    _L0_mix_in = {k: v for k, v in _L0_mix_all.items() if k in ('ln1_g', 'ln1_b', 'Wx', 'bx', 'Wq', 'Wk', 'Wv', 'Wo', 'bo', 'ln2_g', 'ln2_b', 'W1', 'b1', 'W2', 'b2')}
    del _L0_mix_all

    def _L0_ffn_setup():
        import jax, jax.numpy as jnp
        import numpy as np
        BN_EPS = 0.001

        def _bn(h, g, b, m, v):
            return g * (h - m) * jax.lax.rsqrt(v + BN_EPS) + b
        key = jax.random.key(seed)
        ks = jax.random.split(key, 8)
        B, F, Df = (256, 64, 256)
        E, H, D = (8, 256, 256)
        s1 = 1.0 / np.sqrt(Df)
        s2 = 1.0 / np.sqrt(H)
        return {'x': jax.random.normal(ks[0], (B, F, Df), jnp.float32), 'Wr': jax.random.normal(ks[1], (Df, E), jnp.float32) * s1, 'br': jnp.zeros((E,), jnp.float32), 'W1': jax.random.normal(ks[2], (E, Df, H), jnp.float32) * s1, 'b1': jnp.zeros((E, H), jnp.float32), 'g1': jnp.ones((E, H), jnp.float32), 'be1': jnp.zeros((E, H), jnp.float32), 'm1': jnp.zeros((E, H), jnp.float32), 'v1': jnp.ones((E, H), jnp.float32), 'W2': jax.random.normal(ks[3], (E, H, H), jnp.float32) * s2, 'b2': jnp.zeros((E, H), jnp.float32), 'g2': jnp.ones((E, H), jnp.float32), 'be2': jnp.zeros((E, H), jnp.float32), 'm2': jnp.zeros((E, H), jnp.float32), 'v2': jnp.ones((E, H), jnp.float32), 'Wo': jax.random.normal(ks[4], (E, H, D), jnp.float32) * s2, 'bo': jnp.zeros((E, D), jnp.float32)}
    _L0_ffn_all = _L0_ffn_setup()
    _L0_ffn_in = {k: v for k, v in _L0_ffn_all.items() if k in ('Wr', 'br', 'W1', 'b1', 'g1', 'be1', 'm1', 'v1', 'W2', 'b2', 'g2', 'be2', 'm2', 'v2', 'Wo', 'bo')}
    del _L0_ffn_all

    def _L1_gnn_setup():
        import jax, jax.numpy as jnp
        import numpy as np
        import math
        N_NODES = 50000
        N_EDGES = 50000
        C = 256
        H = 8
        HD = C // H

        def _layernorm(x, g, b, eps=1e-05):
            mu = jnp.mean(x, axis=-1, keepdims=True)
            var = jnp.mean(jnp.square(x - mu), axis=-1, keepdims=True)
            return (x - mu) * jax.lax.rsqrt(var + eps) * g + b
        key = jax.random.key(seed)
        ks = jax.random.split(key, 16)
        s = 0.02
        d = {'feat': jax.random.normal(ks[0], (N_NODES, C), jnp.float32), 'edge_src': jax.random.randint(ks[1], (N_EDGES,), 0, N_NODES), 'edge_dst': jax.random.randint(ks[2], (N_EDGES,), 0, N_NODES), 'Wq': jax.random.normal(ks[3], (C, C), jnp.float32) * s, 'bq': jnp.zeros((C,), jnp.float32), 'Wk': jax.random.normal(ks[4], (C, C), jnp.float32) * s, 'bk': jnp.zeros((C,), jnp.float32), 'Wv': jax.random.normal(ks[5], (C, C), jnp.float32) * s, 'bv': jnp.zeros((C,), jnp.float32), 'Wp': jax.random.normal(ks[6], (C, C), jnp.float32) * s, 'bp': jnp.zeros((C,), jnp.float32), 'ln_g': jnp.ones((C,), jnp.float32), 'ln_b': jnp.zeros((C,), jnp.float32), 'W1': jax.random.normal(ks[7], (4 * C, C), jnp.float32) * s, 'b1': jnp.zeros((4 * C,), jnp.float32), 'W2': jax.random.normal(ks[8], (C, 4 * C), jnp.float32) * s, 'b2': jnp.zeros((C,), jnp.float32)}
        return d
    _L1_gnn_all = _L1_gnn_setup()
    _L1_gnn_in = {k: v for k, v in _L1_gnn_all.items() if k in ('Wq', 'bq', 'Wk', 'bk', 'Wv', 'bv', 'Wp', 'bp', 'ln_g', 'ln_b', 'W1', 'b1', 'W2', 'b2')}
    del _L1_gnn_all

    def _L1_mix_setup():
        import jax, jax.numpy as jnp
        import numpy as np
        C_CURV = 1.0
        MIN_NORM = 1e-15
        BALL_EPS = 1e-05
        ATT_EPS = 1e-15
        DIM = 32

        def _norm(x):
            return jnp.clip(jnp.linalg.norm(x, axis=-1, keepdims=True), MIN_NORM)

        def proj(x, c):
            maxnorm = (1.0 - BALL_EPS) / jnp.sqrt(c)
            n = _norm(x)
            return jnp.where(n > maxnorm, x / n * maxnorm, x)

        def expmap0(u, c):
            sc = jnp.sqrt(c)
            n = _norm(u)
            return jnp.tanh(sc * n) * u / (sc * n)

        def logmap0(p, c):
            sc = jnp.sqrt(c)
            n = _norm(p)
            return jnp.arctanh(jnp.clip(sc * n, -1.0 + 1e-07, 1.0 - 1e-07)) * p / (sc * n)

        def mobius_add(x, y, c):
            x2 = jnp.sum(x * x, -1, keepdims=True)
            y2 = jnp.sum(y * y, -1, keepdims=True)
            xy = jnp.sum(x * y, -1, keepdims=True)
            num = (1 + 2 * c * xy + c * y2) * x + (1 - c * x2) * y
            den = 1 + 2 * c * xy + c * c * x2 * y2
            return num / jnp.clip(den, MIN_NORM)

        def conv1d(x, w, pad, groups=1):
            return jax.lax.conv_general_dilated(x, w, (1,), [(pad, pad)], dimension_numbers=('NCH', 'OIH', 'NCH'), feature_group_count=groups)

        def batchnorm(x, gamma, beta):
            mean = jnp.mean(x, axis=(0, 2), keepdims=True)
            var = jnp.var(x, axis=(0, 2), keepdims=True)
            xn = (x - mean) * jax.lax.rsqrt(var + 1e-05)
            return gamma[None, :, None] * xn + beta[None, :, None]

        def _reference_tuple_inner(x, w_qkv, bn_gamma, bn_beta, w_dw, w_pw, w_res, b_res):
            c = C_CURV
            h = logmap0(proj(x, c), c)
            h = jnp.transpose(h, (1, 2, 0))
            h = conv1d(h, w_qkv, pad=2)
            h = batchnorm(h, bn_gamma, bn_beta)
            h = jax.nn.relu(jnp.transpose(h, (2, 0, 1)))
            qkv = proj(expmap0(h, c), c)
            t = jnp.transpose(logmap0(proj(qkv, c), c), (1, 2, 0))
            s = conv1d(t, w_dw, pad=2, groups=t.shape[1])
            s = conv1d(s, w_pw, pad=0, groups=t.shape[1] // DIM)
            cat = jnp.concatenate([t, s], axis=1)
            ai = proj(expmap0(jnp.transpose(cat, (2, 0, 1)), c), c)
            t2 = logmap0(proj(ai, c), c)
            L, N, C2 = t2.shape
            g = C2 // (3 * DIM)
            qkv3 = jnp.transpose(t2, (1, 2, 0)).reshape(N, g, 3 * DIM, L)
            q, k, v = jnp.split(qkv3, 3, axis=2)
            q = jax.nn.relu(q)
            k = jax.nn.relu(k)
            vk = jnp.einsum('ngdl,ngel->ngde', v, k)
            out = jnp.einsum('ngde,ngdl->ngdl', vk, q)
            out = out / (jnp.sum(v, -1, keepdims=True) + ATT_EPS)
            out = jnp.transpose(out.reshape(N, g * DIM, L), (2, 0, 1))
            fx_h = proj(expmap0(out, c), c)
            ft = jnp.transpose(logmap0(proj(fx_h, c), c), (1, 2, 0))
            ft = conv1d(ft, w_res, pad=0) + b_res[None, :, None]
            fx = proj(expmap0(jnp.transpose(ft, (2, 0, 1)), c), c)
            residual = mobius_add(fx, x, c)
            return (fx, residual)
        key = jax.random.key(seed)
        ks = jax.random.split(key, 6)
        L, N, C, TD = (64, 16, 256, 256)
        x = jax.random.normal(ks[0], (L, N, C), jnp.float32) * 0.05
        w_qkv = jax.random.normal(ks[1], (3 * TD, C, 5), jnp.float32) / np.sqrt(C * 5)
        bn_gamma = jnp.ones((3 * TD,), jnp.float32)
        bn_beta = jnp.zeros((3 * TD,), jnp.float32)
        w_dw = jax.random.normal(ks[2], (3 * TD, 1, 5), jnp.float32) / np.sqrt(5.0)
        w_pw = jax.random.normal(ks[3], (3 * TD, DIM, 1), jnp.float32) / np.sqrt(DIM)
        w_res = jax.random.normal(ks[4], (C, 2 * TD, 1), jnp.float32) / np.sqrt(2 * TD)
        b_res = jnp.zeros((C,), jnp.float32)
        return {'x': x, 'w_qkv': w_qkv, 'bn_gamma': bn_gamma, 'bn_beta': bn_beta, 'w_dw': w_dw, 'w_pw': w_pw, 'w_res': w_res, 'b_res': b_res}
    _L1_mix_all = _L1_mix_setup()
    _L1_mix_in = {k: v for k, v in _L1_mix_all.items() if k in ('w_qkv', 'bn_gamma', 'bn_beta', 'w_dw', 'w_pw', 'w_res', 'b_res')}
    del _L1_mix_all

    def _L1_ffn_setup():
        import jax, jax.numpy as jnp
        import numpy as np
        B, S, D, F, E, K = (8, 64, 256, 1024, 8, 2)
        key = jax.random.key(seed)
        ks = jax.random.split(key, 10)
        s = 0.02
        return {'x': jax.random.normal(ks[0], (B, S, D), dtype=jnp.float32), 'Wr': jax.random.normal(ks[1], (D, E), dtype=jnp.float32) * s, 'W1s': jax.random.normal(ks[2], (D, F), dtype=jnp.float32) * s, 'b1s': jnp.zeros((F,), dtype=jnp.float32), 'W2s': jax.random.normal(ks[3], (F, D), dtype=jnp.float32) * s, 'b2s': jnp.zeros((D,), dtype=jnp.float32), 'W1p': jax.random.normal(ks[4], (E, D, F), dtype=jnp.float32) * s, 'b1p': jnp.zeros((E, F), dtype=jnp.float32), 'W2p': jax.random.normal(ks[5], (E, F, D), dtype=jnp.float32) * s, 'b2p': jnp.zeros((E, D), dtype=jnp.float32)}
    _L1_ffn_all = _L1_ffn_setup()
    _L1_ffn_in = {k: v for k, v in _L1_ffn_all.items() if k in ('Wr', 'W1s', 'b1s', 'W2s', 'b2s', 'W1p', 'b1p', 'W2p', 'b2p')}
    del _L1_ffn_all
    return {'x': x, 'src': src, 'dst': dst, 'L0_gnn_W': _L0_gnn_in['W'], 'L0_mix_ln1_g': _L0_mix_in['ln1_g'], 'L0_mix_ln1_b': _L0_mix_in['ln1_b'], 'L0_mix_Wx': _L0_mix_in['Wx'], 'L0_mix_bx': _L0_mix_in['bx'], 'L0_mix_Wq': _L0_mix_in['Wq'], 'L0_mix_Wk': _L0_mix_in['Wk'], 'L0_mix_Wv': _L0_mix_in['Wv'], 'L0_mix_Wo': _L0_mix_in['Wo'], 'L0_mix_bo': _L0_mix_in['bo'], 'L0_mix_ln2_g': _L0_mix_in['ln2_g'], 'L0_mix_ln2_b': _L0_mix_in['ln2_b'], 'L0_mix_W1': _L0_mix_in['W1'], 'L0_mix_b1': _L0_mix_in['b1'], 'L0_mix_W2': _L0_mix_in['W2'], 'L0_mix_b2': _L0_mix_in['b2'], 'L0_ffn_Wr': _L0_ffn_in['Wr'], 'L0_ffn_br': _L0_ffn_in['br'], 'L0_ffn_W1': _L0_ffn_in['W1'], 'L0_ffn_b1': _L0_ffn_in['b1'], 'L0_ffn_g1': _L0_ffn_in['g1'], 'L0_ffn_be1': _L0_ffn_in['be1'], 'L0_ffn_m1': _L0_ffn_in['m1'], 'L0_ffn_v1': _L0_ffn_in['v1'], 'L0_ffn_W2': _L0_ffn_in['W2'], 'L0_ffn_b2': _L0_ffn_in['b2'], 'L0_ffn_g2': _L0_ffn_in['g2'], 'L0_ffn_be2': _L0_ffn_in['be2'], 'L0_ffn_m2': _L0_ffn_in['m2'], 'L0_ffn_v2': _L0_ffn_in['v2'], 'L0_ffn_Wo': _L0_ffn_in['Wo'], 'L0_ffn_bo': _L0_ffn_in['bo'], 'L1_gnn_Wq': _L1_gnn_in['Wq'], 'L1_gnn_bq': _L1_gnn_in['bq'], 'L1_gnn_Wk': _L1_gnn_in['Wk'], 'L1_gnn_bk': _L1_gnn_in['bk'], 'L1_gnn_Wv': _L1_gnn_in['Wv'], 'L1_gnn_bv': _L1_gnn_in['bv'], 'L1_gnn_Wp': _L1_gnn_in['Wp'], 'L1_gnn_bp': _L1_gnn_in['bp'], 'L1_gnn_ln_g': _L1_gnn_in['ln_g'], 'L1_gnn_ln_b': _L1_gnn_in['ln_b'], 'L1_gnn_W1': _L1_gnn_in['W1'], 'L1_gnn_b1': _L1_gnn_in['b1'], 'L1_gnn_W2': _L1_gnn_in['W2'], 'L1_gnn_b2': _L1_gnn_in['b2'], 'L1_mix_w_qkv': _L1_mix_in['w_qkv'], 'L1_mix_bn_gamma': _L1_mix_in['bn_gamma'], 'L1_mix_bn_beta': _L1_mix_in['bn_beta'], 'L1_mix_w_dw': _L1_mix_in['w_dw'], 'L1_mix_w_pw': _L1_mix_in['w_pw'], 'L1_mix_w_res': _L1_mix_in['w_res'], 'L1_mix_b_res': _L1_mix_in['b_res'], 'L1_ffn_Wr': _L1_ffn_in['Wr'], 'L1_ffn_W1s': _L1_ffn_in['W1s'], 'L1_ffn_b1s': _L1_ffn_in['b1s'], 'L1_ffn_W2s': _L1_ffn_in['W2s'], 'L1_ffn_b2s': _L1_ffn_in['b2s'], 'L1_ffn_W1p': _L1_ffn_in['W1p'], 'L1_ffn_b1p': _L1_ffn_in['b1p'], 'L1_ffn_W2p': _L1_ffn_in['W2p'], 'L1_ffn_b2p': _L1_ffn_in['b2p']}

def reference(x, src, dst, L0_gnn_W, L0_mix_ln1_g, L0_mix_ln1_b, L0_mix_Wx, L0_mix_bx, L0_mix_Wq, L0_mix_Wk, L0_mix_Wv, L0_mix_Wo, L0_mix_bo, L0_mix_ln2_g, L0_mix_ln2_b, L0_mix_W1, L0_mix_b1, L0_mix_W2, L0_mix_b2, L0_ffn_Wr, L0_ffn_br, L0_ffn_W1, L0_ffn_b1, L0_ffn_g1, L0_ffn_be1, L0_ffn_m1, L0_ffn_v1, L0_ffn_W2, L0_ffn_b2, L0_ffn_g2, L0_ffn_be2, L0_ffn_m2, L0_ffn_v2, L0_ffn_Wo, L0_ffn_bo, L1_gnn_Wq, L1_gnn_bq, L1_gnn_Wk, L1_gnn_bk, L1_gnn_Wv, L1_gnn_bv, L1_gnn_Wp, L1_gnn_bp, L1_gnn_ln_g, L1_gnn_ln_b, L1_gnn_W1, L1_gnn_b1, L1_gnn_W2, L1_gnn_b2, L1_mix_w_qkv, L1_mix_bn_gamma, L1_mix_bn_beta, L1_mix_w_dw, L1_mix_w_pw, L1_mix_w_res, L1_mix_b_res, L1_ffn_Wr, L1_ffn_W1s, L1_ffn_b1s, L1_ffn_W2s, L1_ffn_b2s, L1_ffn_W1p, L1_ffn_b1p, L1_ffn_W2p, L1_ffn_b2p):
    import jax
    import jax.numpy as jnp

    def _L0_gnn_ref(x, W, edge_index):
        import jax, jax.numpy as jnp
        import numpy as np
        N_NODES = 50000
        N = x.shape[0]
        src, dst = (edge_index[0], edge_index[1])
        h = x @ W
        deg = jax.ops.segment_sum(jnp.ones_like(dst, dtype=h.dtype), dst, num_segments=N)
        deg_inv_sqrt = jnp.where(deg > 0, jax.lax.rsqrt(jnp.maximum(deg, 1)), 0.0)
        norm = deg_inv_sqrt[src] * deg_inv_sqrt[dst]
        msgs = h[src] * norm[:, None]
        out = jax.ops.segment_sum(msgs, dst, num_segments=N)
        return out

    def _L0_mix_ref(x, ln1_g, ln1_b, Wx, bx, Wq, Wk, Wv, Wo, bo, ln2_g, ln2_b, W1, b1, W2, b2):
        import jax, jax.numpy as jnp
        import numpy as np
        B, N, C = (8, 256, 256)
        HEADS, DH, KR = (8, 32, 4)
        INNER = HEADS * DH
        FF = 4 * C
        EPS = 1e-05

        def layernorm(x, g, b):
            mu = jnp.mean(x, axis=-1, keepdims=True)
            var = jnp.mean((x - mu) ** 2, axis=-1, keepdims=True)
            return (x - mu) * jax.lax.rsqrt(var + EPS) * g + b
        b, n, c = x.shape
        h = layernorm(x, ln1_g, ln1_b)
        xm = h @ Wx + bx
        xm = xm.reshape(b, n, HEADS, DH).transpose(0, 2, 1, 3)
        q = jax.nn.softmax(xm @ Wq, axis=-1)
        k = jax.nn.softmax(xm @ Wk, axis=-2)
        v = xm @ Wv
        kv = jnp.einsum('bhnr,bhnd->bhrd', k, v)
        qkv = jnp.einsum('bhnr,bhrd->bhnd', q, kv)
        attn = qkv.transpose(0, 2, 1, 3).reshape(b, n, INNER) @ Wo + bo
        fx = attn + x
        h2 = layernorm(fx, ln2_g, ln2_b)
        m = jax.nn.gelu(h2 @ W1 + b1, approximate=False) @ W2 + b2
        return m + fx

    def _L0_ffn_ref(x, Wr, br, W1, b1, g1, be1, m1, v1, W2, b2, g2, be2, m2, v2, Wo, bo):
        import jax, jax.numpy as jnp
        import numpy as np
        BN_EPS = 0.001

        def _bn(h, g, b, m, v):
            return g * (h - m) * jax.lax.rsqrt(v + BN_EPS) + b
        feat = jnp.mean(x, axis=0)
        w = jax.nn.softmax(feat @ Wr + br, axis=-1)
        h = jnp.einsum('bfd,edh->bfeh', x, W1) + b1
        h = jax.nn.relu(_bn(h, g1, be1, m1, v1))
        h = jnp.einsum('bfeh,ehk->bfek', h, W2) + b2
        h = jax.nn.relu(_bn(h, g2, be2, m2, v2))
        y = jnp.einsum('bfeh,ehd->bfed', h, Wo) + bo
        return jnp.einsum('bfed,fe->bfd', y, w)

    def _L1_gnn_ref(feat, edge_src, edge_dst, Wq, bq, Wk, bk, Wv, bv, Wp, bp, ln_g, ln_b, W1, b1, W2, b2):
        import jax, jax.numpy as jnp
        import numpy as np
        import math
        N_NODES = 50000
        N_EDGES = 50000
        C = 256
        H = 8
        HD = C // H

        def _layernorm(x, g, b, eps=1e-05):
            mu = jnp.mean(x, axis=-1, keepdims=True)
            var = jnp.mean(jnp.square(x - mu), axis=-1, keepdims=True)
            return (x - mu) * jax.lax.rsqrt(var + eps) * g + b
        n = feat.shape[0]
        q = (feat @ Wq.T + bq).reshape(n, H, HD)
        k = (feat @ Wk.T + bk).reshape(n, H, HD)
        v = (feat @ Wv.T + bv).reshape(n, H, HD)
        score = jnp.einsum('ehd,ehd->eh', q[edge_dst], k[edge_src])
        score = jnp.clip(score / math.sqrt(HD), -10.0, 10.0)
        smax = jax.ops.segment_max(score, edge_dst, num_segments=n)
        smax = jnp.where(jnp.isfinite(smax), smax, 0.0)
        ex = jnp.exp(score - smax[edge_dst])
        den = jax.ops.segment_sum(ex, edge_dst, num_segments=n)
        alpha = ex / den[edge_dst]
        wv = jax.ops.segment_sum(alpha[:, :, None] * v[edge_src], edge_dst, num_segments=n).reshape(n, C)
        y = wv @ Wp.T + bp
        x = feat + y
        h = _layernorm(x, ln_g, ln_b)
        h = jax.nn.gelu(h @ W1.T + b1, approximate=False) @ W2.T + b2
        return x + h

    def _L1_mix_ref(x, w_qkv, bn_gamma, bn_beta, w_dw, w_pw, w_res, b_res):
        import jax, jax.numpy as jnp
        import numpy as np
        C_CURV = 1.0
        MIN_NORM = 1e-15
        BALL_EPS = 1e-05
        ATT_EPS = 1e-15
        DIM = 32

        def _norm(x):
            return jnp.clip(jnp.linalg.norm(x, axis=-1, keepdims=True), MIN_NORM)

        def proj(x, c):
            maxnorm = (1.0 - BALL_EPS) / jnp.sqrt(c)
            n = _norm(x)
            return jnp.where(n > maxnorm, x / n * maxnorm, x)

        def expmap0(u, c):
            sc = jnp.sqrt(c)
            n = _norm(u)
            return jnp.tanh(sc * n) * u / (sc * n)

        def logmap0(p, c):
            sc = jnp.sqrt(c)
            n = _norm(p)
            return jnp.arctanh(jnp.clip(sc * n, -1.0 + 1e-07, 1.0 - 1e-07)) * p / (sc * n)

        def mobius_add(x, y, c):
            x2 = jnp.sum(x * x, -1, keepdims=True)
            y2 = jnp.sum(y * y, -1, keepdims=True)
            xy = jnp.sum(x * y, -1, keepdims=True)
            num = (1 + 2 * c * xy + c * y2) * x + (1 - c * x2) * y
            den = 1 + 2 * c * xy + c * c * x2 * y2
            return num / jnp.clip(den, MIN_NORM)

        def conv1d(x, w, pad, groups=1):
            return jax.lax.conv_general_dilated(x, w, (1,), [(pad, pad)], dimension_numbers=('NCH', 'OIH', 'NCH'), feature_group_count=groups)

        def batchnorm(x, gamma, beta):
            mean = jnp.mean(x, axis=(0, 2), keepdims=True)
            var = jnp.var(x, axis=(0, 2), keepdims=True)
            xn = (x - mean) * jax.lax.rsqrt(var + 1e-05)
            return gamma[None, :, None] * xn + beta[None, :, None]

        def _reference_tuple_inner(x, w_qkv, bn_gamma, bn_beta, w_dw, w_pw, w_res, b_res):
            c = C_CURV
            h = logmap0(proj(x, c), c)
            h = jnp.transpose(h, (1, 2, 0))
            h = conv1d(h, w_qkv, pad=2)
            h = batchnorm(h, bn_gamma, bn_beta)
            h = jax.nn.relu(jnp.transpose(h, (2, 0, 1)))
            qkv = proj(expmap0(h, c), c)
            t = jnp.transpose(logmap0(proj(qkv, c), c), (1, 2, 0))
            s = conv1d(t, w_dw, pad=2, groups=t.shape[1])
            s = conv1d(s, w_pw, pad=0, groups=t.shape[1] // DIM)
            cat = jnp.concatenate([t, s], axis=1)
            ai = proj(expmap0(jnp.transpose(cat, (2, 0, 1)), c), c)
            t2 = logmap0(proj(ai, c), c)
            L, N, C2 = t2.shape
            g = C2 // (3 * DIM)
            qkv3 = jnp.transpose(t2, (1, 2, 0)).reshape(N, g, 3 * DIM, L)
            q, k, v = jnp.split(qkv3, 3, axis=2)
            q = jax.nn.relu(q)
            k = jax.nn.relu(k)
            vk = jnp.einsum('ngdl,ngel->ngde', v, k)
            out = jnp.einsum('ngde,ngdl->ngdl', vk, q)
            out = out / (jnp.sum(v, -1, keepdims=True) + ATT_EPS)
            out = jnp.transpose(out.reshape(N, g * DIM, L), (2, 0, 1))
            fx_h = proj(expmap0(out, c), c)
            ft = jnp.transpose(logmap0(proj(fx_h, c), c), (1, 2, 0))
            ft = conv1d(ft, w_res, pad=0) + b_res[None, :, None]
            fx = proj(expmap0(jnp.transpose(ft, (2, 0, 1)), c), c)
            residual = mobius_add(fx, x, c)
            return (fx, residual)
        return _reference_tuple_inner(x, w_qkv, bn_gamma, bn_beta, w_dw, w_pw, w_res, b_res)[0]

    def _L1_ffn_ref(x, Wr, W1s, b1s, W2s, b2s, W1p, b1p, W2p, b2p):
        import jax, jax.numpy as jnp
        import numpy as np
        B, S, D, F, E, K = (8, 64, 256, 1024, 8, 2)
        gelu = lambda t: jax.nn.gelu(t, approximate=False)
        shared = gelu(x @ W1s + b1s) @ W2s + b2s
        rw = jax.nn.softmax(x @ Wr, axis=-1)
        topw, topi = jax.lax.top_k(rw, K)
        topw = topw / jnp.sum(topw, axis=-1, keepdims=True)
        mask = jnp.sum(jax.nn.one_hot(topi, E, dtype=topw.dtype) * topw[..., None], axis=-2)
        h = gelu(jnp.einsum('bsd,edf->bsef', x, W1p) + b1p)
        priv = jnp.einsum('bsef,efd->bsed', h, W2p) + b2p
        routed = jnp.einsum('bsed,bse->bsd', priv, mask)
        return shared + routed
    edge_index = jnp.stack([src, dst])
    xn = _layernorm(x, axis=-1)
    x = x + _L0_gnn_ref(xn, L0_gnn_W, edge_index) + _L0_mix_ref(xn[None], L0_mix_ln1_g, L0_mix_ln1_b, L0_mix_Wx, L0_mix_bx, L0_mix_Wq, L0_mix_Wk, L0_mix_Wv, L0_mix_Wo, L0_mix_bo, L0_mix_ln2_g, L0_mix_ln2_b, L0_mix_W1, L0_mix_b1, L0_mix_W2, L0_mix_b2)[0]
    x = x + _L0_ffn_ref(_layernorm(x, axis=-1)[None], L0_ffn_Wr, L0_ffn_br, L0_ffn_W1, L0_ffn_b1, L0_ffn_g1, L0_ffn_be1, L0_ffn_m1, L0_ffn_v1, L0_ffn_W2, L0_ffn_b2, L0_ffn_g2, L0_ffn_be2, L0_ffn_m2, L0_ffn_v2, L0_ffn_Wo, L0_ffn_bo)[0]
    xn = _layernorm(x, axis=-1)
    x = x + _L1_gnn_ref(xn, src, dst, L1_gnn_Wq, L1_gnn_bq, L1_gnn_Wk, L1_gnn_bk, L1_gnn_Wv, L1_gnn_bv, L1_gnn_Wp, L1_gnn_bp, L1_gnn_ln_g, L1_gnn_ln_b, L1_gnn_W1, L1_gnn_b1, L1_gnn_W2, L1_gnn_b2) + _L1_mix_ref(xn[None], L1_mix_w_qkv, L1_mix_bn_gamma, L1_mix_bn_beta, L1_mix_w_dw, L1_mix_w_pw, L1_mix_w_res, L1_mix_b_res)[0]
    x = x + _L1_ffn_ref(_layernorm(x, axis=-1)[None], L1_ffn_Wr, L1_ffn_W1s, L1_ffn_b1s, L1_ffn_W2s, L1_ffn_b2s, L1_ffn_W1p, L1_ffn_b1p, L1_ffn_W2p, L1_ffn_b2p)[0]
    return x

_drawn_inputs = setup_inputs


def setup_inputs(seed=0):
    import zlib

    import numpy as np

    out = dict(_drawn_inputs(seed))
    spreads = {'L0_mix_ln1_g': (1.0, 0.6),
     'L0_mix_ln1_b': (0.0, 0.8),
     'L0_mix_bx': (0.0, 0.8),
     'L0_mix_bo': (0.0, 0.562),
     'L0_mix_ln2_g': (1.0, 0.6),
     'L0_mix_ln2_b': (0.0, 2.0),
     'L0_mix_b1': (0.0, 1.363),
     'L0_mix_b2': (0.0, 0.549),
     'L0_ffn_br': (0.0, 0.447),
     'L0_ffn_b1': (0.0, 0.601),
     'L0_ffn_g1': (1.0, 0.591),
     'L0_ffn_be1': (0.0, 0.604),
     'L0_ffn_m1': (0.0, 0.593),
     'L0_ffn_v1': (1.0, 0.6),
     'L0_ffn_b2': (0.0, 0.436),
     'L0_ffn_g2': (1.0, 0.569),
     'L0_ffn_be2': (0.0, 1.7),
     'L0_ffn_m2': (0.0, 0.443),
     'L0_ffn_v2': (1.0, 0.6),
     'L0_ffn_bo': (0.0, 1.235),
     'L1_gnn_bq': (0.0, 0.8),
     'L1_gnn_bk': (0.0, 0.8),
     'L1_gnn_bv': (0.0, 0.717),
     'L1_gnn_bp': (0.0, 0.658),
     'L1_gnn_ln_g': (1.0, 0.6),
     'L1_gnn_ln_b': (0.0, 2.0),
     'L1_gnn_b1': (0.0, 0.651),
     'L1_gnn_b2': (0.0, 0.57),
     'L1_mix_bn_gamma': (1.0, 0.6),
     'L1_mix_bn_beta': (0.0, 2.0),
     'L1_mix_b_res': (0.0, 2.0),
     'L1_ffn_b1s': (0.0, 0.704),
     'L1_ffn_b2s': (0.0, 0.717),
     'L1_ffn_b1p': (0.0, 2.0),
     'L1_ffn_b2p': (0.0, 0.971)}
    factors = {'L0_mix_Wx': 8.0,
     'L0_mix_Wq': 8.0,
     'L0_mix_Wk': 8.0,
     'L0_mix_Wv': 8.0,
     'L0_mix_Wo': 8.0,
     'L1_gnn_Wq': 8.0,
     'L1_gnn_Wk': 8.0,
     'L1_gnn_Wv': 5.638,
     'L1_gnn_Wp': 3.688,
     'L1_mix_w_qkv': 25.432,
     'L1_mix_w_dw': 64.0,
     'L1_mix_w_pw': 64.0,
     'L1_mix_w_res': 23.184,
     'L1_ffn_W1s': 3.698,
     'L1_ffn_W1p': 5.267}
    for name, (base, spread) in spreads.items():
        noise = np.random.default_rng([zlib.crc32(name.encode()), seed]).standard_normal(out[name].shape)
        drawn = base * np.exp(spread * noise) if base else spread * noise
        out[name] = jnp.asarray(drawn.astype(out[name].dtype))
    for name, factor in factors.items():
        out[name] = (out[name] * factor).astype(out[name].dtype)
    return out
```

```python
from contextlib import ExitStack, contextmanager

import concourse.bass as bass
from concourse import mybir

F32 = mybir.dt.float32
BF16 = mybir.dt.bfloat16
I32 = mybir.dt.int32
ALU = mybir.AluOpType
ACT = mybir.ActivationFunctionType
AX_X = mybir.AxisListType.X

N = 3125
C = 256
CB = C // 128
R = 125
T = N // R
J = 5
CHUNKS = T // J
COLS = J * R
HALVES = ((0, 313), (313, 312))
E = 50000
G = E // (J * R)
ET = E // R
F = 4 * C
FB = F // 128
X8 = 8
HD = C // X8
KR = 4
EPS = 1e-5
AHEAD = 1
RNE = 12582912.0


class Chain:

    def __init__(self, eng, sem):
        self.eng, self.sem, self.base, self.n = eng, sem, 0, 0

    def link(self, ins):
        self.n += 1
        ins.then_inc(self.sem, 1)
        self.eng.wait_ge(self.sem, self.base + self.n)

    def done(self, sem):
        self.eng.sem_inc(sem, 1)

    def enter(self, i, steps):
        self.start, self.steps = self.n, steps
        self.base = i * steps

    def leave(self, trips):
        assert self.n - self.start == self.steps, self.n - self.start
        self.base = 0
        self.n = self.start + self.steps * trips


class Phase:

    def __init__(self, nc, name, stack):
        self.nc, self.name, self.stack, self.sems = nc, name, stack, []

    def sb(self, name, shape, dt=F32):
        return self.stack.enter_context(self.nc.sbuf_tensor(f"{self.name}_{name}", shape, dt))

    def ps(self, name, shape):
        return self.stack.enter_context(self.nc.psum_tensor(f"{self.name}_{name}", shape, F32))

    def sem(self, name):
        self.sems.append(self.nc.alloc_semaphore(f"{self.name}_{name}"))
        return self.sems[-1]

    def ahead(self, *sems):
        for sem in sems:
            self.nc.gpsimd.sem_inc(sem, AHEAD)


@contextmanager
def phase(nc, name):
    with ExitStack() as stack:
        ph = Phase(nc, name, stack)
        yield ph
        nc.clear_and_free_semaphores(ph.sems)
        nc.all_engine_barrier()


def repeat_last(ap, n):
    return ap.unsqueeze(len(ap.shape)).broadcast_to([*ap.shape, n])


def repeat_mid(ap, n):
    return ap.unsqueeze(1).broadcast_to([ap.shape[0], n, *ap.shape[1:]])


def constants(nc, m):
    with phase(nc, "cst") as ph:
        s_set, s_fill = ph.sem("set"), ph.sem("fill")
        with nc.Block() as block:

            @block.gpsimd
            def _(pool):
                pool.memset(m.ident[:, :], 0.0).then_inc(s_fill, 1)
                pool.memset(m.ones[:, :], 1.0).then_inc(s_set, 1)
                pool.memset(m.eps[:, :], EPS).then_inc(s_set, 1)
                pool.memset(m.before[:, :], 1.0).then_inc(s_fill, 1)
                pool.iota(m.row_no[:, :], pattern=[[1, R]], base=0, channel_multiplier=0,
                          allow_small_or_imprecise_dtypes=True).then_inc(s_set, 1)
                pool.iota(m.tile_starts[:, :], pattern=[[R, T - 1]], base=R, channel_multiplier=0,
                          allow_small_or_imprecise_dtypes=True).then_inc(s_set, 1)
                pool.wait_ge(s_fill, 2)
                pool.affine_select(out=m.ident[:, :], in_=m.ident[:, :], compare_op=ALU.not_equal, fill=1.0,
                                   base=0, pattern=[[-1, 128]], channel_multiplier=1).then_inc(s_set, 1)
                pool.affine_select(out=m.before[:, :], in_=m.before[:, :], compare_op=ALU.is_gt, fill=0.0,
                                   base=0, pattern=[[1, G]], channel_multiplier=-1).then_inc(s_set, 1)
                pool.wait_ge(s_set, 6)


def edge_tables(nc, m, src, dst):
    with phase(nc, "edg") as ph:
        raw = ph.sb("raw", [G, 2, J * R], I32)
        rawf = ph.sb("rawf", [G, 2, J * R])
        ends = ph.sb("ends", [G, 2])
        below = ph.sb("below", [G, 2, T - 1])
        span = ph.sb("span", [G, 2])
        last = ph.sb("last", [G, 2])
        tileno = ph.sb("tileno", [R, ET])
        rowno = ph.sb("rowno", [R, ET])
        tileb = ph.sb("tileb", [R, ET], BF16)
        rowb = ph.sb("rowb", [R, ET], BF16)
        nob = ph.sb("nob", [R, R], BF16)
        SET = 20
        hot_row = ph.sb("hot_row", [R, 2, SET, R], BF16)
        hot_tile = ph.sb("hot_tile", [R, 2, SET, T], BF16)
        turned = ph.ps("turned", [R, 2, 512])
        rows = ph.ps("rows", [1, 512])
        count = ph.ps("count", [R, 2, 512])
        s_in, s_f, s_turned, s_span, s_rows = (ph.sem(x) for x in ("in", "f", "turned", "span", "rows"))
        s_hot, s_count, s_v = ph.sem("hot"), ph.sem("count"), ph.sem("v")
        with nc.Block() as block:

            @block.sync
            def _(sp):
                sp.dma_start(raw[:, 0, :], dst.rearrange("(g e) -> g e", g=G)).then_inc(s_in, 16)
                sp.dma_start(raw[:, 1, :], src.rearrange("(g e) -> g e", g=G)).then_inc(s_in, 16)

            @block.vector
            def _(dve):
                v = Chain(dve, s_v)
                dve.wait_ge(s_in, 32)
                dve.tensor_copy(rawf[:, :, :], raw[:, :, :]).then_inc(s_f, 1)
                dve.wait_ge(s_f, 1)
                dve.tensor_reduce(ends[:, 0:1], rawf[:, 0, :], AX_X, ALU.min)
                v.link(dve.tensor_reduce(ends[:, 1:2], rawf[:, 0, :], AX_X, ALU.max))
                for k in range(2):
                    last_ins = dve.tensor_scalar(below[:, k, :], m.tile_starts[:, :], ends[:, k:k + 1], None, ALU.is_le)
                v.link(last_ins)
                v.link(dve.tensor_reduce(last[:, :], below[:, :, :], AX_X, ALU.add))
                dve.tensor_copy(span[:, 0:1], last[:, 0:1])
                v.link(dve.tensor_tensor(span[:, 1:2], last[:, 1:2], last[:, 0:1], ALU.subtract))
                dve.tensor_scalar(span[:, 1:2], span[:, 1:2], 1.0, None, ALU.add).then_inc(s_span, 1)
                dve.wait_ge(s_turned, 1)
                dve.tensor_copy(m.edge_dst[:, :, :],
                                turned[:, 0, 0:J * G].rearrange("p (j g) -> p g j", j=J))
                v.link(dve.tensor_copy(m.edge_dsti[:, 0:G, :],
                                       turned[:, 0, 0:J * G].rearrange("p (j g) -> p g j", j=J)))
                v.link(dve.tensor_copy(m.edge_src[:, 0:G, :],
                                       turned[:, 1, 0:J * G].rearrange("p (j g) -> p g j", j=J)))
                dve.wait_ge(s_rows, 1)
                v.link(dve.tensor_copy(m.group_table[:, :], rows[:, 0:3 * G]))
                flat = m.edge_dst[:, :, :].rearrange("p g j -> p (g j)")
                v.link(dve.tensor_scalar(tileno[:, :], flat, 1.0 / R, 0.5 / R - 0.5, ALU.mult, ALU.add))
                v.link(dve.tensor_scalar(tileno[:, :], tileno[:, :], RNE, RNE, ALU.add, ALU.subtract))
                v.link(dve.scalar_tensor_tensor(out=rowno[:, :], in0=tileno[:, :], scalar=-float(R), in1=flat,
                                                op0=ALU.mult, op1=ALU.add))
                dve.tensor_copy(tileb[:, :], tileno[:, :])
                dve.tensor_copy(rowb[:, :], rowno[:, :])
                dve.tensor_copy(nob[:, :], m.row_no[0:R, :])
                v.link(dve.memset(m.degree[:, :], 0.0))
                steps = 6
                with dve.Fori(0, ET // SET // 2) as i:
                    v.enter(i, 2)
                    for s in range(2):
                        at = i * (2 * SET) + s * SET
                        dve.tensor_tensor(hot_row[:, s, :, :], repeat_mid(nob[:, :], SET),
                                          repeat_last(rowb[:, bass.ds(at, SET)], R), ALU.is_equal)
                        dve.tensor_tensor(hot_tile[:, s, :, :], repeat_mid(nob[:, 0:T], SET),
                                          repeat_last(tileb[:, bass.ds(at, SET)], T),
                                          ALU.is_equal).then_inc(s_hot, 1)
                    for s in range(2):
                        dve.wait_ge(s_count, i * 2 + (s + 1))
                        v.link(dve.tensor_tensor(m.degree[:, :], m.degree[:, :], count[:, s, 0:T], ALU.add))
                v.leave(ET // SET // 2)
                v.link(dve.tensor_scalar(m.degree_s[:, 0, :], m.degree[:, :], 1.0, None, ALU.max))
                dve.tensor_scalar(m.degree_s[:, 1, :], m.degree[:, :], 1.0, None, ALU.min).then_inc(s_span, 1)
                dve.wait_ge(s_rows, 2)
                v.link(dve.reciprocal(m.degree_s[:, 0, :], m.degree_s[:, 0, :]))
                v.link(dve.tensor_tensor(m.inv_sqrt_degree[:, :], m.degree_s[:, 0, :], m.degree_s[:, 1, :], ALU.mult))

            @block.scalar
            def _(act):
                act.wait_ge(s_span, 2)
                act.activation(m.degree_s[:, 0, :], m.degree_s[:, 0, :], ACT.Sqrt).then_inc(s_rows, 1)

            @block.tensor
            def _(pe):
                pe.wait_ge(s_f, 1)
                for k in range(2):
                    for j in range(J):
                        last_ins = pe.transpose(turned[:, k, j * G:(j + 1) * G], rawf[:, k, j * R:(j + 1) * R],
                                                m.ident[0:G, 0:G])
                last_ins.then_inc(s_turned, 1)
                pe.wait_ge(s_span, 1)
                pe.matmul(rows[:, 0:G], span[:, 0:1], m.ident[0:G, 0:G], start=True, stop=True)
                pe.matmul(rows[:, G:2 * G], span[:, 1:2], m.ident[0:G, 0:G], start=True, stop=True)
                pe.matmul(rows[:, 2 * G:3 * G], span[:, 1:2], m.before[:, :], start=True, stop=True)\
                    .then_inc(s_rows, 1)
                with pe.Fori(0, ET // SET // 2) as i:
                    for s in range(2):
                        pe.wait_ge(s_hot, i * 2 + (s + 1))
                        for k in range(SET):
                            last_ins = pe.matmul(count[:, s, 0:T], hot_row[:, s, k, :], hot_tile[:, s, k, :],
                                                 start=(k == 0), stop=(k == SET - 1))
                        last_ins.then_inc(s_count, 1)


def join_stats(v, stats, mv):
    dve = v.eng
    a_mean, b_mean = stats[:, :, 1], stats[:, :, 4]
    v.link(dve.tensor_tensor(mv[:, 0, :], a_mean, b_mean, ALU.subtract))
    v.link(dve.scalar_tensor_tensor(out=mv[:, 1, :], in0=mv[:, 0, :], scalar=C / 4.0, in1=mv[:, 0, :],
                                    op0=ALU.mult, op1=ALU.mult))
    v.link(dve.tensor_tensor(mv[:, 1, :], mv[:, 1, :], stats[:, :, 2], ALU.add))
    v.link(dve.tensor_tensor(mv[:, 1, :], mv[:, 1, :], stats[:, :, 5], ALU.add))
    v.link(dve.tensor_tensor(mv[:, 0, :], a_mean, b_mean, ALU.add))
    v.link(dve.tensor_scalar(mv[:, 0, :], mv[:, 0, :], 0.5, None, ALU.mult))
    v.link(dve.tensor_scalar(mv[:, 1, :], mv[:, 1, :], 1.0 / C, None, ALU.mult))


def layernorm(nc, m, name, source, rows_out, cols):
    with phase(nc, name) as ph:
        stats = ph.sb("stats", [R, T, 6])
        mv = ph.sb("mv", [R, 2, T])
        sd = ph.sb("sd", [R, T])
        normed = ph.sb("normed", [R, J, C])
        turned = ph.ps("turned", [128, J, 512])
        s_stats, s_mv, s_sd, s_v = (ph.sem(x) for x in ("stats", "mv", "sd", "v"))
        s_normed, s_turned, s_free, s_done, s_rows = (ph.sem(x) for x in ("normed", "turned", "free", "done", "rows"))
        with nc.Block() as block:

            @block.vector
            def _(dve):
                v = Chain(dve, s_v)
                with dve.Fori(0, T) as t:
                    dve.bn_stats(stats[:, t, :], source[:, t, :]).then_inc(s_stats, 1)
                dve.wait_ge(s_stats, T)
                join_stats(v, stats, mv)
                v.done(s_mv)
                dve.wait_ge(s_sd, 1)
                v.link(dve.reciprocal(sd[:, :], sd[:, :]))
                with dve.Fori(0, CHUNKS) as c:
                    for j in range(J):
                        dve.wait_ge(s_free, c * J + (j + 1))
                        dve.tensor_scalar(normed[:, j, :], source[:, c * J + j, :], mv[:, 0, bass.ds(c * J + j, 1)],
                                          sd[:, bass.ds(c * J + j, 1)], ALU.subtract, ALU.mult).then_inc(s_normed, 1)

            @block.gpsimd
            def _(pool):
                if rows_out is not None:
                    with pool.Fori(0, CHUNKS) as c:
                        for j in range(J):
                            pool.wait_ge(s_normed, c * J + (j + 1))
                            pool.tensor_copy(rows_out[:, c * J + j, :], normed[:, j, :]).then_inc(s_rows, 1)

            @block.scalar
            def _(act):
                act.wait_ge(s_mv, 1)
                act.activation(sd[:, :], mv[:, 1, :], ACT.Sqrt, bias=m.eps[0:R, :]).then_inc(s_sd, 1)
                act.sem_inc(s_free, J)
                with act.Fori(0, CHUNKS) as c:
                    for j in range(J):
                        act.wait_ge(s_turned, c * J + (j + 1))
                        at = c * COLS + j * R
                        n = 0
                        for target, gain, shift in cols:
                            if gain is None:
                                ins = act.activation(target[:, :, bass.ds(at, R)],
                                                     turned[:, j, 0:CB * R].rearrange("p (b r) -> p b r", b=CB),
                                                     ACT.Copy)
                            else:
                                for b in range(CB):
                                    ins = act.activation(target[:, b, bass.ds(at, R)], turned[:, j, b * R:(b + 1) * R],
                                                         ACT.Identity, bias=shift[:, b:b + 1], scale=gain[:, b:b + 1])
                        ins.then_inc(s_done, 1)
                        if rows_out is not None:
                            act.wait_ge(s_rows, c * J + (j + 1))
                        act.wait_ge(s_done, c * J + (j + 1))
                        act.sem_inc(s_free, 1)

            @block.tensor
            def _(pe):
                with pe.Fori(0, CHUNKS) as c:
                    for j in range(J):
                        pe.wait_ge(s_normed, c * J + (j + 1))
                        for b in range(CB):
                            ins = pe.transpose(turned[:, j, b * R:(b + 1) * R], normed[:, j, b * 128:(b + 1) * 128],
                                               m.ident[0:R, 0:R])
                        ins.then_inc(s_turned, 1)


def scaled_rows(nc, m, W):
    with phase(nc, "hs") as ph:
        w = ph.sb("w", [128, CB, C])
        zc = ph.sb("zc", [128, CB, COLS])
        out = ph.sb("out", [R, J, C])
        prod = ph.ps("prod", [R, J, 512])
        s_w, s_zc, s_prod, s_out, s_stored = (ph.sem(x) for x in ("w", "zc", "prod", "out", "stored"))
        ph.ahead(s_out, s_prod, s_stored)
        with nc.Block() as block:

            @block.sync
            def _(sp):
                sp.dma_start(w[:, :, :], W.rearrange("(b p) n -> p b n", p=128)).then_inc(s_w, 16)
                with sp.Fori(0, CHUNKS) as c:
                    sp.wait_ge(s_out, (c + 1) * J + AHEAD)
                    sp.dma_start(m.gather0.rearrange("(t p) n -> p t n", p=R)[:, bass.ds(c * J, J), :],
                                 out[:, :, :]).then_inc(s_stored, 16)
                sp.wait_ge(s_stored, 16 * CHUNKS + AHEAD)

            @block.scalar
            def _(act):
                with act.Fori(0, CHUNKS) as c:
                    act.wait_ge(s_prod, c * J + AHEAD)
                    act.activation(zc[:, :, :], m.z_cols[:, :, bass.ds(c * COLS, COLS)], ACT.Copy).then_inc(s_zc, 1)

            @block.tensor
            def _(pe):
                pe.wait_ge(s_w, 16)
                with pe.Fori(0, CHUNKS) as c:
                    pe.wait_ge(s_zc, c + 1)
                    pe.wait_ge(s_out, c * J + AHEAD)
                    for j in range(J):
                        for b in range(CB):
                            ins = pe.matmul(prod[:, j, 0:C], zc[:, b, j * R:(j + 1) * R], w[:, b, :],
                                            start=(b == 0), stop=(b == CB - 1))
                        ins.then_inc(s_prod, 1)

            @block.vector
            def _(dve):
                with dve.Fori(0, CHUNKS) as c:
                    dve.wait_ge(s_stored, c * 16 + AHEAD)
                    for j in range(J):
                        dve.wait_ge(s_prod, c * J + (j + 1) + AHEAD)
                        dve.tensor_scalar(out[:, j, :], prod[:, j, 0:C],
                                          m.inv_sqrt_degree[:, bass.ds(c * J + j, 1)], None, ALU.mult)\
                            .then_inc(s_out, 1)


def message_sum(nc, m):
    with phase(nc, "ms") as ph:
        index = ph.sb("index", [R, 2, J], I32)
        got = ph.sb("got", [R, 2, J, C])
        hot = ph.sb("hot", [R, J, R])
        node_no = ph.sb("node_no", [R, N])
        s_node = ph.sem("node")
        summed = ph.sb("summed", [R, T, C])
        total = ph.ps("total", [R, 512])
        s_index, s_got = ph.sem("index"), [ph.sem(f"got{s}") for s in range(2)]
        s_hot, s_total, s_added, s_group, s_zero = (ph.sem(x) for x in ("hot", "total", "added", "group", "zero"))
        s_pace = ph.sem("pace")
        with nc.Block() as block:

            def bounds(eng, g):
                first = eng.value_load(m.group_table[0:1, bass.ds(g, 1)], min_val=0, max_val=T - 1)
                count = eng.value_load(m.group_table[0:1, bass.ds(g + G, 1)], min_val=1, max_val=T)
                before = eng.value_load(m.group_table[0:1, bass.ds(g + 2 * G, 1)], min_val=0, max_val=T * G)
                return first, count, before

            @block.gpsimd
            def _(pool):
                pool.iota(node_no[:, :], pattern=[[1, N]], base=0, channel_multiplier=0,
                          allow_small_or_imprecise_dtypes=True).then_inc(s_node, 1)
                with pool.Fori(0, G // 2) as i:
                    for s in range(2):
                        pool.wait_ge(s_index, i * 2 + (s + 1))
                        pool.sem_inc(s_pace, 1)
                        for j in range(J):
                            pool.indirect_dma_start(
                                out=got[:, s, j, :], out_offset=None, in_=m.gather0,
                                in_offset=bass.IndirectOffsetOnAxis(ap=index[:, s, j:j + 1], axis=0)
                            ).then_inc(s_got[s], 16)

            @block.vector
            def _(dve):
                dve.memset(summed[:, :, :], 0.0).then_inc(s_zero, 1)
                dve.wait_ge(s_zero, 1)
                dve.wait_ge(s_node, 1)
                for s in range(2):
                    dve.tensor_copy(index[:, s, :], m.edge_src[:, s, :]).then_inc(s_index, 1)
                with dve.Fori(0, G // 2) as i:
                    for s in range(2):
                        g = i * 2 + s
                        first, count, before = bounds(dve, g)
                        with dve.Fori(0, count) as k:
                            tile = dve.snap(nc.s_assert_within(first + k, 0, T - 1))
                            dve.tensor_tensor(hot[:, :, :],
                                              repeat_mid(node_no[:, bass.ds(tile * R, R)], J),
                                              repeat_last(m.edge_dst[:, g, :], R), ALU.is_equal).then_inc(s_hot, 1)
                            dve.wait_ge(s_total, before + k + 1)
                            dve.tensor_tensor(summed[:, tile, :], summed[:, tile, :], total[:, 0:C],
                                              ALU.add).then_inc(s_added, 1)
                            dve.wait_ge(s_added, before + k + 1)
                        dve.wait_ge(s_got[s], (i + 1) * (16 * J))
                        nxt = m.edge_src[:, bass.ds(g + 2, 1), :].rearrange("p a j -> p (a j)")
                        dve.tensor_copy(index[:, s, :], nxt).then_inc(s_index, 1)
                with dve.Fori(0, T) as t:
                    dve.scalar_tensor_tensor(out=m.x[:, t, :], in0=summed[:, t, :],
                                             scalar=m.inv_sqrt_degree[:, bass.ds(t, 1)], in1=m.x[:, t, :],
                                             op0=ALU.mult, op1=ALU.add).then_inc(s_zero, 1)

            @block.tensor
            def _(pe):
                with pe.Fori(0, G // 2) as i:
                    for s in range(2):
                        g = i * 2 + s
                        first, count, before = bounds(pe, g)
                        pe.wait_ge(s_got[s], (i + 1) * (16 * J))
                        pe.sem_inc(s_pace, 1)
                        with pe.Fori(0, count) as k:
                            pe.wait_ge(s_hot, before + k + 1)
                            for j in range(J):
                                ins = pe.matmul(total[:, 0:C], hot[:, j, :], got[:, s, j, :],
                                                start=(j == 0), stop=(j == J - 1))
                            ins.then_inc(s_total, 1)


def load_vectors(nc, m, a):
    plan, at = [], 0
    blocks = {}
    for name in ("L0_mix_ln1_g", "L0_mix_ln1_b", "L0_mix_bx", "L0_mix_ln2_g", "L0_mix_ln2_b", "L0_mix_b1",
                 "L0_ffn_b1", "L0_ffn_g1", "L0_ffn_be1", "L0_ffn_m1", "L0_ffn_v1",
                 "L0_ffn_b2", "L0_ffn_g2", "L0_ffn_be2", "L0_ffn_m2", "L0_ffn_v2",
                 "L1_gnn_ln_g", "L1_gnn_ln_b", "L1_gnn_b1", "L1_mix_bn_gamma", "L1_mix_bn_beta",
                 "L1_mix_w_dw", "L1_ffn_b1s", "L1_ffn_b1p"):
        ap = a[name]
        if name == "L1_mix_w_dw":
            ap = ap.rearrange("c a k -> (c a) k")[:, 2:3].rearrange("(b p) k -> b (p k)", p=128)
        elif len(ap.shape) == 2:
            ap = ap.rearrange("e (b p) -> (e b) p", p=128)
        else:
            ap = ap.rearrange("(b p) -> b p", p=128)
        n = ap.shape[0]
        blocks[name] = (at, n)
        done = 0
        while done < n:
            k = min(n - done, 128 - at % 128)
            plan.append((at // 128, at % 128, k, ap[done:done + k, :]))
            at += k
            done += k
    total = -(-at // 128)
    rows = [("L0_mix_bo", C), ("L0_mix_b2", C), ("L0_ffn_br", X8), ("L1_gnn_bq", C), ("L1_gnn_bk", C),
            ("L1_gnn_bv", C), ("L1_gnn_bp", C), ("L1_gnn_b2", C), ("L1_mix_b_res", C), ("L1_ffn_b2s", C)]
    with phase(nc, "vec") as ph:
        stack = ph.sb("stack", [128, total, 128])
        turned = ph.ps("turned", [128, total, 128])
        s_in, s_row, s_turned, s_zero = ph.sem("in"), ph.sem("row"), ph.sem("turned"), ph.sem("zero")
        with nc.Block() as block:

            @block.sync
            def _(sp):
                sp.wait_ge(s_zero, 1)
                for b, p, k, ap in plan:
                    sp.dma_start(stack[p:p + k, b, :], ap, allow_slow_non_contiguous=True).then_inc(s_in, 16)
                for i, (name, n) in enumerate(rows):
                    sp.dma_start(m.rowvec[:, i, 0:n], a[name].unsqueeze(0).broadcast_to([R, n])).then_inc(s_row, 16)
                sp.wait_ge(s_row, 16 * len(rows))

            @block.tensor
            def _(pe):
                pe.wait_ge(s_in, 16 * len(plan))
                for b in range(total):
                    ins = pe.transpose(turned[:, b, :], stack[:, b, :], m.ident[:, :])
                ins.then_inc(s_turned, 1)

            @block.vector
            def _(dve):
                dve.memset(stack[:, :, :], 0.0).then_inc(s_zero, 1)
                dve.wait_ge(s_turned, 1)
                dve.tensor_copy(m.colvec[:, 0:total * 128].rearrange("p (b c) -> p b c", b=total), turned[:, :, :])\
                    .then_inc(s_zero, 1)
                dve.wait_ge(s_zero, 2)
    m.col = {name: m.colvec[:, at:at + n] for name, (at, n) in blocks.items()}
    m.row = {name: m.rowvec[:, i, 0:n] for i, (name, n) in enumerate(rows)}


def feed_forward(nc, m, name, trips, slots, W1, b1, W2, gate):
    with phase(nc, name) as ph:
        w1 = ph.sb("w1", [128, slots, CB, F])
        w2 = ph.sb("w2", [128, slots, FB, C])
        hidden = ph.sb("hidden", [128, FB, COLS])
        bias = ph.sb("bias", [128, FB])
        s_bias = ph.sem("bias")
        up = ph.ps("up", [128, 4, 512])
        down = ph.ps("down", [R, 4, 512])
        s_w = [ph.sem(f"w{s}") for s in range(slots)]
        s_wfree, s_up, s_hidden, s_down, s_added = (ph.sem(x) for x in ("wfree", "up", "hidden", "down", "added"))
        s_pace = ph.sem("pace")
        units = FB * len(HALVES)
        ph.ahead(s_added, s_hidden)
        with nc.Block() as block:

            @block.sync
            def _(sp):
                with sp.Fori(0, trips) as i:
                    for s in range(slots):
                        e = i * slots + s
                        sp.wait_ge(s_wfree, e + 1)
                        sp.dma_start(w1[:, s, :, :], W1(e).rearrange("(b p) n -> p b n", p=128)).then_inc(s_w[s], 16)
                        sp.dma_start(w2[:, s, :, :], W2(e).rearrange("(b p) n -> p b n", p=128)).then_inc(s_w[s], 16)

            @block.tensor
            def _(pe):
                pe.sem_inc(s_wfree, slots)
                with pe.Fori(0, trips) as i:
                    for s in range(slots):
                        pe.wait_ge(s_w[s], (i + 1) * 32)
                        pe.sem_inc(s_pace, 1)
                        with pe.Fori(0, CHUNKS) as c:
                            step = (i * slots + s) * CHUNKS + c
                            for u in range(units):
                                f, (at, n) = u // 2, HALVES[u % 2]
                                if u == 0:
                                    pe.wait_ge(s_hidden, step * units + AHEAD)
                                elif u >= 4:
                                    pe.wait_ge(s_hidden, step * units + (u - 3) + AHEAD)
                                for b in range(CB):
                                    ins = pe.matmul(up[:, u % 4, 0:n], w1[:, s, b, f * 128:(f + 1) * 128],
                                                    m.z_cols[:, b, bass.ds(c * COLS + at, n)],
                                                    start=(b == 0), stop=(b == CB - 1))
                                ins.then_inc(s_up, 1)
                            for j in range(J):
                                if j == 0:
                                    pe.wait_ge(s_added, step * J + AHEAD)
                                elif j == 4:
                                    pe.wait_ge(s_added, step * J + 1 + AHEAD)
                                for f in range(FB):
                                    if j == 0:
                                        pe.wait_ge(s_hidden, step * units + 2 * (f + 1) + AHEAD)
                                    ins = pe.matmul(down[:, j % 4, 0:C], hidden[:, f, j * R:(j + 1) * R],
                                                    w2[:, s, f, :], start=(f == 0), stop=(f == FB - 1))
                                ins.then_inc(s_down, 1)

            @block.scalar
            def _(act):
                with act.Fori(0, trips) as i:
                    for s in range(slots):
                        e = i * slots + s
                        act.wait_ge(s_hidden, e * (units * CHUNKS) + AHEAD)
                        act.sem_inc(s_pace, 1)
                        act.activation(bias[:, :], b1[:, bass.ds(e * FB, FB)], ACT.Copy).then_inc(s_bias, 1)
                        act.wait_ge(s_bias, e + 1)
                        with act.Fori(0, CHUNKS) as c:
                            step = e * CHUNKS + c
                            for u in range(units):
                                f, (at, n) = u // 2, HALVES[u % 2]
                                act.wait_ge(s_up, step * units + (u + 1))
                                act.activation(hidden[:, f, at:at + n], up[:, u % 4, 0:n], ACT.Gelu,
                                               bias=bias[:, f:f + 1]).then_inc(s_hidden, 1)

            @block.vector
            def _(dve):
                with dve.Fori(0, trips) as i:
                    for s in range(slots):
                        e = i * slots + s
                        with dve.Fori(0, CHUNKS) as c:
                            step = e * CHUNKS + c
                            for j in range(J):
                                t = c * J + j
                                dve.wait_ge(s_down, step * J + (j + 1))
                                if gate is None:
                                    dve.tensor_tensor(m.x[:, t, :], m.x[:, t, :], down[:, j % 4, 0:C], ALU.add)\
                                        .then_inc(s_added, 1)
                                else:
                                    dve.scalar_tensor_tensor(out=m.x[:, t, :], in0=down[:, j % 4, 0:C],
                                                             scalar=gate[:, t, bass.ds(e, 1)], in1=m.x[:, t, :],
                                                             op0=ALU.mult, op1=ALU.add).then_inc(s_added, 1)
                        dve.sem_inc(s_wfree, 1)


def mixer0(nc, m, a):
    with phase(nc, "mix") as ph:
        wx = ph.sb("wx", [128, CB, C])
        wo = ph.sb("wo", [128, CB, C])
        QV = X8 * KR + C
        wqv = ph.sb("wqv", [128, CB, QV])
        wk = ph.sb("wk", [128, CB, X8 * KR])
        mine = ph.sb("mine", [X8 * KR, X8, HD])
        mixed = ph.sb("mixed", [128, CB, COLS])
        k_cols = ph.sb("k_cols", [X8 * KR, N])
        q = ph.sb("q", [R, T * X8, KR])
        qstat = ph.sb("qstat", [R, T * X8])
        kmax = ph.sb("kmax", [X8 * KR, 1])
        ksums = ph.sb("ksums", [X8 * KR, CHUNKS])
        ksum = ph.sb("ksum", [X8 * KR, 1])
        ek = ph.sb("ek", [X8 * KR, COLS])
        ek_rows = ph.sb("ek_rows", [R, J, X8 * KR])
        kv = ph.sb("kv", [X8 * KR, C])
        kv_cols = ph.sb("kv_cols", [128, CB, X8 * KR])
        read = ph.sb("read", [X8 * KR, C])
        qc = ph.sb("qc", [R, J, X8 * KR])
        q_cols = ph.sb("q_cols", [X8 * KR, COLS])
        bank4 = ph.ps("bank4", [128, 4, 512])
        kbank = ph.ps("kbank", [X8 * KR, 2, 512])
        rbank = ph.ps("rbank", [R, 2, 512])
        s_w, s_zero, s_mask, s_bd = ph.sem("w"), ph.sem("zero"), ph.sem("mask"), ph.sem("bd")
        s_mix, s_mixed, s_k, s_kout, s_qv, s_qvout = (ph.sem(x) for x in ("mix", "mixed", "k", "kout", "qv", "qvout"))
        s_v, s_kmax, s_ek, s_ekt, s_ekr, s_kv, s_kvadd = (ph.sem(x) for x in ("v", "kmax", "ek", "ekt", "ekr", "kv", "kvadd"))
        s_kvm, s_kvt, s_kvc, s_read, s_readout = (ph.sem(x) for x in ("kvm", "kvt", "kvc", "read", "readout"))
        s_qmax, s_qexp, s_qc, s_qt, s_qcols, s_at, s_fx = (ph.sem(x) for x in ("qmax", "qexp", "qc", "qt", "qcols", "at", "fx"))
        s_act = ph.sem("act")
        bo, b2 = m.row["L0_mix_bo"], m.row["L0_mix_b2"]
        nbd = 3 * X8
        ph.ahead(s_ekr, s_ekt, s_fx, s_kout, s_kv, s_kvadd, s_mixed, s_qcols, s_qt, s_qv, s_qvout)
        with nc.Block() as block:

            @block.gpsimd
            def _(pool):
                pool.memset(wqv[:, :, :], 0.0).then_inc(s_zero, 1)
                pool.memset(wk[:, :, :], 0.0).then_inc(s_zero, 1)
                pool.memset(mine[:, :, :], 1.0).then_inc(s_mask, 1)
                pool.wait_ge(s_mask, 1)
                pool.affine_select(out=mine[:, :, :], in_=mine[:, :, :], compare_op=ALU.is_ge, fill=0.0, base=0,
                                   pattern=[[-KR, X8], [0, HD]], channel_multiplier=1).then_inc(s_mask, 1)
                pool.wait_ge(s_mask, 2)
                pool.affine_select(out=mine[:, :, :], in_=mine[:, :, :], compare_op=ALU.is_ge, fill=0.0,
                                   base=KR - 1, pattern=[[KR, X8], [0, HD]], channel_multiplier=-1)\
                    .then_inc(s_mask, 1)

            @block.sync
            def _(sp):
                sp.dma_start(wx[:, :, :], a["L0_mix_Wx"].rearrange("(b p) n -> p b n", p=128)).then_inc(s_w, 16)
                sp.dma_start(wo[:, :, :], a["L0_mix_Wo"].rearrange("(b p) n -> p b n", p=128)).then_inc(s_w, 16)
                sp.wait_ge(s_zero, 2)
                for h in range(X8):
                    p = slice(HD * (h % 4), HD * (h % 4) + HD)
                    sp.dma_start(wqv[p, h // 4, KR * h:KR * h + KR], a["L0_mix_Wq"]).then_inc(s_bd, 16)
                    sp.dma_start(wk[p, h // 4, KR * h:KR * h + KR], a["L0_mix_Wk"]).then_inc(s_bd, 16)
                    at = X8 * KR + HD * h
                    sp.dma_start(wqv[p, h // 4, at:at + HD], a["L0_mix_Wv"]).then_inc(s_bd, 16)

            @block.tensor
            def _(pe):
                pe.wait_ge(s_w, 32)
                pe.wait_ge(s_bd, 16 * nbd)
                pe.sem_inc(s_act, 1)
                with pe.Fori(0, CHUNKS) as c:
                    for u in range(4):
                        o, (at, n) = u // 2, HALVES[u % 2]
                        if u == 0:
                            pe.wait_ge(s_mixed, c * 4 + AHEAD)
                        for b in range(CB):
                            ins = pe.matmul(bank4[:, u, 0:n], wx[:, b, o * 128:(o + 1) * 128],
                                            m.z_cols[:, b, bass.ds(c * COLS + at, n)],
                                            start=(b == 0), stop=(b == CB - 1))
                        ins.then_inc(s_mix, 1)
                    pe.wait_ge(s_mixed, c * 4 + 4 + AHEAD)
                    pe.wait_ge(s_kout, c * 2 + AHEAD)
                    for u, (at, n) in enumerate(HALVES):
                        for b in range(CB):
                            ins = pe.matmul(kbank[:, u, 0:n], wk[:, b, :], mixed[:, b, at:at + n],
                                            start=(b == 0), stop=(b == CB - 1))
                        ins.then_inc(s_k, 1)
                    for j in range(J):
                        pe.wait_ge(s_qvout, (c * J + (j - 1) if j else c * J) + AHEAD)
                        for b in range(CB):
                            ins = pe.matmul(rbank[:, j % 2, 0:QV], mixed[:, b, j * R:(j + 1) * R], wqv[:, b, :],
                                            start=(b == 0), stop=(b == CB - 1))
                        ins.then_inc(s_qv, 1)
                with pe.Fori(0, CHUNKS) as c:
                    pe.wait_ge(s_ek, c + 1)
                    pe.wait_ge(s_ekr, c + AHEAD)
                    pe.wait_ge(s_qvout, CHUNKS * J + AHEAD)
                    pe.sem_inc(s_act, 1)
                    for j in range(J):
                        ins = pe.transpose(rbank[:, 0, j * X8 * KR:(j + 1) * X8 * KR], ek[:, j * R:(j + 1) * R],
                                           m.ident[0:X8 * KR, 0:X8 * KR])
                    ins.then_inc(s_ekt, 1)
                    pe.wait_ge(s_ekr, c + 1 + AHEAD)
                    pe.wait_ge(s_kvadd, c + AHEAD)
                    for j in range(J):
                        ins = pe.matmul(kbank[:, 0, 0:C], ek_rows[:, j, :], m.y[:, c * J + j, :],
                                        start=(j == 0), stop=(j == J - 1))
                    ins.then_inc(s_kv, 1)
                pe.wait_ge(s_kvm, 1)
                for b in range(CB):
                    ins = pe.transpose(bank4[:, 0, b * X8 * KR:(b + 1) * X8 * KR], kv[:, b * 128:(b + 1) * 128],
                                       m.ident[0:X8 * KR, 0:X8 * KR])
                ins.then_inc(s_kvt, 1)
                pe.wait_ge(s_kvc, 1)
                for b in range(CB):
                    ins = pe.matmul(kbank[:, 1, 0:C], kv_cols[:, b, :], wo[:, b, :], start=(b == 0), stop=(b == CB - 1))
                ins.then_inc(s_read, 1)
                pe.wait_ge(s_readout, 1)
                with pe.Fori(0, CHUNKS) as c:
                    pe.wait_ge(s_qc, c + 1)
                    pe.wait_ge(s_qcols, c + AHEAD)
                    for j in range(J):
                        ins = pe.transpose(bank4[0:X8 * KR, j // 4, (j % 4) * R:(j % 4 + 1) * R], qc[:, j, :],
                                           m.ident[0:R, 0:R])
                    ins.then_inc(s_qt, 1)
                    pe.wait_ge(s_qcols, c + 1 + AHEAD)
                    for j in range(J):
                        pe.wait_ge(s_fx, (c * J + (j - 1) if j else c * J) + AHEAD)
                        pe.matmul(rbank[:, j % 2, 0:C], q_cols[:, j * R:(j + 1) * R], read[:, :],
                                  start=True, stop=True).then_inc(s_at, 1)

            @block.scalar
            def _(act):
                with act.Fori(0, CHUNKS) as c:
                    for u in range(4):
                        o, (at, n) = u // 2, HALVES[u % 2]
                        act.wait_ge(s_mix, c * 4 + (u + 1))
                        if u == 0:
                            act.wait_ge(s_qv, c * J + AHEAD)
                        act.activation(mixed[:, o, at:at + n], bank4[:, u, 0:n], ACT.Identity,
                                       bias=m.col["L0_mix_bx"][:, o:o + 1]).then_inc(s_mixed, 1)
                    for u, (at, n) in enumerate(HALVES):
                        act.wait_ge(s_k, c * 2 + (u + 1))
                        act.activation(k_cols[:, bass.ds(c * COLS + at, n)], kbank[:, u, 0:n], ACT.Copy)\
                            .then_inc(s_kout, 1)
                act.wait_ge(s_kmax, 1)
                with act.Fori(0, CHUNKS) as c:
                    act.wait_ge(s_ekt, c + AHEAD)
                    act.activation(ek[:, :], k_cols[:, bass.ds(c * COLS, COLS)], ACT.Exp, bias=kmax[:, :],
                                   accum_out=ksums[:, bass.ds(c, 1)]).then_inc(s_ek, 1)
                act.wait_ge(s_qmax, 1)
                act.activation(q[:, :, :], q[:, :, :], ACT.Exp).then_inc(s_qexp, 1)

            @block.vector
            def _(dve):
                v = Chain(dve, s_v)
                q_t = q[:, :, :].rearrange("p (t h) k -> p t (h k)", t=T)
                with dve.Fori(0, CHUNKS) as c:
                    for j in range(J):
                        dve.wait_ge(s_qv, c * J + (j + 1) + AHEAD)
                        dve.tensor_copy(q_t[:, c * J + j, :], rbank[:, j % 2, 0:X8 * KR])
                        dve.tensor_copy(m.y[:, c * J + j, :], rbank[:, j % 2, X8 * KR:QV]).then_inc(s_qvout, 1)
                dve.wait_ge(s_kout, 2 * CHUNKS + AHEAD)
                v.link(dve.tensor_reduce(kmax[:, :], k_cols[:, :], AX_X, ALU.max))
                dve.tensor_scalar(kmax[:, :], kmax[:, :], -1.0, None, ALU.mult).then_inc(s_kmax, 1)
                dve.wait_ge(s_qvout, T + AHEAD)
                v.link(dve.tensor_reduce(qstat[:, :], q[:, :, :], AX_X, ALU.max))
                v.link(dve.tensor_tensor(q[:, :, :], q[:, :, :], repeat_last(qstat[:, :], KR), ALU.subtract))
                v.done(s_qmax)
                v.link(dve.memset(kv[:, :], 0.0))
                with dve.Fori(0, CHUNKS) as c:
                    v.enter(c, 1)
                    dve.wait_ge(s_ekt, c + 1 + AHEAD)
                    dve.wait_ge(s_kv, c + AHEAD)
                    dve.tensor_copy(ek_rows[:, :, :].rearrange("p j k -> p (j k)"), rbank[:, 0, 0:J * X8 * KR])\
                        .then_inc(s_ekr, 1)
                    dve.wait_ge(s_kv, c + 1 + AHEAD)
                    v.link(dve.tensor_tensor(kv[:, :], kv[:, :], kbank[:, 0, 0:C], ALU.add))
                    dve.sem_inc(s_kvadd, 1)
                v.leave(CHUNKS)
                dve.wait_ge(s_mask, 3)
                dve.tensor_tensor(kv[:, :], kv[:, :], mine[:, :, :].rearrange("p h d -> p (h d)"), ALU.mult)\
                    .then_inc(s_kvm, 1)
                dve.wait_ge(s_kvt, 1)
                dve.tensor_copy(kv_cols[:, :, :].rearrange("p b k -> p (b k)"), bank4[:, 0, 0:CB * X8 * KR])\
                    .then_inc(s_kvc, 1)
                v.link(dve.tensor_reduce(ksum[:, :], ksums[:, :], AX_X, ALU.add))
                v.link(dve.reciprocal(ksum[:, :], ksum[:, :]))
                dve.wait_ge(s_read, 1)
                dve.tensor_scalar(read[:, :], kbank[:, 1, 0:C], ksum[:, :], None, ALU.mult).then_inc(s_readout, 1)
                dve.wait_ge(s_qexp, 1)
                v.link(dve.tensor_reduce(qstat[:, :], q[:, :, :], AX_X, ALU.add))
                v.link(dve.reciprocal(qstat[:, :], qstat[:, :]))
                with dve.Fori(0, CHUNKS) as c:
                    v.enter(c, 3 * J)
                    dve.wait_ge(s_qt, c + AHEAD)
                    dve.tensor_tensor(qc[:, :, :].rearrange("p j (h k) -> p (j h) k", k=KR),
                                      q[:, bass.ds(c * J * X8, J * X8), :],
                                      repeat_last(qstat[:, bass.ds(c * J * X8, J * X8)], KR), ALU.mult)\
                        .then_inc(s_qc, 1)
                    dve.wait_ge(s_qt, c + 1 + AHEAD)
                    dve.tensor_copy(q_cols[:, 0:4 * R], bank4[0:X8 * KR, 0, 0:4 * R])
                    dve.tensor_copy(q_cols[:, 4 * R:5 * R], bank4[0:X8 * KR, 1, 0:R]).then_inc(s_qcols, 1)
                    for j in range(J):
                        y = m.y[:, c * J + j, :]
                        x = m.x[:, c * J + j, :]
                        dve.wait_ge(s_at, c * J + (j + 1))
                        dve.tensor_tensor(y, rbank[:, j % 2, 0:C], bo, ALU.add).then_inc(s_fx, 1)
                        dve.wait_ge(s_fx, c * J + (j + 1) + AHEAD)
                        v.link(dve.tensor_tensor(y, y, m.z[:, c * J + j, :], ALU.add))
                        v.link(dve.tensor_tensor(x, x, y, ALU.add))
                        v.link(dve.tensor_tensor(x, x, b2, ALU.add))
                v.leave(CHUNKS)


def router(nc, m, name, Wr, br, top2, bias2, bias_row=None):
    with phase(nc, name) as ph:
        wr = ph.sb("wr", [128, CB, X8])
        b2 = ph.sb("b2", [X8, C])
        zc = ph.sb("zc", [128, CB, COLS])
        stat = ph.sb("stat", [R, 2, T])
        work = ph.sb("work", [R, 2, T, X8])
        prefer = ph.sb("prefer", [R, X8])
        gc = ph.sb("gc", [R, J, X8])
        g_cols = ph.sb("g_cols", [X8, COLS])
        score = ph.ps("score", [R, J, X8])
        turned = ph.ps("turned", [X8, 2, 512])
        bank = ph.ps("bank", [R, 2, 512])
        s_w, s_zc, s_score, s_read, s_exp, s_gone, s_v = (ph.sem(x) for x in ("w", "zc", "score", "read", "exp", "gone", "v"))
        s_gc, s_turned, s_gcols, s_prod, s_added, s_pace = (ph.sem(x) for x in ("gc", "turned", "gcols", "prod", "added", "pace"))
        s_prefer = ph.sem("prefer")
        gate = m.gate
        ph.ahead(s_added, s_gcols, s_prod, s_read, s_score, s_turned)
        with nc.Block() as block:

            @block.sync
            def _(sp):
                sp.dma_start(wr[:, :, :], Wr.rearrange("(b p) n -> p b n", p=128)).then_inc(s_w, 16)
                sp.dma_start(b2[:, :], bias2).then_inc(s_w, 16)

            @block.gpsimd
            def _(pool):
                pool.iota(prefer[:, :], pattern=[[-1, X8]], base=X8, channel_multiplier=0,
                          allow_small_or_imprecise_dtypes=True).then_inc(s_prefer, 1)

            @block.scalar
            def _(act):
                with act.Fori(0, CHUNKS) as c:
                    act.wait_ge(s_score, c + AHEAD)
                    act.activation(zc[:, :, :], m.z_cols[:, :, bass.ds(c * COLS, COLS)], ACT.Copy).then_inc(s_zc, 1)
                act.wait_ge(s_exp, 1)
                act.activation(gate[:, :, :], gate[:, :, :], ACT.Exp).then_inc(s_gone, 1)

            @block.tensor
            def _(pe):
                pe.wait_ge(s_w, 32)
                with pe.Fori(0, CHUNKS) as c:
                    pe.wait_ge(s_zc, c + 1)
                    pe.wait_ge(s_read, c + AHEAD)
                    for j in range(J):
                        for b in range(CB):
                            ins = pe.matmul(score[:, j, :], zc[:, b, j * R:(j + 1) * R], wr[:, b, :],
                                            start=(b == 0), stop=(b == CB - 1))
                    ins.then_inc(s_score, 1)
                with pe.Fori(0, CHUNKS) as c:
                    pe.wait_ge(s_gc, c + 1)
                    pe.wait_ge(s_gcols, c + AHEAD)
                    pe.sem_inc(s_pace, 1)
                    for j in range(J):
                        ins = pe.transpose(turned[:, j // 4, (j % 4) * R:(j % 4 + 1) * R], gc[:, j, :],
                                           m.ident[0:R, 0:R])
                    ins.then_inc(s_turned, 1)
                    pe.wait_ge(s_gcols, c + 1 + AHEAD)
                    for j in range(J):
                        pe.wait_ge(s_added, (c * J + (j - 1) if j else c * J) + AHEAD)
                        pe.matmul(bank[:, j % 2, 0:C], g_cols[:, j * R:(j + 1) * R], b2[:, :],
                                  start=True, stop=True).then_inc(s_prod, 1)

            @block.vector
            def _(dve):
                v = Chain(dve, s_v)
                with dve.Fori(0, CHUNKS) as c:
                    dve.wait_ge(s_score, c + 1 + AHEAD)
                    if br is None:
                        ins = dve.tensor_copy(gate[:, bass.ds(c * J, J), :], score[:, :, :])
                    else:
                        ins = dve.tensor_tensor(gate[:, bass.ds(c * J, J), :], score[:, :, :], repeat_mid(br, J), ALU.add)
                    ins.then_inc(s_read, 1)
                dve.wait_ge(s_read, CHUNKS + AHEAD)
                v.link(dve.tensor_reduce(stat[:, 0, :], gate[:, :, :], AX_X, ALU.max))
                v.link(dve.tensor_tensor(gate[:, :, :], gate[:, :, :], repeat_last(stat[:, 0, :], X8), ALU.subtract))
                v.done(s_exp)
                dve.wait_ge(s_gone, 1)
                v.link(dve.tensor_reduce(stat[:, 0, :], gate[:, :, :], AX_X, ALU.add))
                v.link(dve.reciprocal(stat[:, 0, :], stat[:, 0, :]))
                v.link(dve.tensor_tensor(gate[:, :, :], gate[:, :, :], repeat_last(stat[:, 0, :], X8), ALU.mult))
                if top2:
                    left, pick = work[:, 0, :, :], work[:, 1, :, :]
                    v.link(dve.tensor_copy(left, gate[:, :, :]))
                    dve.wait_ge(s_prefer, 1)
                    for _ in range(2):
                        v.link(dve.tensor_reduce(stat[:, 0, :], left, AX_X, ALU.max))
                        v.link(dve.tensor_tensor(pick, left, repeat_last(stat[:, 0, :], X8), ALU.is_equal))
                        v.link(dve.tensor_tensor(pick, pick, repeat_mid(prefer[:, :], T), ALU.mult))
                        v.link(dve.tensor_reduce(stat[:, 1, :], pick, AX_X, ALU.max))
                        v.link(dve.tensor_tensor(pick, pick, repeat_last(stat[:, 1, :], X8), ALU.is_equal))
                        v.link(dve.scalar_tensor_tensor(out=left, in0=pick, scalar=-4.0, in1=left,
                                                        op0=ALU.mult, op1=ALU.add))
                    v.link(dve.tensor_scalar(pick, left, -1.0, None, ALU.is_lt))
                    v.link(dve.tensor_tensor(gate[:, :, :], gate[:, :, :], pick, ALU.mult))
                    v.link(dve.tensor_reduce(stat[:, 0, :], gate[:, :, :], AX_X, ALU.add))
                    v.link(dve.reciprocal(stat[:, 0, :], stat[:, 0, :]))
                    v.link(dve.tensor_tensor(gate[:, :, :], gate[:, :, :], repeat_last(stat[:, 0, :], X8), ALU.mult))
                with dve.Fori(0, CHUNKS) as c:
                    if bias_row is not None:
                        v.enter(c, 1)
                        dve.wait_ge(s_added, c * J + AHEAD)
                        chunk = m.x[:, bass.ds(c * J, J), :]
                        v.link(dve.tensor_tensor(chunk, chunk, repeat_mid(bias_row, J), ALU.add))
                    dve.wait_ge(s_turned, c + AHEAD)
                    dve.tensor_copy(gc[:, :, :], gate[:, bass.ds(c * J, J), :]).then_inc(s_gc, 1)
                    dve.wait_ge(s_turned, c + 1 + AHEAD)
                    dve.wait_ge(s_prod, c * J + AHEAD)
                    dve.tensor_copy(g_cols[:, 0:4 * R], turned[:, 0, 0:4 * R])
                    dve.tensor_copy(g_cols[:, 4 * R:5 * R], turned[:, 1, 0:R]).then_inc(s_gcols, 1)
                    for j in range(J):
                        x = m.x[:, c * J + j, :]
                        dve.wait_ge(s_prod, c * J + (j + 1) + AHEAD)
                        dve.tensor_tensor(x, x, bank[:, j % 2, 0:C], ALU.add).then_inc(s_added, 1)
                if bias_row is not None:
                    v.leave(CHUNKS)


def experts0(nc, m, a):
    with phase(nc, "ex0") as ph:
        NV = X8 * CB
        w = ph.sb("w", [128, 2, 3, CB, C])
        scale = ph.sb("scale", [128, 2, NV])
        shift = ph.sb("shift", [128, 2, NV])
        now = ph.sb("now", [128, 2, 2, CB])
        s_now = ph.sem("now")
        bn_eps = ph.sb("bn_eps", [128, 1])
        h1 = ph.sb("h1", [128, CB, COLS])
        h2 = ph.sb("h2", [128, CB, COLS])
        up = ph.ps("up", [128, 4, 512])
        down = ph.ps("down", [R, 4, 512])
        s_w = [ph.sem(f"w{s}") for s in range(2)]
        s_eps, s_var, s_sd, s_bn, s_v = (ph.sem(x) for x in ("eps", "var", "sd", "bn", "v"))
        s_wfree, s_up, s_h, s_down, s_added, s_pace = (ph.sem(x) for x in ("wfree", "up", "h", "down", "added", "pace"))
        col = m.col
        ph.ahead(s_added, s_down, s_h)
        with nc.Block() as block:

            @block.sync
            def _(sp):
                with sp.Fori(0, X8 // 2) as i:
                    for s in range(2):
                        e = i * 2 + s
                        sp.wait_ge(s_wfree, e + 1)
                        for k, W in enumerate((a["L0_ffn_W1"], a["L0_ffn_W2"], a["L0_ffn_Wo"])):
                            sp.dma_start(w[:, s, k, :, :],
                                         W[bass.ds(e, 1), :, :].rearrange("e (b p) n -> p (e b) n", p=128))\
                                .then_inc(s_w[s], 16)

            @block.tensor
            def _(pe):
                pe.sem_inc(s_wfree, 2)
                with pe.Fori(0, X8 // 2) as i:
                    for s in range(2):
                        pe.wait_ge(s_w[s], (i + 1) * 48)
                        pe.sem_inc(s_pace, 1)
                        with pe.Fori(0, CHUNKS) as c:
                            step = (i * 2 + s) * CHUNKS + c
                            for u in range(8):
                                layer, (at, n), o = u // 4, HALVES[u // 2 % 2], u % 2
                                if u == 0:
                                    pe.wait_ge(s_h, step * 8 + AHEAD)
                                elif u == 4 or u == 6:
                                    pe.wait_ge(s_h, step * 8 + (u - 2) + AHEAD)
                                for b in range(CB):
                                    if layer == 0:
                                        rhs = m.z_cols[:, b, bass.ds(c * COLS + at, n)]
                                    else:
                                        rhs = h1[:, b, at:at + n]
                                    ins = pe.matmul(up[:, u % 4, 0:n], w[:, s, layer, b, o * 128:(o + 1) * 128], rhs,
                                                    start=(b == 0), stop=(b == CB - 1))
                                ins.then_inc(s_up, 1)
                            for j in range(J):
                                if j == 0:
                                    pe.wait_ge(s_added, step * J + AHEAD)
                                    pe.wait_ge(s_h, step * 8 + 6 + AHEAD)
                                elif j == 2:
                                    pe.wait_ge(s_h, step * 8 + 8 + AHEAD)
                                elif j == 4:
                                    pe.wait_ge(s_added, step * J + 1 + AHEAD)
                                for b in range(CB):
                                    ins = pe.matmul(down[:, j % 4, 0:C], h2[:, b, j * R:(j + 1) * R], w[:, s, 2, b, :],
                                                    start=(b == 0), stop=(b == CB - 1))
                                ins.then_inc(s_down, 1)

            @block.scalar
            def _(act):
                act.wait_ge(s_eps, 1)
                act.activation(scale[:, 0, :], col["L0_ffn_v1"], ACT.Sqrt, bias=bn_eps[:, :])
                act.activation(scale[:, 1, :], col["L0_ffn_v2"], ACT.Sqrt, bias=bn_eps[:, :]).then_inc(s_sd, 1)
                act.wait_ge(s_bn, 1)
                with act.Fori(0, X8) as e:
                    act.wait_ge(s_h, e * (8 * CHUNKS) + AHEAD)
                    act.sem_inc(s_pace, 1)
                    act.activation(now[:, 0, :, :], scale[:, :, bass.ds(e * CB, CB)], ACT.Copy).then_inc(s_now, 1)
                    act.activation(now[:, 1, :, :], shift[:, :, bass.ds(e * CB, CB)], ACT.Copy).then_inc(s_now, 1)
                    act.wait_ge(s_now, e * 2 + 2)
                    with act.Fori(0, CHUNKS) as c:
                        step = e * CHUNKS + c
                        for u in range(8):
                            layer, (at, n), o = u // 4, HALVES[u // 2 % 2], u % 2
                            to = h1 if layer == 0 else h2
                            act.wait_ge(s_up, step * 8 + (u + 1))
                            if u == 4:
                                act.wait_ge(s_down, step * J + AHEAD)
                            act.activation(to[:, o, at:at + n], up[:, u % 4, 0:n], ACT.Relu,
                                           bias=now[:, 1, layer, o:o + 1],
                                           scale=now[:, 0, layer, o:o + 1]).then_inc(s_h, 1)

            @block.vector
            def _(dve):
                v = Chain(dve, s_v)
                dve.memset(bn_eps[:, :], 1e-3).then_inc(s_eps, 1)
                dve.wait_ge(s_sd, 1)
                v.link(dve.reciprocal(scale[:, :, :], scale[:, :, :]))
                for k in range(2):
                    b, g, be, mean = (col[f"L0_ffn_{x}{k + 1}"] for x in ("b", "g", "be", "m"))
                    v.link(dve.tensor_tensor(scale[:, k, :], scale[:, k, :], g, ALU.mult))
                    v.link(dve.tensor_tensor(shift[:, k, :], b, mean, ALU.subtract))
                    v.link(dve.tensor_tensor(shift[:, k, :], shift[:, k, :], scale[:, k, :], ALU.mult))
                    v.link(dve.tensor_tensor(shift[:, k, :], shift[:, k, :], be, ALU.add))
                v.done(s_bn)
                with dve.Fori(0, X8) as e:
                    with dve.Fori(0, CHUNKS) as c:
                        step = e * CHUNKS + c
                        for j in range(J):
                            t = c * J + j
                            dve.wait_ge(s_down, step * J + (j + 1) + AHEAD)
                            dve.scalar_tensor_tensor(out=m.x[:, t, :], in0=down[:, j % 4, 0:C],
                                                     scalar=m.gate[:, t, bass.ds(e, 1)], in1=m.x[:, t, :],
                                                     op0=ALU.mult, op1=ALU.add).then_inc(s_added, 1)
                    dve.sem_inc(s_wfree, 1)


def turned_weights(nc, m, a):
    plan = [("wq", a["L1_gnn_Wq"], C, C, 1), ("wk", a["L1_gnn_Wk"], C, C, 1), ("wv", a["L1_gnn_Wv"], C, C, 1),
            ("wp", a["L1_gnn_Wp"], C, C, 1), ("w1", a["L1_gnn_W1"], F, C, 1), ("w2", a["L1_gnn_W2"], C, F, 1),
            ("conv", a["L1_mix_w_qkv"].rearrange("o i k -> o (i k)"), 3 * C, C, 5),
            ("res", a["L1_mix_w_res"].rearrange("o i k -> o (i k)"), C, 2 * C, 1)]
    m.turned = {name: nc.dram_tensor(f"turned_{name}", [k, n], F32).ap() for name, _, n, k, _ in plan}
    blocks = [(name, W, o, k, taps) for name, W, n, k, taps in plan for o in range(n // 128)]
    with phase(nc, "tw") as ph:
        wide = max(k * taps for _, _, _, k, taps in plan)
        rows = ph.sb("rows", [128, 2, wide])
        cols = ph.sb("cols", [128, 2, FB, 128])
        bank = ph.ps("bank", [128, 2, FB, 128])
        s_in = [ph.sem(f"in{s}") for s in range(2)]
        s_out = [ph.sem(f"out{s}") for s in range(2)]
        s_turned, s_cols = ph.sem("turned"), ph.sem("cols")
        with nc.Block() as block:

            @block.sync
            def _(sp):
                for i, (name, W, o, k, taps) in enumerate(blocks):
                    if i >= 2:
                        sp.wait_ge(s_turned, i - 1)
                    sp.dma_start(rows[:, i % 2, 0:k * taps], W[o * 128:(o + 1) * 128, :]).then_inc(s_in[i % 2], 16)

            @block.tensor
            def _(pe):
                for i, (name, W, o, k, taps) in enumerate(blocks):
                    pe.wait_ge(s_in[i % 2], 16 * (i // 2 + 1))
                    if i >= 2:
                        pe.wait_ge(s_cols, i - 1)
                    taken = rows[:, i % 2, 0:k * taps].rearrange("p (i k) -> p i k", k=taps)[:, :, taps // 2]
                    for b in range(k // 128):
                        ins = pe.transpose(bank[:, i % 2, b, :], taken[:, b * 128:(b + 1) * 128], m.ident[:, :])
                    ins.then_inc(s_turned, 1)

            @block.vector
            def _(dve):
                for i, (name, W, o, k, taps) in enumerate(blocks):
                    kb = k // 128
                    dve.wait_ge(s_turned, i + 1)
                    if i >= 2:
                        dve.wait_ge(s_out[i % 2], 16 * (i // 2))
                    dve.tensor_copy(cols[:, i % 2, 0:kb, :], bank[:, i % 2, 0:kb, :]).then_inc(s_cols, 1)

            @block.scalar
            def _(act):
                for i, (name, W, o, k, taps) in enumerate(blocks):
                    kb = k // 128
                    act.wait_ge(s_cols, i + 1)
                    act.dma_start(m.turned[name].rearrange("(b p) n -> p b n", p=128)[:, :, o * 128:(o + 1) * 128],
                                  cols[:, i % 2, 0:kb, :]).then_inc(s_out[i % 2], 16)
                n = len(blocks)
                act.wait_ge(s_out[0], 16 * ((n + 1) // 2))
                act.wait_ge(s_out[1], 16 * (n // 2))


def query_rows(nc, m, a):
    with phase(nc, "qkv") as ph:
        w = ph.sb("w", [128, CB, 3 * C])
        zc = ph.sb("zc", [128, CB, COLS])
        out = ph.sb("out", [R, J, 3 * C])
        bias = ph.sb("bias", [R, 3 * C])
        prod = ph.ps("prod", [R, 2, 2, 512])
        s_w, s_bias, s_zc, s_prod, s_out, s_stored = (ph.sem(x) for x in ("w", "bias", "zc", "prod", "out", "stored"))
        ph.ahead(s_out, s_prod, s_stored)
        with nc.Block() as block:

            @block.sync
            def _(sp):
                for i, name in enumerate(("wq", "wk", "wv")):
                    sp.dma_start(w[:, :, i * C:(i + 1) * C], m.turned[name].rearrange("(b p) n -> p b n", p=128))\
                        .then_inc(s_w, 16)
                with sp.Fori(0, CHUNKS) as c:
                    sp.wait_ge(s_out, (c + 1) * J + AHEAD)
                    sp.dma_start(m.gather_q.rearrange("(t p) n -> p t n", p=R)[:, bass.ds(c * J, J), :],
                                 out[:, :, 0:C]).then_inc(s_stored, 16)
                    sp.dma_start(m.gather_kv.rearrange("(t p) n -> p t n", p=R)[:, bass.ds(c * J, J), :],
                                 out[:, :, C:3 * C]).then_inc(s_stored, 16)
                sp.wait_ge(s_stored, 32 * CHUNKS + AHEAD)

            @block.scalar
            def _(act):
                with act.Fori(0, CHUNKS) as c:
                    act.wait_ge(s_prod, c * J + AHEAD)
                    act.activation(zc[:, :, :], m.z_cols[:, :, bass.ds(c * COLS, COLS)], ACT.Copy).then_inc(s_zc, 1)

            @block.tensor
            def _(pe):
                pe.wait_ge(s_w, 48)
                with pe.Fori(0, CHUNKS) as c:
                    pe.wait_ge(s_zc, c + 1)
                    for j in range(J):
                        pe.wait_ge(s_out, (c * J + (j - 1) if j else c * J) + AHEAD)
                        for k, (at, n) in enumerate(((0, 512), (512, 256))):
                            for b in range(CB):
                                ins = pe.matmul(prod[:, j % 2, k, 0:n], zc[:, b, j * R:(j + 1) * R], w[:, b, at:at + n],
                                                start=(b == 0), stop=(b == CB - 1))
                        ins.then_inc(s_prod, 1)

            @block.vector
            def _(dve):
                for i, name in enumerate(("q", "k", "v")):
                    dve.tensor_copy(bias[:, i * C:(i + 1) * C], m.row[f"L1_gnn_b{name}"]).then_inc(s_bias, 1)
                dve.wait_ge(s_bias, 3)
                with dve.Fori(0, CHUNKS) as c:
                    dve.wait_ge(s_stored, c * 32 + AHEAD)
                    for j in range(J):
                        dve.wait_ge(s_prod, c * J + (j + 1) + AHEAD)
                        dve.tensor_tensor(out[:, j, 0:512], prod[:, j % 2, 0, :], bias[:, 0:512], ALU.add)
                        dve.tensor_tensor(out[:, j, 512:768], prod[:, j % 2, 1, 0:256], bias[:, 512:768], ALU.add)\
                            .then_inc(s_out, 1)


def attention_sum(nc, m):
    with phase(nc, "as") as ph:
        W = C + X8
        index = ph.sb("index", [R, 2, 2, J], I32)
        gq = ph.sb("gq", [R, 2, J, C])
        gkv = ph.sb("gkv", [R, 2, J, 2 * C])
        score = ph.sb("score", [R, J * X8])
        spread = ph.sb("spread", [R, J, W])
        hot = ph.sb("hot", [R, J, R])
        node_no = ph.sb("node_no", [R, N])
        s_node = ph.sem("node")
        summed = ph.sb("summed", [R, T, W])
        none = ph.sb("none", [R, T, X8])
        total = ph.ps("total", [R, 512])
        s_index, s_got = ph.sem("index"), [ph.sem(f"got{s}") for s in range(2)]
        s_hot, s_total, s_added, s_zero, s_pace = (ph.sem(x) for x in ("hot", "total", "added", "zero", "pace"))
        s_v, s_score, s_exp, s_spread = (ph.sem(x) for x in ("v", "score", "exp", "spread"))
        with nc.Block() as block:

            def bounds(eng, g):
                first = eng.value_load(m.group_table[0:1, bass.ds(g, 1)], min_val=0, max_val=T - 1)
                count = eng.value_load(m.group_table[0:1, bass.ds(g + G, 1)], min_val=1, max_val=T)
                before = eng.value_load(m.group_table[0:1, bass.ds(g + 2 * G, 1)], min_val=0, max_val=T * G)
                return first, count, before

            @block.gpsimd
            def _(pool):
                pool.iota(node_no[:, :], pattern=[[1, N]], base=0, channel_multiplier=0,
                          allow_small_or_imprecise_dtypes=True).then_inc(s_node, 1)
                with pool.Fori(0, G // 2) as i:
                    for s in range(2):
                        pool.wait_ge(s_index, i * 2 + (s + 1))
                        pool.sem_inc(s_pace, 1)
                        for j in range(J):
                            for into, table, k in ((gkv, m.gather_kv, 0), (gq, m.gather_q, 1)):
                                pool.indirect_dma_start(
                                    out=into[:, s, j, :], out_offset=None, in_=table,
                                    in_offset=bass.IndirectOffsetOnAxis(ap=index[:, s, k, j:j + 1], axis=0)
                                ).then_inc(s_got[s], 16)

            @block.scalar
            def _(act):
                ex = spread[:, :, C:W]
                with act.Fori(0, G) as g:
                    act.wait_ge(s_score, g + 1)
                    act.activation(ex, score[:, :].rearrange("p (j h) -> p j h", j=J), ACT.Exp).then_inc(s_exp, 1)

            @block.vector
            def _(dve):
                v = Chain(dve, s_v)
                dve.memset(summed[:, :, :], 0.0).then_inc(s_zero, 1)
                dve.wait_ge(s_zero, 1)
                dve.wait_ge(s_node, 1)
                for s in range(2):
                    dve.tensor_copy(index[:, s, 0, :], m.edge_src[:, s, :])
                    dve.tensor_copy(index[:, s, 1, :], m.edge_dsti[:, s, :]).then_inc(s_index, 1)
                with dve.Fori(0, G // 2) as i:
                    v.enter(i, 2 * 3)
                    for s in range(2):
                        g = i * 2 + s
                        dve.wait_ge(s_got[s], (i + 1) * (32 * J))
                        kk, vv = gkv[:, s, :, 0:C], gkv[:, s, :, C:2 * C]
                        v.link(dve.tensor_tensor(gq[:, s, :, :], gq[:, s, :, :], kk, ALU.mult))
                        v.link(dve.tensor_reduce(score[:, :], gq[:, s, :, :].rearrange("p j (h d) -> p (j h) d", h=X8),
                                                 AX_X, ALU.add))
                        v.link(dve.tensor_scalar(score[:, :], score[:, :], HD ** -0.5, 10.0, ALU.mult, ALU.min))
                        dve.tensor_scalar(score[:, :], score[:, :], -10.0, None, ALU.max).then_inc(s_score, 1)
                        dve.wait_ge(s_exp, g + 1)
                        dve.tensor_tensor(spread[:, :, 0:C].rearrange("p j (h d) -> p j h d", h=X8),
                                          vv.rearrange("p j (h d) -> p j h d", h=X8),
                                          repeat_last(spread[:, :, C:W], HD), ALU.mult).then_inc(s_spread, 1)
                        first, count, before = bounds(dve, g)
                        with dve.Fori(0, count) as k:
                            tile = dve.snap(nc.s_assert_within(first + k, 0, T - 1))
                            dve.tensor_tensor(hot[:, :, :],
                                              repeat_mid(node_no[:, bass.ds(tile * R, R)], J),
                                              repeat_last(m.edge_dst[:, g, :], R), ALU.is_equal).then_inc(s_hot, 1)
                            dve.wait_ge(s_total, before + k + 1)
                            dve.tensor_tensor(summed[:, tile, :], summed[:, tile, :], total[:, 0:W],
                                              ALU.add).then_inc(s_added, 1)
                            dve.wait_ge(s_added, before + k + 1)
                        dve.wait_ge(s_spread, g + 1)
                        for k, table in enumerate((m.edge_src, m.edge_dsti)):
                            ins = dve.tensor_copy(index[:, s, k, :],
                                                  table[:, bass.ds(g + 2, 1), :].rearrange("p a j -> p (a j)"))
                        ins.then_inc(s_index, 1)
                v.leave(G // 2)
                den = summed[:, :, C:W]
                v.link(dve.tensor_scalar(none[:, :, :], den, 0.0, None, ALU.is_equal))
                v.link(dve.tensor_tensor(none[:, :, :], none[:, :, :], den, ALU.add))
                v.link(dve.reciprocal(none[:, :, :], none[:, :, :]))
                with dve.Fori(0, T) as t:
                    dve.tensor_tensor(m.y[:, t, :].rearrange("p (h d) -> p h d", h=X8),
                                      summed[:, t, 0:C].rearrange("p (h d) -> p h d", h=X8),
                                      repeat_last(none[:, t, :], HD), ALU.mult).then_inc(s_zero, 1)
                dve.wait_ge(s_zero, T + 1)

            @block.tensor
            def _(pe):
                with pe.Fori(0, G) as g:
                    first, count, before = bounds(pe, g)
                    pe.wait_ge(s_spread, g + 1)
                    pe.sem_inc(s_pace, 1)
                    with pe.Fori(0, count) as k:
                        pe.wait_ge(s_hot, before + k + 1)
                        for j in range(J):
                            ins = pe.matmul(total[:, 0:W], hot[:, j, :], spread[:, j, :],
                                            start=(j == 0), stop=(j == J - 1))
                        ins.then_inc(s_total, 1)


def attention_out(nc, m):
    with phase(nc, "ao") as ph:
        w = ph.sb("w", [128, CB, C])
        rows = ph.sb("rows", [R, J, C])
        cols = ph.sb("cols", [128, J, CB, R])
        turned = ph.ps("turned", [128, 2, 512])
        bank = ph.ps("bank", [R, 2, 512])
        s_w, s_rows, s_turned, s_cols, s_prod, s_y, s_v = (ph.sem(x) for x in ("w", "rows", "turned", "cols", "prod", "y", "v"))
        bp, b2 = m.row["L1_gnn_bp"], m.row["L1_gnn_b2"]
        ph.ahead(s_cols, s_prod, s_turned, s_y)
        with nc.Block() as block:

            @block.sync
            def _(sp):
                sp.dma_start(w[:, :, :], m.turned["wp"].rearrange("(b p) n -> p b n", p=128)).then_inc(s_w, 16)

            @block.scalar
            def _(act):
                with act.Fori(0, CHUNKS) as c:
                    act.wait_ge(s_turned, c * J + AHEAD)
                    act.activation(rows[:, :, :], m.y[:, bass.ds(c * J, J), :], ACT.Copy).then_inc(s_rows, 1)
                    for j in range(J):
                        act.wait_ge(s_turned, c * J + (j + 1) + AHEAD)
                        if j == 0:
                            act.wait_ge(s_prod, c * J + AHEAD)
                        act.activation(cols[:, j, :, :].rearrange("p b r -> p (b r)"), turned[:, j % 2, 0:CB * R],
                                       ACT.Copy).then_inc(s_cols, 1)

            @block.tensor
            def _(pe):
                pe.wait_ge(s_w, 16)
                with pe.Fori(0, CHUNKS) as c:
                    pe.wait_ge(s_rows, c + 1)
                    for j in range(J):
                        pe.wait_ge(s_cols, (c * J + (j - 1) if j else c * J) + AHEAD)
                        for b in range(CB):
                            ins = pe.transpose(turned[:, j % 2, b * R:(b + 1) * R], rows[:, j, b * 128:(b + 1) * 128],
                                               m.ident[0:R, 0:R])
                        ins.then_inc(s_turned, 1)
                    for j in range(J):
                        pe.wait_ge(s_cols, c * J + (j + 1) + AHEAD)
                        pe.wait_ge(s_y, (c * J + (j - 1) if j else c * J) + AHEAD)
                        for b in range(CB):
                            ins = pe.matmul(bank[:, j % 2, 0:C], cols[:, j, b, :], w[:, b, :],
                                            start=(b == 0), stop=(b == CB - 1))
                        ins.then_inc(s_prod, 1)

            @block.vector
            def _(dve):
                v = Chain(dve, s_v)
                with dve.Fori(0, CHUNKS) as c:
                    v.enter(c, 3 * J)
                    for j in range(J):
                        x, y, z = (k[:, c * J + j, :] for k in (m.x, m.y, m.z))
                        dve.wait_ge(s_prod, c * J + (j + 1) + AHEAD)
                        dve.tensor_tensor(y, bank[:, j % 2, 0:C], bp, ALU.add).then_inc(s_y, 1)
                        dve.wait_ge(s_y, c * J + (j + 1) + AHEAD)
                        v.link(dve.tensor_tensor(y, y, z, ALU.add))
                        v.link(dve.tensor_tensor(x, x, y, ALU.add))
                        v.link(dve.tensor_tensor(x, x, b2, ALU.add))
                v.leave(CHUNKS)

C3 = 3 * C
OB = C3 // 128
CAT = 2 * C3
GW = 3 * HD
GN = CAT // GW
CO = GN * HD
BALL = 0.99999
MIN_NORM = 1e-15


def ball_log_rows(nc, m):
    with phase(nc, "bl") as ph:
        square = ph.sb("square", [R, C])
        n2 = ph.sb("n2", [R, T])
        norm, inv, c_, u, w, lnw, one = (ph.sb(x, [R, T]) for x in ("norm", "inv", "c", "u", "w", "lnw", "one"))
        rows = ph.sb("rows", [R, J, C])
        turned = ph.ps("turned", [128, J, 512])
        s_sq, s_norm, s_w, s_ln, s_v = (ph.sem(x) for x in ("sq", "norm", "w", "ln", "v"))
        s_rows, s_turned, s_out, s_pace = (ph.sem(x) for x in ("rows", "turned", "out", "pace"))
        ph.ahead(s_out, s_sq, s_turned)
        with nc.Block() as block:

            @block.scalar
            def _(act):
                with act.Fori(0, T) as t:
                    act.wait_ge(s_sq, t + AHEAD)
                    act.sem_inc(s_pace, 1)
                    act.activation(square[:, :], m.z[:, t, :], ACT.Square, accum_out=n2[:, bass.ds(t, 1)])\
                        .then_inc(s_sq, 1)
                act.wait_ge(s_sq, T + AHEAD)
                act.activation(norm[:, :], n2[:, :], ACT.Sqrt).then_inc(s_norm, 1)
                act.wait_ge(s_w, 1)
                act.activation(lnw[:, :], w[:, :], ACT.Ln).then_inc(s_ln, 1)
                with act.Fori(0, CHUNKS) as c:
                    for j in range(J):
                        act.wait_ge(s_turned, c * J + (j + 1) + AHEAD)
                        act.activation(m.z_cols[:, :, bass.ds(c * COLS + j * R, R)],
                                       turned[:, j, 0:CB * R].rearrange("p (b r) -> p b r", b=CB), ACT.Copy)\
                            .then_inc(s_out, 1)

            @block.vector
            def _(dve):
                v = Chain(dve, s_v)
                dve.wait_ge(s_norm, 1)
                v.link(dve.tensor_scalar(norm[:, :], norm[:, :], MIN_NORM, None, ALU.max))
                v.link(dve.reciprocal(inv[:, :], norm[:, :]))
                v.link(dve.tensor_scalar(c_[:, :], norm[:, :], BALL, None, ALU.min))
                v.link(dve.tensor_scalar(u[:, :], c_[:, :], -1.0, 1.0, ALU.mult, ALU.add))
                v.link(dve.reciprocal(u[:, :], u[:, :]))
                v.link(dve.scalar_tensor_tensor(out=u[:, :], in0=u[:, :], scalar=2.0, in1=c_[:, :],
                                                op0=ALU.mult, op1=ALU.mult))
                v.link(dve.tensor_scalar(w[:, :], u[:, :], 1.0, None, ALU.add))
                v.done(s_w)
                v.link(dve.tensor_scalar(one[:, :], w[:, :], 1.0, None, ALU.is_equal))
                v.link(dve.scalar_tensor_tensor(out=c_[:, :], in0=w[:, :], scalar=-1.0, in1=one[:, :],
                                                op0=ALU.add, op1=ALU.add))
                v.link(dve.reciprocal(c_[:, :], c_[:, :]))
                dve.wait_ge(s_ln, 1)
                v.link(dve.tensor_tensor(lnw[:, :], lnw[:, :], one[:, :], ALU.add))
                v.link(dve.tensor_tensor(lnw[:, :], lnw[:, :], c_[:, :], ALU.mult))
                v.link(dve.tensor_tensor(lnw[:, :], lnw[:, :], u[:, :], ALU.mult))
                v.link(dve.scalar_tensor_tensor(out=inv[:, :], in0=lnw[:, :], scalar=0.5, in1=inv[:, :],
                                                op0=ALU.mult, op1=ALU.mult))
                with dve.Fori(0, CHUNKS) as c:
                    dve.wait_ge(s_turned, c * J + AHEAD)
                    for j in range(J):
                        dve.tensor_scalar(rows[:, j, :], m.z[:, c * J + j, :], inv[:, bass.ds(c * J + j, 1)], None,
                                          ALU.mult).then_inc(s_rows, 1)

            @block.tensor
            def _(pe):
                with pe.Fori(0, CHUNKS) as c:
                    pe.wait_ge(s_out, c * J + AHEAD)
                    for j in range(J):
                        pe.wait_ge(s_rows, c * J + (j + 1))
                        for b in range(CB):
                            ins = pe.transpose(turned[:, j, b * R:(b + 1) * R], rows[:, j, b * 128:(b + 1) * 128],
                                               m.ident[0:R, 0:R])
                        ins.then_inc(s_turned, 1)


def ball_mixer(nc, m, a):
    import math
    reach = math.atanh(BALL)
    with phase(nc, "bm") as ph:
        wc = ph.sb("wc", [128, CB, C3])
        pw = ph.sb("pw", [128, OB, HD])
        diag = ph.sb("diag", [128, 128])
        mine = ph.sb("mine", [128, 128 // HD, HD])
        branch = ph.sb("branch", [128, OB, 128])
        wr = ph.sb("wr", [128, CO // 128, C])
        y = ph.sb("y", [128, OB, N])
        stats = ph.sb("stats", [128, OB, 2 * CHUNKS, 6])
        mv = ph.sb("mv", [128, OB, 2])
        scale = ph.sb("scale", [128, OB])
        shift = ph.sb("shift", [128, OB])
        act_c = ph.sb("act_c", [128, OB, R])
        cat = ph.sb("cat", [R, 2, C3])
        junk = ph.sb("junk", [R, C3])
        s2 = ph.sb("s2", [R, 4])
        nr = ph.sb("nr", [R, 8])
        qk = ph.sb("qk", [R, GN, 2 * HD])
        val = ph.sb("val", [R, GN, HD])
        ratio = ph.sb("ratio", [R, GN, HD])
        ksum = ph.sb("ksum", [R, GN])
        o_cols = ph.sb("o_cols", [128, CO // 128, R])
        fx = ph.sb("fx", [R, C])
        up = ph.ps("up", [128, 4, 512])
        cbank = ph.ps("cbank", [R, 3, 512])
        obank = ph.ps("obank", [128, 512])
        s_w, s_mask, s_diag, s_turn, s_both = (ph.sem(x) for x in ("w", "mask", "diag", "turn", "both"))
        s_up, s_y, s_stats, s_sd, s_bn, s_v, s_pace = (ph.sem(x) for x in ("up", "y", "stats", "sd", "bn", "v", "pace"))
        s_act, s_cat, s_catr, s_sq, s_nrm, s_s2, s_nr = (ph.sem(x) for x in ("act", "cat", "catr", "sq", "nrm", "s2", "nr"))
        s_o, s_ot, s_oc, s_f, s_fx, s_sq2, s_sq3, s_tanh = (ph.sem(x) for x in ("o", "ot", "oc", "f", "fx", "sq2", "sq3", "tanh"))
        s_n3, s_n2, s_sq4 = ph.sem("n3"), ph.sem("n2"), ph.sem("sq4")
        units = OB * len(HALVES)
        col = m.col
        ph.ahead(s_cat, s_catr, s_fx, s_oc, s_ot, s_sq2, s_sq3, s_tanh, s_y)
        with nc.Block() as block:

            @block.gpsimd
            def _(pool):
                pool.memset(mine[:, :, :], 1.0).then_inc(s_mask, 1)
                pool.wait_ge(s_mask, 1)
                pool.affine_select(out=mine[:, :, :], in_=mine[:, :, :], compare_op=ALU.is_ge, fill=0.0, base=0,
                                   pattern=[[-HD, 4], [0, HD]], channel_multiplier=1).then_inc(s_mask, 1)
                pool.wait_ge(s_mask, 2)
                pool.affine_select(out=mine[:, :, :], in_=mine[:, :, :], compare_op=ALU.is_ge, fill=0.0,
                                   base=HD - 1, pattern=[[HD, 4], [0, HD]], channel_multiplier=-1).then_inc(s_mask, 1)

            @block.sync
            def _(sp):
                sp.dma_start(pw[:, :, :], a["L1_mix_w_pw"].rearrange("(b p) i k -> p b (i k)", p=128)).then_inc(s_w, 16)
                sp.dma_start(wc[:, :, :], m.turned["conv"].rearrange("(b p) n -> p b n", p=128)).then_inc(s_w, 16)
                sp.dma_start(wr[:, :, :], m.turned["res"].rearrange("(b p) n -> p b n", p=128)).then_inc(s_w, 16)

            @block.tensor
            def _(pe):
                for o in range(OB):
                    pe.wait_ge(s_diag, o + 1)
                    pe.transpose(obank[:, 0:128], diag[:, :], m.ident[:, :]).then_inc(s_turn, 1)
                pe.wait_ge(s_both, OB)
                pe.wait_ge(s_w, 48)
                pe.sem_inc(s_pace, 1)
                with pe.Fori(0, CHUNKS) as c:
                    for u in range(units):
                        o, (at, n) = u // 2, HALVES[u % 2]
                        pe.wait_ge(s_y, (c * units + (u - 3) if u > 3 else c * units) + AHEAD)
                        for b in range(CB):
                            ins = pe.matmul(up[:, u % 4, 0:n], wc[:, b, o * 128:(o + 1) * 128],
                                            m.z_cols[:, b, bass.ds(c * COLS + at, n)],
                                            start=(b == 0), stop=(b == CB - 1))
                        ins.then_inc(s_up, 1)
                with pe.Fori(0, T) as t:
                    pe.wait_ge(s_act, t + 1)
                    pe.wait_ge(s_catr, t + AHEAD)
                    for o in range(OB):
                        at = (o % 2) * 256
                        pe.transpose(cbank[:, o // 2, at:at + 128], act_c[:, o, :], m.ident[:, :])
                        ins = pe.matmul(cbank[:, o // 2, at + 128:at + 256], act_c[:, o, :], branch[:, o, :],
                                        start=True, stop=True)
                    ins.then_inc(s_cat, 1)
                    pe.wait_ge(s_o, t + 1)
                    pe.wait_ge(s_oc, t + AHEAD)
                    for b in range(CO // 128):
                        ins = pe.transpose(obank[:, b * R:(b + 1) * R],
                                           val[:, :, :].rearrange("p g d -> p (g d)")[:, b * 128:(b + 1) * 128],
                                           m.ident[0:R, 0:R])
                    ins.then_inc(s_ot, 1)
                    pe.wait_ge(s_oc, t + 1 + AHEAD)
                    pe.wait_ge(s_fx, t + AHEAD)
                    for b in range(CO // 128):
                        ins = pe.matmul(up[0:R, 0, 0:C], o_cols[:, b, :], wr[:, b, :],
                                        start=(b == 0), stop=(b == CO // 128 - 1))
                    ins.then_inc(s_f, 1)

            @block.scalar
            def _(act):
                with act.Fori(0, CHUNKS) as c:
                    for u in range(units):
                        o, (at, n) = u // 2, HALVES[u % 2]
                        act.wait_ge(s_up, c * units + (u + 1))
                        act.activation(y[:, o, bass.ds(c * COLS + at, n)], up[:, u % 4, 0:n], ACT.Copy)\
                            .then_inc(s_y, 1)
                act.wait_ge(s_stats, 1)
                act.activation(scale[:, :], mv[:, :, 1], ACT.Sqrt, bias=m.eps[:, :]).then_inc(s_sd, 1)
                act.wait_ge(s_bn, 1)
                with act.Fori(0, T) as t:
                    act.wait_ge(s_cat, t + AHEAD)
                    act.sem_inc(s_pace, 1)
                    for o in range(OB):
                        ins = act.activation(act_c[:, o, :], y[:, o, bass.ds(t * R, R)], ACT.Relu,
                                             bias=shift[:, o:o + 1], scale=scale[:, o:o + 1])
                    ins.then_inc(s_act, 1)
                    act.wait_ge(s_catr, t + 1 + AHEAD)
                    act.wait_ge(s_sq2, t + AHEAD)
                    act.activation(junk[:, :], cat[:, 0, :], ACT.Square, accum_out=s2[:, 0:1]).then_inc(s_sq, 1)
                    act.wait_ge(s_sq, t * 2 + 1)
                    act.activation(junk[:, :], cat[:, 1, :], ACT.Square, accum_out=s2[:, 1:2]).then_inc(s_sq, 1)
                    act.wait_ge(s_s2, t + 1)
                    act.activation(nr[:, 0:2], nr[:, 0:2], ACT.Sqrt).then_inc(s_nrm, 1)
                    act.wait_ge(s_o, t + 1)
                    act.wait_ge(s_sq, t * 2 + 2)
                    act.activation(junk[:, 0:CO], val[:, :, :].rearrange("p g d -> p (g d)"), ACT.Square,
                                   accum_out=s2[:, 2:3]).then_inc(s_sq2, 1)
                    act.wait_ge(s_sq2, t + 1 + AHEAD)
                    act.activation(nr[:, 2:3], s2[:, 2:3], ACT.Sqrt).then_inc(s_n2, 1)
                    act.wait_ge(s_ot, t + 1 + AHEAD)
                    act.activation(o_cols[:, :, :].rearrange("p b r -> p (b r)"), obank[:, 0:CO // 128 * R], ACT.Copy)\
                        .then_inc(s_oc, 1)
                    act.wait_ge(s_fx, t + 1 + AHEAD)
                    act.activation(junk[:, 0:C], fx[:, :], ACT.Square, accum_out=s2[:, 3:4]).then_inc(s_sq3, 1)
                    act.wait_ge(s_sq3, t + 1 + AHEAD)
                    act.activation(nr[:, 3:4], s2[:, 3:4], ACT.Sqrt).then_inc(s_n3, 1)
                    act.wait_ge(s_n3, t + 1)
                    act.activation(nr[:, 4:5], nr[:, 3:4], ACT.Tanh).then_inc(s_tanh, 1)

            @block.vector
            def _(dve):
                v = Chain(dve, s_v)
                dve.wait_ge(s_w, 48)
                dve.wait_ge(s_mask, 3)
                for o in range(OB):
                    if o:
                        dve.wait_ge(s_turn, o)
                    dve.tensor_tensor(diag[:, :].rearrange("p (g i) -> p g i", i=HD), repeat_mid(pw[:, o, :], 4),
                                      mine[:, :, :], ALU.mult).then_inc(s_diag, 1)
                    dve.wait_ge(s_turn, o + 1)
                    dve.tensor_scalar(branch[:, o, :], obank[:, 0:128], col["L1_mix_w_dw"][:, o:o + 1], None,
                                      ALU.mult).then_inc(s_both, 1)
                with dve.Fori(0, CHUNKS) as c:
                    for u in range(units):
                        o, (at, n) = u // 2, HALVES[u % 2]
                        dve.wait_ge(s_y, c * units + (u + 1) + AHEAD)
                        ins = dve.bn_stats(stats[:, o, c * 2 + u % 2, :], y[:, o, bass.ds(c * COLS + at, n)])
                        ins.then_inc(s_sq4, 1)
                dve.wait_ge(s_sq4, CHUNKS * units)
                for o in range(OB):
                    ins = dve.bn_aggr(mv[:, o, :], stats[:, o, :, :].rearrange("p n k -> p (n k)"))
                v.link(ins)
                v.done(s_stats)
                dve.wait_ge(s_sd, 1)
                v.link(dve.reciprocal(scale[:, :], scale[:, :]))
                v.link(dve.tensor_tensor(scale[:, :], scale[:, :], col["L1_mix_bn_gamma"], ALU.mult))
                v.link(dve.tensor_tensor(shift[:, :], mv[:, :, 0], scale[:, :], ALU.mult))
                v.link(dve.tensor_tensor(shift[:, :], col["L1_mix_bn_beta"], shift[:, :], ALU.subtract))
                v.done(s_bn)

                def radial(n, k):
                    v.link(dve.tensor_scalar(nr[:, n:n + 1], nr[:, n:n + 1], MIN_NORM, None, ALU.max))
                    v.link(dve.reciprocal(nr[:, k:k + 1], nr[:, n:n + 1]))
                    v.link(dve.scalar_tensor_tensor(out=nr[:, k:k + 1], in0=nr[:, n:n + 1], scalar=reach,
                                                    in1=nr[:, k:k + 1], op0=ALU.min, op1=ALU.mult))

                with dve.Fori(0, T) as t:
                    v.enter(t, 22)
                    dve.wait_ge(s_cat, t + 1 + AHEAD)
                    bank = cbank[:, :, :].rearrange("p a (b w c) -> p (a b) w c", b=2, w=2)
                    for k in range(2):
                        ins = dve.tensor_copy(cat[:, k, :].rearrange("p (o c) -> p o c", o=OB), bank[:, :, k, :])
                    ins.then_inc(s_catr, 1)
                    dve.wait_ge(s_sq, t * 2 + 2)
                    dve.wait_ge(s_tanh, t + AHEAD)
                    dve.tensor_copy(nr[:, 0:1], s2[:, 0:1])
                    v.link(dve.tensor_tensor(nr[:, 1:2], s2[:, 0:1], s2[:, 1:2], ALU.add))
                    v.done(s_s2)
                    dve.wait_ge(s_nrm, t + 1)
                    radial(0, 5)
                    v.link(dve.tensor_tensor(nr[:, 1:2], nr[:, 1:2], nr[:, 5:6], ALU.mult))
                    radial(1, 6)
                    v.link(dve.tensor_tensor(nr[:, 6:7], nr[:, 6:7], nr[:, 5:6], ALU.mult))
                    groups = cat[:, :, :].rearrange("p a c -> p (a c)").rearrange("p (g w) -> p g w", w=GW)
                    gamma = nr[:, 6:7]
                    dve.wait_ge(s_ot, t + AHEAD)
                    dve.wait_ge(s_sq2, t + AHEAD)
                    dve.tensor_scalar(val[:, :, :], groups[:, :, 2 * HD:GW], gamma, None, ALU.mult)
                    v.link(dve.tensor_scalar(qk[:, :, :], groups[:, :, 0:2 * HD], gamma, 0.0, ALU.mult, ALU.max))
                    v.link(dve.tensor_scalar(ratio[:, :, :], val[:, :, :], 1e-15, None, ALU.add))
                    v.link(dve.reciprocal(ratio[:, :, :], ratio[:, :, :]))
                    dve.tensor_reduce(ksum[:, :], qk[:, :, HD:2 * HD], AX_X, ALU.add)
                    v.link(dve.tensor_tensor(val[:, :, :], val[:, :, :], qk[:, :, 0:HD], ALU.mult))
                    v.link(dve.tensor_tensor(val[:, :, :], val[:, :, :], repeat_last(ksum[:, :], HD), ALU.mult))
                    v.link(dve.tensor_tensor(val[:, :, :], val[:, :, :], ratio[:, :, :], ALU.mult))
                    v.done(s_o)
                    dve.wait_ge(s_n2, t + 1)
                    radial(2, 7)
                    dve.wait_ge(s_f, t + 1)
                    dve.wait_ge(s_sq3, t + AHEAD)
                    dve.scalar_tensor_tensor(out=fx[:, :], in0=up[0:R, 0, 0:C], scalar=nr[:, 7:8],
                                             in1=m.row["L1_mix_b_res"], op0=ALU.mult, op1=ALU.add).then_inc(s_fx, 1)
                    dve.wait_ge(s_tanh, t + 1 + AHEAD)
                    v.link(dve.tensor_scalar(nr[:, 3:4], nr[:, 3:4], MIN_NORM, None, ALU.max))
                    v.link(dve.reciprocal(nr[:, 3:4], nr[:, 3:4]))
                    v.link(dve.scalar_tensor_tensor(out=nr[:, 4:5], in0=nr[:, 4:5], scalar=BALL, in1=nr[:, 3:4],
                                                    op0=ALU.min, op1=ALU.mult))
                    v.link(dve.scalar_tensor_tensor(out=m.x[:, t, :], in0=fx[:, :], scalar=nr[:, 4:5],
                                                    in1=m.x[:, t, :], op0=ALU.mult, op1=ALU.add))
                v.leave(T)


class Memory:
    pass


def graph_layers(nc, a, out):
    m = Memory()
    with ExitStack() as stack:
        def sb(name, shape, dt=F32):
            return stack.enter_context(nc.sbuf_tensor(name, shape, dt))

        m.ident = sb("ident", [128, 128])
        m.ones = sb("ones", [128, 128])
        m.eps = sb("eps", [128, 1])
        m.before = sb("before", [G, G])
        m.row_no = sb("row_no", [128, R])
        m.tile_starts = sb("tile_starts", [G, T - 1])
        m.edge_dst = sb("edge_dst", [R, G, J])
        m.edge_dsti = sb("edge_dsti", [R, G + 2, J], I32)
        m.edge_src = sb("edge_src", [R, G + 2, J], I32)
        m.group_table = sb("group_table", [1, 3 * G], I32)
        m.degree = sb("degree", [R, T])
        m.degree_s = sb("degree_s", [R, 2, T])
        m.inv_sqrt_degree = sb("inv_sqrt_degree", [R, T])
        m.x = sb("x_rows", [R, T, C])
        m.colvec = sb("colvec", [128, 384])
        m.rowvec = sb("rowvec", [R, 10, C])
        m.gate = sb("gate", [R, T, X8])
        m.z = sb("z_rows", [R, T, C])
        m.z_cols = sb("z_cols", [128, CB, N])
        m.gather_q = nc.dram_tensor("gather_q", [N, C], F32).ap()
        m.gather_kv = nc.dram_tensor("gather_kv", [N, 2 * C], F32).ap()
        m.gather0 = nc.dram_tensor("gather0", [N, C], F32).ap()
        y_stack = ExitStack()

        def take_y(turn):
            m.y = y_stack.enter_context(nc.sbuf_tensor(f"y_rows{turn}", [R, T, C], F32))

        def free_y():
            y_stack.close()

        take_y(0)
        with nc.semaphore("x_in") as s_x, nc.Block() as block:

            @block.sync
            def _(sp):
                sp.dma_start(m.x[:, :, :], a["x"].rearrange("(t p) n -> p t n", p=R)).then_inc(s_x, 16)
                sp.wait_ge(s_x, 16)

            @block.gpsimd
            def _(pool):
                pool.memset(m.edge_src[:, :, :], 0)
                pool.memset(m.edge_dsti[:, :, :], 0)

        constants(nc, m)
        edge_tables(nc, m, a["src"], a["dst"])
        layernorm(nc, m, "ln0", m.x, m.z, [(m.z_cols, None, None)])
        scaled_rows(nc, m, a["L0_gnn_W"])
        load_vectors(nc, m, a)
        message_sum(nc, m)
        col = m.col
        layernorm(nc, m, "ln1", m.z, None, [(m.z_cols, col["L0_mix_ln1_g"], col["L0_mix_ln1_b"])])
        mixer0(nc, m, a)
        layernorm(nc, m, "ln2", m.y, None, [(m.z_cols, col["L0_mix_ln2_g"], col["L0_mix_ln2_b"])])
        feed_forward(nc, m, "ff0", 1, 1, lambda e: a["L0_mix_W1"], col["L0_mix_b1"], lambda e: a["L0_mix_W2"], None)
        layernorm(nc, m, "ln3", m.x, None, [(m.z_cols, None, None)])
        router(nc, m, "ro0", a["L0_ffn_Wr"], m.row["L0_ffn_br"], False, a["L0_ffn_bo"])
        experts0(nc, m, a)
        layernorm(nc, m, "ln4", m.x, m.z, [(m.z_cols, None, None)])
        turned_weights(nc, m, a)
        query_rows(nc, m, a)
        ball_log_rows(nc, m)
        free_y()
        ball_mixer(nc, m, a)
        take_y(1)
        attention_sum(nc, m)
        attention_out(nc, m)
        layernorm(nc, m, "ln5", m.y, None, [(m.z_cols, col["L1_gnn_ln_g"], col["L1_gnn_ln_b"])])
        feed_forward(nc, m, "ff1", 1, 1, lambda e: m.turned["w1"], col["L1_gnn_b1"], lambda e: m.turned["w2"], None)
        free_y()
        layernorm(nc, m, "ln6", m.x, None, [(m.z_cols, None, None)])
        router(nc, m, "ro1", a["L1_ffn_Wr"], None, True, a["L1_ffn_b2p"], m.row["L1_ffn_b2s"])
        feed_forward(nc, m, "ff2", 1, 1, lambda e: a["L1_ffn_W1s"], col["L1_ffn_b1s"], lambda e: a["L1_ffn_W2s"], None)
        expert = lambda W: lambda e: W[bass.ds(e, 1), :, :].rearrange("e k n -> (e k) n")
        feed_forward(nc, m, "ff3", X8 // 2, 2, expert(a["L1_ffn_W1p"]), col["L1_ffn_b1p"], expert(a["L1_ffn_W2p"]), m.gate)
        with nc.semaphore("out") as s_out, nc.Block() as block:

            @block.sync
            def _(sp):
                sp.dma_start(out.rearrange("(t p) n -> p t n", p=R), m.x[:, :, :]).then_inc(s_out, 16)
                sp.wait_ge(s_out, 16)


def kernel(**inputs):
    import numpy as np
    from concourse import bacc
    from concourse.bass_utils import run_bass_kernel_spmd

    nc = bacc.Bacc("TRN2", target_bir_lowering=False, num_devices=1)
    arrays, a = {}, {}
    for name, given in inputs.items():
        array = np.ascontiguousarray(given)
        arrays[f"in_{name}"] = array
        a[name] = nc.dram_tensor(f"in_{name}", array.shape, mybir.dt.from_np(array.dtype),
                                          kind="ExternalInput").ap()
    out = nc.dram_tensor("out", (N, C), F32, kind="ExternalOutput").ap()
    graph_layers(nc, a, out)
    return run_bass_kernel_spmd(nc, [arrays], core_ids=[0]).results[0]["out"]
```

```python
from contextlib import ExitStack, contextmanager

import concourse.bass as bass
from concourse import mybir

F32 = mybir.dt.float32
F16 = mybir.dt.float16
BF16 = mybir.dt.bfloat16
I32 = mybir.dt.int32
ALU = mybir.AluOpType
ACT = mybir.ActivationFunctionType
AX_X = mybir.AxisListType.X

N = 3125
C = 256
CB = C // 128
R = 125
T = N // R
J = 5
CHUNKS = T // J
COLS = J * R
HALVES = ((0, 313), (313, 312))
E = 50000
G = E // (J * R)
ET = E // R
SLOTS = 4
F = 4 * C
FB = F // 128
X8 = 8
HD = C // X8
KR = 4
EPS = 1e-5
WS = 64.0
AHEAD = 1
RNE = 12582912.0


class Chain:

    def __init__(self, eng, sem):
        self.eng, self.sem, self.base, self.n = eng, sem, 0, 0

    def link(self, ins):
        self.n += 1
        ins.then_inc(self.sem, 1)
        self.eng.wait_ge(self.sem, self.base + self.n)

    def done(self, sem):
        self.eng.sem_inc(sem, 1)

    def enter(self, i, steps):
        self.start, self.steps = self.n, steps
        self.base = i * steps

    def leave(self, trips):
        assert self.n - self.start == self.steps, self.n - self.start
        self.base = 0
        self.n = self.start + self.steps * trips


class Phase:

    def __init__(self, nc, name, stack):
        self.nc, self.name, self.stack, self.sems = nc, name, stack, []

    def sb(self, name, shape, dt=F32):
        return self.stack.enter_context(self.nc.sbuf_tensor(f"{self.name}_{name}", shape, dt))

    def ps(self, name, shape, dt=F32):
        return self.stack.enter_context(self.nc.psum_tensor(f"{self.name}_{name}", shape, dt))

    def sem(self, name):
        self.sems.append(self.nc.alloc_semaphore(f"{self.name}_{name}"))
        return self.sems[-1]

    def ahead(self, *sems):
        for sem in sems:
            self.nc.gpsimd.sem_inc(sem, AHEAD)


@contextmanager
def phase(nc, name):
    with ExitStack() as stack:
        ph = Phase(nc, name, stack)
        yield ph
        nc.clear_and_free_semaphores(ph.sems)
        nc.all_engine_barrier()


def repeat_last(ap, n):
    return ap.unsqueeze(len(ap.shape)).broadcast_to([*ap.shape, n])


def repeat_mid(ap, n):
    return ap.unsqueeze(1).broadcast_to([ap.shape[0], n, *ap.shape[1:]])


def constants(nc, m):
    with phase(nc, "cst") as ph:
        s_set, s_fill = ph.sem("set"), ph.sem("fill")
        with nc.Block() as block:

            @block.gpsimd
            def _(pool):
                pool.memset(m.ident[:, :], 0.0).then_inc(s_fill, 1)
                pool.memset(m.ones[:, :], 1.0).then_inc(s_set, 1)
                pool.memset(m.eps[:, :], EPS).then_inc(s_set, 1)
                pool.memset(m.ident16[:, :], 0.0).then_inc(s_fill, 1)
                pool.memset(m.before[:, :], 1.0).then_inc(s_fill, 1)
                pool.iota(m.row_no[:, :], pattern=[[1, R]], base=0, channel_multiplier=0,
                          allow_small_or_imprecise_dtypes=True).then_inc(s_set, 1)
                pool.iota(m.tile_starts[:, :], pattern=[[R, T - 1]], base=R, channel_multiplier=0,
                          allow_small_or_imprecise_dtypes=True).then_inc(s_set, 1)
                pool.wait_ge(s_fill, 3)
                pool.affine_select(out=m.ident[:, :], in_=m.ident[:, :], compare_op=ALU.not_equal, fill=1.0,
                                   base=0, pattern=[[-1, 128]], channel_multiplier=1).then_inc(s_set, 1)
                pool.affine_select(out=m.ident16[:, :], in_=m.ident16[:, :], compare_op=ALU.not_equal, fill=1.0,
                                   base=0, pattern=[[-1, 128]], channel_multiplier=1).then_inc(s_set, 1)
                pool.affine_select(out=m.before[:, :], in_=m.before[:, :], compare_op=ALU.is_gt, fill=0.0,
                                   base=0, pattern=[[1, G]], channel_multiplier=-1).then_inc(s_set, 1)
                pool.wait_ge(s_set, 7)


def edge_tables(nc, m, src, dst):
    with phase(nc, "edg") as ph:
        raw = ph.sb("raw", [G, 2, J * R], I32)
        rawf = ph.sb("rawf", [G, 2, J * R])
        ends = ph.sb("ends", [G, 2])
        below = ph.sb("below", [G, 2, T - 1])
        span = ph.sb("span", [G, 2])
        last = ph.sb("last", [G, 2])
        tileno = ph.sb("tileno", [R, ET])
        rowno = ph.sb("rowno", [R, ET])
        tileb = ph.sb("tileb", [R, ET], BF16)
        rowb = ph.sb("rowb", [R, ET], BF16)
        nob = ph.sb("nob", [R, R], BF16)
        SET = 20
        hot_row = ph.sb("hot_row", [R, 2, SET, R], BF16)
        hot_tile = ph.sb("hot_tile", [R, 2, SET, T], BF16)
        turned = ph.ps("turned", [R, 2, 512])
        rows = ph.ps("rows", [1, 512])
        count = ph.ps("count", [R, 2, 512])
        s_in, s_f, s_turned, s_span, s_rows = (ph.sem(x) for x in ("in", "f", "turned", "span", "rows"))
        s_hot, s_count, s_v = ph.sem("hot"), ph.sem("count"), ph.sem("v")
        with nc.Block() as block:

            @block.sync
            def _(sp):
                sp.dma_start(raw[:, 0, :], dst.rearrange("(g e) -> g e", g=G)).then_inc(s_in, 16)
                sp.dma_start(raw[:, 1, :], src.rearrange("(g e) -> g e", g=G)).then_inc(s_in, 16)

            @block.vector
            def _(dve):
                v = Chain(dve, s_v)
                dve.wait_ge(s_in, 32)
                dve.tensor_copy(rawf[:, :, :], raw[:, :, :]).then_inc(s_f, 1)
                dve.wait_ge(s_f, 1)
                dve.tensor_reduce(ends[:, 0:1], rawf[:, 0, :], AX_X, ALU.min)
                v.link(dve.tensor_reduce(ends[:, 1:2], rawf[:, 0, :], AX_X, ALU.max))
                for k in range(2):
                    last_ins = dve.tensor_scalar(below[:, k, :], m.tile_starts[:, :], ends[:, k:k + 1], None, ALU.is_le)
                v.link(last_ins)
                v.link(dve.tensor_reduce(last[:, :], below[:, :, :], AX_X, ALU.add))
                dve.tensor_copy(span[:, 0:1], last[:, 0:1])
                v.link(dve.tensor_tensor(span[:, 1:2], last[:, 1:2], last[:, 0:1], ALU.subtract))
                dve.tensor_scalar(span[:, 1:2], span[:, 1:2], 1.0, None, ALU.add).then_inc(s_span, 1)
                dve.wait_ge(s_turned, 1)
                dve.tensor_copy(m.edge_dst[:, :, :],
                                turned[:, 0, 0:J * G].rearrange("p (j g) -> p g j", j=J))
                v.link(dve.tensor_copy(m.edge_dsti[:, 0:G, :],
                                       turned[:, 0, 0:J * G].rearrange("p (j g) -> p g j", j=J)))
                v.link(dve.tensor_copy(m.edge_src[:, 0:G, :],
                                       turned[:, 1, 0:J * G].rearrange("p (j g) -> p g j", j=J)))
                dve.wait_ge(s_rows, 1)
                v.link(dve.tensor_copy(m.group_table[:, :], rows[:, 0:3 * G]))
                flat = m.edge_dst[:, :, :].rearrange("p g j -> p (g j)")
                v.link(dve.tensor_scalar(tileno[:, :], flat, 1.0 / R, 0.5 / R - 0.5, ALU.mult, ALU.add))
                v.link(dve.tensor_scalar(tileno[:, :], tileno[:, :], RNE, RNE, ALU.add, ALU.subtract))
                v.link(dve.scalar_tensor_tensor(out=rowno[:, :], in0=tileno[:, :], scalar=-float(R), in1=flat,
                                                op0=ALU.mult, op1=ALU.add))
                dve.tensor_copy(tileb[:, :], tileno[:, :])
                dve.tensor_copy(rowb[:, :], rowno[:, :])
                dve.tensor_copy(nob[:, :], m.row_no[0:R, :])
                v.link(dve.memset(m.degree[:, :], 0.0))
                steps = 6
                with dve.Fori(0, ET // SET // 2) as i:
                    v.enter(i, 2)
                    for s in range(2):
                        at = i * (2 * SET) + s * SET
                        dve.tensor_tensor(hot_row[:, s, :, :], repeat_mid(nob[:, :], SET),
                                          repeat_last(rowb[:, bass.ds(at, SET)], R), ALU.is_equal)
                        dve.tensor_tensor(hot_tile[:, s, :, :], repeat_mid(nob[:, 0:T], SET),
                                          repeat_last(tileb[:, bass.ds(at, SET)], T),
                                          ALU.is_equal).then_inc(s_hot, 1)
                    for s in range(2):
                        dve.wait_ge(s_count, i * 2 + (s + 1))
                        v.link(dve.tensor_tensor(m.degree[:, :], m.degree[:, :], count[:, s, 0:T], ALU.add))
                v.leave(ET // SET // 2)
                v.link(dve.tensor_scalar(m.degree_s[:, 0, :], m.degree[:, :], 1.0, None, ALU.max))
                dve.tensor_scalar(m.degree_s[:, 1, :], m.degree[:, :], 1.0, None, ALU.min).then_inc(s_span, 1)
                dve.wait_ge(s_rows, 2)
                v.link(dve.reciprocal(m.degree_s[:, 0, :], m.degree_s[:, 0, :]))
                v.link(dve.tensor_tensor(m.inv_sqrt_degree[:, :], m.degree_s[:, 0, :], m.degree_s[:, 1, :], ALU.mult))

            @block.scalar
            def _(act):
                act.wait_ge(s_span, 2)
                act.activation(m.degree_s[:, 0, :], m.degree_s[:, 0, :], ACT.Sqrt).then_inc(s_rows, 1)

            @block.tensor
            def _(pe):
                pe.wait_ge(s_f, 1)
                for k in range(2):
                    for j in range(J):
                        last_ins = pe.transpose(turned[:, k, j * G:(j + 1) * G], rawf[:, k, j * R:(j + 1) * R],
                                                m.ident[0:G, 0:G])
                last_ins.then_inc(s_turned, 1)
                pe.wait_ge(s_span, 1)
                pe.matmul(rows[:, 0:G], span[:, 0:1], m.ident[0:G, 0:G], start=True, stop=True)
                pe.matmul(rows[:, G:2 * G], span[:, 1:2], m.ident[0:G, 0:G], start=True, stop=True)
                pe.matmul(rows[:, 2 * G:3 * G], span[:, 1:2], m.before[:, :], start=True, stop=True)\
                    .then_inc(s_rows, 1)
                with pe.Fori(0, ET // SET // 2) as i:
                    for s in range(2):
                        pe.wait_ge(s_hot, i * 2 + (s + 1))
                        for k in range(SET):
                            last_ins = pe.matmul(count[:, s, 0:T], hot_row[:, s, k, :], hot_tile[:, s, k, :],
                                                 start=(k == 0), stop=(k == SET - 1))
                        last_ins.then_inc(s_count, 1)


def join_stats(v, stats, mv):
    dve = v.eng
    a_mean, b_mean = stats[:, :, 1], stats[:, :, 4]
    v.link(dve.tensor_tensor(mv[:, 0, :], a_mean, b_mean, ALU.subtract))
    v.link(dve.scalar_tensor_tensor(out=mv[:, 1, :], in0=mv[:, 0, :], scalar=C / 4.0, in1=mv[:, 0, :],
                                    op0=ALU.mult, op1=ALU.mult))
    v.link(dve.tensor_tensor(mv[:, 1, :], mv[:, 1, :], stats[:, :, 2], ALU.add))
    v.link(dve.tensor_tensor(mv[:, 1, :], mv[:, 1, :], stats[:, :, 5], ALU.add))
    v.link(dve.tensor_tensor(mv[:, 0, :], a_mean, b_mean, ALU.add))
    v.link(dve.tensor_scalar(mv[:, 0, :], mv[:, 0, :], 0.5, None, ALU.mult))
    v.link(dve.tensor_scalar(mv[:, 1, :], mv[:, 1, :], 1.0 / C, None, ALU.mult))


def layernorm(nc, m, name, source, rows_out=None):
    with phase(nc, name) as ph:
        stats = ph.sb("stats", [R, T, 6])
        mv = ph.sb("mv", [R, 2, T])
        sd = ph.sb("sd", [R, T])
        z32 = ph.sb("z32", [R, J, C])
        z16 = ph.sb("z16", [R, J, 2, C], F16)
        turned = ph.ps("turned", [128, J, 2, 2 * CB, 128], F16)
        s_stats, s_mv, s_sd, s_v = (ph.sem(x) for x in ("stats", "mv", "sd", "v"))
        s_z32, s_high, s_low, s_turned, s_out, s_rows = (ph.sem(x) for x in ("z32", "high", "low", "turned", "out", "rows"))
        ph.ahead(s_turned, s_out, s_low, s_rows)
        with nc.Block() as block:

            @block.vector
            def _(dve):
                v = Chain(dve, s_v)
                with dve.Fori(0, T) as t:
                    dve.bn_stats(stats[:, t, :], source[:, t, :]).then_inc(s_stats, 1)
                dve.wait_ge(s_stats, T)
                join_stats(v, stats, mv)
                v.done(s_mv)
                dve.wait_ge(s_sd, 1)
                v.link(dve.reciprocal(sd[:, :], sd[:, :]))
                with dve.Fori(0, CHUNKS) as c:
                    dve.wait_ge(s_low, c * J + AHEAD)
                    if rows_out is not None:
                        dve.wait_ge(s_rows, c * J + AHEAD)
                    for j in range(J):
                        dve.tensor_scalar(z32[:, j, :], source[:, c * J + j, :], mv[:, 0, bass.ds(c * J + j, 1)],
                                          sd[:, bass.ds(c * J + j, 1)], ALU.subtract, ALU.mult).then_inc(s_z32, 1)
                    for j in range(J):
                        dve.wait_ge(s_high, c * J + (j + 1))
                        dve.tensor_tensor(z16[:, j, 1, :], z32[:, j, :], z16[:, j, 0, :], ALU.subtract)\
                            .then_inc(s_low, 1)

            @block.gpsimd
            def _(pool):
                if rows_out is not None:
                    with pool.Fori(0, CHUNKS) as c:
                        for j in range(J):
                            pool.wait_ge(s_z32, c * J + (j + 1))
                            pool.tensor_copy(rows_out[:, c * J + j, :], z32[:, j, :]).then_inc(s_rows, 1)

            @block.scalar
            def _(act):
                act.wait_ge(s_mv, 1)
                act.activation(sd[:, :], mv[:, 1, :], ACT.Sqrt, bias=m.eps[0:R, :]).then_inc(s_sd, 1)
                with act.Fori(0, CHUNKS) as c:
                    act.wait_ge(s_turned, c * J + AHEAD)
                    for j in range(J):
                        act.wait_ge(s_z32, c * J + (j + 1))
                        act.activation(z16[:, j, 0, :], z32[:, j, :], ACT.Copy).then_inc(s_high, 1)
                    for j in range(J):
                        act.wait_ge(s_turned, c * J + (j + 1) + AHEAD)
                        act.activation(m.zc[:, :, :, bass.ds(c * COLS + j * R, R)].rearrange("p k b r -> p (k b) r"),
                                       turned[:, j, 0, :, 0:R], ACT.Copy).then_inc(s_out, 1)

            @block.tensor
            def _(pe):
                with pe.Fori(0, CHUNKS) as c:
                    pe.wait_ge(s_out, c * J + AHEAD)
                    for j in range(J):
                        pe.wait_ge(s_low, c * J + (j + 1) + AHEAD)
                        for k in range(2):
                            for b in range(CB):
                                ins = pe.transpose(turned[:, j, 0, k * CB + b, 0:R], z16[:, j, k, b * 128:(b + 1) * 128],
                                                   m.ident16[0:R, 0:R])
                        ins.then_inc(s_turned, 1)


def layernorm_cols(nc, m, name, source, rows_out, cols):
    with phase(nc, name) as ph:
        stats = ph.sb("stats", [R, T, 6])
        mv = ph.sb("mv", [R, 2, T])
        sd = ph.sb("sd", [R, T])
        normed = ph.sb("normed", [R, J, C])
        turned = ph.ps("turned", [128, J, 512])
        s_stats, s_mv, s_sd, s_v = (ph.sem(x) for x in ("stats", "mv", "sd", "v"))
        s_normed, s_turned, s_free, s_done, s_rows = (ph.sem(x) for x in ("normed", "turned", "free", "done", "rows"))
        with nc.Block() as block:

            @block.vector
            def _(dve):
                v = Chain(dve, s_v)
                with dve.Fori(0, T) as t:
                    dve.bn_stats(stats[:, t, :], source[:, t, :]).then_inc(s_stats, 1)
                dve.wait_ge(s_stats, T)
                join_stats(v, stats, mv)
                v.done(s_mv)
                dve.wait_ge(s_sd, 1)
                v.link(dve.reciprocal(sd[:, :], sd[:, :]))
                with dve.Fori(0, CHUNKS) as c:
                    for j in range(J):
                        dve.wait_ge(s_free, c * J + (j + 1))
                        dve.tensor_scalar(normed[:, j, :], source[:, c * J + j, :], mv[:, 0, bass.ds(c * J + j, 1)],
                                          sd[:, bass.ds(c * J + j, 1)], ALU.subtract, ALU.mult).then_inc(s_normed, 1)

            @block.gpsimd
            def _(pool):
                if rows_out is not None:
                    with pool.Fori(0, CHUNKS) as c:
                        for j in range(J):
                            pool.wait_ge(s_normed, c * J + (j + 1))
                            pool.tensor_copy(rows_out[:, c * J + j, :], normed[:, j, :]).then_inc(s_rows, 1)

            @block.scalar
            def _(act):
                act.wait_ge(s_mv, 1)
                act.activation(sd[:, :], mv[:, 1, :], ACT.Sqrt, bias=m.eps[0:R, :]).then_inc(s_sd, 1)
                act.sem_inc(s_free, J)
                with act.Fori(0, CHUNKS) as c:
                    for j in range(J):
                        act.wait_ge(s_turned, c * J + (j + 1))
                        at = c * COLS + j * R
                        n = 0
                        for target, gain, shift in cols:
                            if gain is None:
                                ins = act.activation(target[:, :, bass.ds(at, R)],
                                                     turned[:, j, 0:CB * R].rearrange("p (b r) -> p b r", b=CB),
                                                     ACT.Copy)
                            else:
                                for b in range(CB):
                                    ins = act.activation(target[:, b, bass.ds(at, R)], turned[:, j, b * R:(b + 1) * R],
                                                         ACT.Identity, bias=shift[:, b:b + 1], scale=gain[:, b:b + 1])
                        ins.then_inc(s_done, 1)
                        if rows_out is not None:
                            act.wait_ge(s_rows, c * J + (j + 1))
                        act.wait_ge(s_done, c * J + (j + 1))
                        act.sem_inc(s_free, 1)

            @block.tensor
            def _(pe):
                with pe.Fori(0, CHUNKS) as c:
                    for j in range(J):
                        pe.wait_ge(s_normed, c * J + (j + 1))
                        for b in range(CB):
                            ins = pe.transpose(turned[:, j, b * R:(b + 1) * R], normed[:, j, b * 128:(b + 1) * 128],
                                               m.ident[0:R, 0:R])
                        ins.then_inc(s_turned, 1)


def product(pe, out, left, right, parts=3):
    terms = [(0, 0), (1, 0), (0, 1)]
    todo = [(k, n, b) for b in range(CB) for k, n in terms]
    for i, (k, n, b) in enumerate(todo):
        ins = pe.matmul(out, left(k, b), right(n, b), start=(i == 0), stop=(i == len(todo) - 1))
    return ins


def scaled_rows(nc, m, W):
    with phase(nc, "hs") as ph:
        w = ph.sb("w", [128, CB, C])
        w16 = ph.sb("w16", [128, 2, CB, C], F16)
        out32 = ph.sb("out32", [R, J, C])
        out = ph.sb("out", [R, J, 2, C], F16)
        prod = ph.ps("prod", [R, J, 512])
        s_w, s_split, s_prod, s_out, s_high, s_low, s_stored = (
            ph.sem(x) for x in ("w", "split", "prod", "out", "high", "low", "stored"))
        ph.ahead(s_stored, s_out, s_low)
        with nc.Block() as block:

            @block.sync
            def _(sp):
                sp.dma_start(w[:, :, :], W.rearrange("(b p) n -> p b n", p=128)).then_inc(s_w, 16)
                with sp.Fori(0, CHUNKS) as c:
                    sp.wait_ge(s_low, (c + 1) * J + AHEAD)
                    sp.dma_start(m.gather0.rearrange("(t p) n -> p t n", p=R)[:, bass.ds(c * J, J), :],
                                 out[:, :, :, :].rearrange("p j k n -> p j (k n)")).then_inc(s_stored, 16)
                sp.wait_ge(s_stored, 16 * CHUNKS + AHEAD)

            @block.scalar
            def _(act):
                act.wait_ge(s_w, 16)
                act.activation(w16[:, 0, :, :], w[:, :, :], ACT.Copy, scale=WS).then_inc(s_split, 1)
                with act.Fori(0, CHUNKS) as c:
                    act.wait_ge(s_stored, c * 16 + AHEAD)
                    for j in range(J):
                        act.wait_ge(s_out, c * J + (j + 1) + AHEAD)
                        act.activation(out[:, j, 0, :], out32[:, j, :], ACT.Copy).then_inc(s_high, 1)

            @block.tensor
            def _(pe):
                pe.wait_ge(s_split, 2)
                with pe.Fori(0, CHUNKS) as c:
                    pe.wait_ge(s_out, c * J + AHEAD)
                    for j in range(J):
                        product(pe, prod[:, j, 0:C], lambda k, b: m.zc[:, k, b, bass.ds(c * COLS + j * R, R)],
                                lambda k, b: w16[:, k, b, :]).then_inc(s_prod, 1)

            @block.vector
            def _(dve):
                dve.wait_ge(s_split, 1)
                dve.scalar_tensor_tensor(out=w16[:, 1, :, :], in0=w[:, :, :], scalar=WS, in1=w16[:, 0, :, :],
                                         op0=ALU.mult, op1=ALU.subtract).then_inc(s_split, 1)
                with dve.Fori(0, CHUNKS) as c:
                    dve.wait_ge(s_low, c * J + AHEAD)
                    for j in range(J):
                        dve.wait_ge(s_prod, c * J + (j + 1))
                        dve.tensor_scalar(out32[:, j, :], prod[:, j, 0:C], m.inv_sqrt_degree[:, bass.ds(c * J + j, 1)],
                                          1.0 / WS, ALU.mult, ALU.mult).then_inc(s_out, 1)
                    for j in range(J):
                        dve.wait_ge(s_high, c * J + (j + 1))
                        if j == 0:
                            dve.wait_ge(s_stored, c * 16 + AHEAD)
                        dve.tensor_tensor(out[:, j, 1, :], out32[:, j, :], out[:, j, 0, :], ALU.subtract)\
                            .then_inc(s_low, 1)


def group_bounds(eng, m, g):
    first = eng.value_load(m.group_table[0:1, bass.ds(g, 1)], min_val=0, max_val=T - 1)
    count = eng.value_load(m.group_table[0:1, bass.ds(g + G, 1)], min_val=1, max_val=T)
    before = eng.value_load(m.group_table[0:1, bass.ds(g + 2 * G, 1)], min_val=0, max_val=T * G)
    return first, count, before


def add_visit(nc, dve, summed, total, visit, last, s_total, s_added):
    tile = dve.snap(last, min_val=0, max_val=T - 1)
    into, fresh = summed[:, tile, :], total[:, dve.snap((visit + 1) % 2), 0:summed.shape[2]]
    dve.wait_ge(s_total, visit + AHEAD)
    dve.wait_ge(s_added, visit + AHEAD)
    dve.tensor_tensor(into, into, fresh, ALU.add).then_inc(s_added, 1)


def message_sum(nc, m):
    with phase(nc, "ms") as ph:
        index = ph.sb("index", [R, SLOTS, J], I32)
        got = ph.sb("got", [R, SLOTS, J, 2 * C], F16)
        hot = ph.sb("hot", [R, 2, J, R], F16)
        node_no = ph.sb("node_no", [R, N])
        s_node = ph.sem("node")
        summed = ph.sb("summed", [R, T, C])
        total = ph.ps("total", [R, 2, 512])
        s_index, s_got = ph.sem("index"), [ph.sem(f"got{s}") for s in range(SLOTS)]
        s_hot, s_total, s_added, s_zero = (ph.sem(x) for x in ("hot", "total", "added", "zero"))
        s_pace = ph.sem("pace")
        ph.ahead(s_total, s_added)
        with nc.Block() as block:

            @block.gpsimd
            def _(pool):
                pool.iota(node_no[:, :], pattern=[[1, N]], base=0, channel_multiplier=0,
                          allow_small_or_imprecise_dtypes=True).then_inc(s_node, 1)
                with pool.Fori(0, G // SLOTS) as i:
                    for s in range(SLOTS):
                        pool.wait_ge(s_index, i * SLOTS + (s + 1))
                        pool.sem_inc(s_pace, 1)
                        for j in range(J):
                            pool.indirect_dma_start(
                                out=got[:, s, j, :], out_offset=None, in_=m.gather0,
                                in_offset=bass.IndirectOffsetOnAxis(ap=index[:, s, j:j + 1], axis=0)
                            ).then_inc(s_got[s], 16)

            @block.vector
            def _(dve):
                dve.memset(summed[:, :, :], 0.0).then_inc(s_zero, 1)
                dve.memset(total[:, :, :], 0.0).then_inc(s_zero, 1)
                dve.wait_ge(s_zero, 2)
                dve.wait_ge(s_node, 1)
                for s in range(SLOTS - 1):
                    dve.tensor_copy(index[:, s, :], m.edge_src[:, s, :]).then_inc(s_index, 1)
                with dve.register("last_tile") as last:
                    dve.reg_mov(last, 0)
                    with dve.Fori(0, G // SLOTS) as i:
                        for s in range(SLOTS):
                            g = i * SLOTS + s
                            first, count, before = group_bounds(dve, m, g)
                            with dve.Fori(0, count) as k:
                                visit = dve.snap(before + k)
                                tile = dve.snap(nc.s_assert_within(first + k, 0, T - 1))
                                dve.tensor_tensor(hot[:, visit % 2, :, :],
                                                  repeat_mid(node_no[:, bass.ds(tile * R, R)], J),
                                                  repeat_last(m.edge_dst[:, g, :], R), ALU.is_equal)\
                                    .then_inc(s_hot, 1)
                                add_visit(nc, dve, summed, total, visit, last, s_total, s_added)
                                dve.reg_mov(last, tile)
                            free = (s - 1) % SLOTS
                            nxt = m.edge_src[:, bass.ds(g + SLOTS - 1, 1), :].rearrange("p a j -> p (a j)")
                            dve.tensor_copy(index[:, free, :], nxt).then_inc(s_index, 1)
                    add_visit(nc, dve, summed, total, dve.snap(before + count), last, s_total, s_added)
                    dve.wait_ge(s_added, before + count + 1 + AHEAD)
                    dve.sem_inc(s_pace, 1)
                with dve.Fori(0, T) as t:
                    dve.scalar_tensor_tensor(out=m.x[:, t, :], in0=summed[:, t, :],
                                             scalar=m.inv_sqrt_degree[:, bass.ds(t, 1)], in1=m.x[:, t, :],
                                             op0=ALU.mult, op1=ALU.add).then_inc(s_zero, 1)

            @block.tensor
            def _(pe):
                pe.wait_ge(s_zero, 2)
                with pe.Fori(0, G // SLOTS) as i:
                    for s in range(SLOTS):
                        g = i * SLOTS + s
                        first, count, before = group_bounds(pe, m, g)
                        pe.wait_ge(s_got[s], (i + 1) * (16 * J))
                        pe.sem_inc(s_pace, 1)
                        with pe.Fori(0, count) as k:
                            visit = pe.snap(before + k)
                            pe.wait_ge(s_hot, visit + 1)
                            pe.wait_ge(s_added, visit + AHEAD)
                            for j in range(J):
                                for p in range(2):
                                    ins = pe.matmul(total[:, visit % 2, 0:C], hot[:, visit % 2, j, :],
                                                    got[:, s, j, p * C:(p + 1) * C],
                                                    start=(j + p == 0), stop=(j + p == J))
                            ins.then_inc(s_total, 1)


def load_vectors(nc, m, a):
    plan, at = [], 0
    blocks = {}
    for name in ("L0_mix_ln1_g", "L0_mix_ln1_b", "L0_mix_bx", "L0_mix_ln2_g", "L0_mix_ln2_b", "L0_mix_b1",
                 "L0_ffn_b1", "L0_ffn_g1", "L0_ffn_be1", "L0_ffn_m1", "L0_ffn_v1",
                 "L0_ffn_b2", "L0_ffn_g2", "L0_ffn_be2", "L0_ffn_m2", "L0_ffn_v2",
                 "L1_gnn_ln_g", "L1_gnn_ln_b", "L1_gnn_b1", "L1_mix_bn_gamma", "L1_mix_bn_beta",
                 "L1_mix_w_dw", "L1_ffn_b1s", "L1_ffn_b1p"):
        ap = a[name]
        if name == "L1_mix_w_dw":
            ap = ap.rearrange("c a k -> (c a) k")[:, 2:3].rearrange("(b p) k -> b (p k)", p=128)
        elif len(ap.shape) == 2:
            ap = ap.rearrange("e (b p) -> (e b) p", p=128)
        else:
            ap = ap.rearrange("(b p) -> b p", p=128)
        n = ap.shape[0]
        blocks[name] = (at, n)
        done = 0
        while done < n:
            k = min(n - done, 128 - at % 128)
            plan.append((at // 128, at % 128, k, ap[done:done + k, :]))
            at += k
            done += k
    total = -(-at // 128)
    rows = [("L0_mix_bo", C), ("L0_mix_b2", C), ("L0_ffn_br", X8), ("L1_gnn_bq", C), ("L1_gnn_bk", C),
            ("L1_gnn_bv", C), ("L1_gnn_bp", C), ("L1_gnn_b2", C), ("L1_mix_b_res", C), ("L1_ffn_b2s", C)]
    with phase(nc, "vec") as ph:
        stack = ph.sb("stack", [128, total, 128])
        turned = ph.ps("turned", [128, total, 128])
        s_in, s_row, s_turned, s_zero = ph.sem("in"), ph.sem("row"), ph.sem("turned"), ph.sem("zero")
        with nc.Block() as block:

            @block.sync
            def _(sp):
                sp.wait_ge(s_zero, 1)
                for b, p, k, ap in plan:
                    sp.dma_start(stack[p:p + k, b, :], ap, allow_slow_non_contiguous=True).then_inc(s_in, 16)
                for i, (name, n) in enumerate(rows):
                    sp.dma_start(m.rowvec[:, i, 0:n], a[name].unsqueeze(0).broadcast_to([R, n])).then_inc(s_row, 16)
                sp.wait_ge(s_row, 16 * len(rows))

            @block.tensor
            def _(pe):
                pe.wait_ge(s_in, 16 * len(plan))
                for b in range(total):
                    ins = pe.transpose(turned[:, b, :], stack[:, b, :], m.ident[:, :])
                ins.then_inc(s_turned, 1)

            @block.vector
            def _(dve):
                dve.memset(stack[:, :, :], 0.0).then_inc(s_zero, 1)
                dve.wait_ge(s_turned, 1)
                dve.tensor_copy(m.colvec[:, 0:total * 128].rearrange("p (b c) -> p b c", b=total), turned[:, :, :])\
                    .then_inc(s_zero, 1)
                dve.wait_ge(s_zero, 2)
    m.col = {name: m.colvec[:, at:at + n] for name, (at, n) in blocks.items()}
    m.row = {name: m.rowvec[:, i, 0:n] for i, (name, n) in enumerate(rows)}


def feed_forward(nc, m, name, experts, W1, b1, W2, gate=None, gain=None, bias_in=None):
    slots = min(experts, 2)
    WALL = CB * F + FB * C
    PIECE = -(-WALL // CHUNKS)
    STRIDE = (WALL - PIECE) // (CHUNKS - 1)
    with phase(nc, name) as ph:
        w = ph.sb("w", [128, WALL])
        w16 = ph.sb("w16", [128, slots, 2, WALL], F16)
        hidden = ph.sb("hidden", [128, 2, FB, COLS], F16)
        h32 = ph.sb("h32", [128, 4, HALVES[0][1]])
        bias = ph.sb("bias", [128, FB])
        gain_s = ph.sb("gain_s", [128, CB])
        up = ph.ps("up", [128, 4, 512])
        down = ph.ps("down", [128, 4, 512])
        s_w, s_high, s_low, s_gain, s_through, s_bias, s_pace = (
            ph.sem(x) for x in ("w", "high", "low", "gain", "through", "bias", "pace"))
        s_up, s_h32, s_hidden, s_down, s_added = (ph.sem(x) for x in ("up", "h32", "hidden", "down", "added"))
        ph.ahead(s_h32, s_hidden, s_added)
        units = FB * len(HALVES)
        w1_32 = w[:, 0:CB * F].rearrange("p (b n) -> p b n", b=CB)

        def part(s, k, layer, b, at, n):
            start = b * F + at if layer == 0 else CB * F + b * C + at
            return w16[:, s, k, start:start + n]

        with nc.Block() as block:

            @block.sync
            def _(sp):
                def load(e):
                    sp.dma_start(w1_32, W1(e).rearrange("(b p) n -> p b n", p=128)).then_inc(s_w, 16)
                    sp.dma_start(w[:, CB * F:].rearrange("p (b n) -> p b n", b=FB),
                                 W2(e).rearrange("(b p) n -> p b n", p=128)).then_inc(s_w, 16)

                load(0)
                if experts > 1:
                    sp.wait_ge(s_low, 1)
                    load(1)
                    with sp.Fori(1, experts) as e:
                        sp.wait_ge(s_low, e * CHUNKS + 1)
                        load((e + 1) % experts)
                    sp.wait_ge(s_w, 32 * (experts + 1))

            @block.tensor
            def _(pe):
                if bias_in is not None:
                    pe.wait_ge(s_w, 32)
                    for f in range(FB):
                        for b in range(CB):
                            ins = pe.matmul(down[:, 0, f:f + 1], w1_32[:, b, f * 128:(f + 1) * 128],
                                            bias_in[:, b:b + 1], start=(b == 0), stop=(b == CB - 1))
                    ins.then_inc(s_through, 1)
                    pe.wait_ge(s_bias, 1)
                with pe.Fori(0, max(experts // 2, 1)) as i:
                    for s in range(slots):
                        e = i * slots + s
                        pe.wait_ge(s_low, e * CHUNKS + 1)
                        pe.sem_inc(s_pace, 1)
                        with pe.Fori(0, CHUNKS) as c:
                            step = e * CHUNKS + c
                            for u in range(units):
                                f, (at, n) = u // 2, HALVES[u % 2]
                                pe.wait_ge(s_h32, step * units + max(u - 3, 0) + AHEAD)
                                product(pe, up[:, u % 4, 0:n], lambda k, b: part(s, k, 0, b, f * 128, 128),
                                        lambda k, b: m.zc[:, k, b, bass.ds(c * COLS + at, n)]).then_inc(s_up, 1)
                            for j in range(J):
                                if j == 0 or j == 4:
                                    pe.wait_ge(s_added, step * J + j // 4 + AHEAD)
                                for f in range(FB):
                                    if j == 0:
                                        pe.wait_ge(s_hidden, step * units + 2 * (f + 1) + AHEAD)
                                    for n, (k, r) in enumerate(((0, 0), (1, 0), (0, 1))):
                                        ins = pe.matmul(down[0:R, j % 4, 0:C], hidden[:, k, f, j * R:(j + 1) * R],
                                                        part(s, r, 1, f, 0, C), start=(f + n == 0),
                                                        stop=(f == FB - 1 and n == 2))
                                ins.then_inc(s_down, 1)

            @block.scalar
            def _(act):
                act.wait_ge(s_w, 32)
                if gain is None:
                    act.activation(w16[:, 0, 0, :], w[:, :], ACT.Copy, scale=WS).then_inc(s_high, 1)
                else:
                    act.wait_ge(s_gain, 1)
                    for b in range(CB):
                        act.activation(w16[:, 0, 0, b * F:(b + 1) * F], w[:, b * F:(b + 1) * F], ACT.Copy,
                                       scale=gain_s[:, b:b + 1])
                    act.activation(w16[:, 0, 0, CB * F:], w[:, CB * F:], ACT.Copy, scale=WS).then_inc(s_high, 1)
                    act.wait_ge(s_bias, 1)
                with act.Fori(0, max(experts // 2, 1)) as i:
                    for s in range(slots):
                        e = i * slots + s
                        if bias_in is None:
                            act.wait_ge(s_h32, e * (units * CHUNKS) + AHEAD)
                            act.sem_inc(s_pace, 1)
                            act.activation(bias[:, :], b1[:, bass.ds(e * FB, FB)], ACT.Copy).then_inc(s_bias, 1)
                            act.wait_ge(s_bias, e + 1)
                        with act.Fori(0, CHUNKS) as c:
                            step = e * CHUNKS + c
                            for u in range(units):
                                f, (at, n) = u // 2, HALVES[u % 2]
                                act.wait_ge(s_up, step * units + (u + 1))
                                act.wait_ge(s_hidden, step * units + max(u - 3, 0) + AHEAD)
                                act.activation(h32[:, u % 4, 0:n], up[:, u % 4, 0:n], ACT.Gelu, scale=1.0 / WS,
                                               bias=bias[:, f:f + 1])
                                act.activation(hidden[:, 0, f, at:at + n], up[:, u % 4, 0:n], ACT.Gelu,
                                               scale=1.0 / WS, bias=bias[:, f:f + 1]).then_inc(s_h32, 1)
                            if experts > 1:
                                act.wait_ge(s_w, (e + 2) * 32)
                                act.sem_inc(s_pace, 1)
                                piece = bass.ds(c * STRIDE, PIECE)
                                act.activation(w16[:, 1 - s, 0, piece], w[:, piece], ACT.Copy, scale=WS)\
                                    .then_inc(s_high, 1)

            @block.vector
            def _(dve):
                if gain is not None:
                    dve.tensor_scalar(gain_s[:, :], gain, WS, None, ALU.mult).then_inc(s_gain, 1)
                    dve.wait_ge(s_gain, 1)
                dve.wait_ge(s_high, 1)
                if gain is None:
                    ins = dve.scalar_tensor_tensor(out=w16[:, 0, 1, :], in0=w[:, :], scalar=WS, in1=w16[:, 0, 0, :],
                                                   op0=ALU.mult, op1=ALU.subtract)
                else:
                    for b in range(CB):
                        at = slice(b * F, (b + 1) * F)
                        dve.scalar_tensor_tensor(out=w16[:, 0, 1, at], in0=w[:, at], scalar=gain_s[:, b:b + 1],
                                                 in1=w16[:, 0, 0, at], op0=ALU.mult, op1=ALU.subtract)
                    ins = dve.scalar_tensor_tensor(out=w16[:, 0, 1, CB * F:], in0=w[:, CB * F:], scalar=WS,
                                                   in1=w16[:, 0, 0, CB * F:], op0=ALU.mult, op1=ALU.subtract)
                ins.then_inc(s_low, 1)
                if bias_in is not None:
                    dve.wait_ge(s_through, 1)
                    dve.tensor_tensor(bias[:, :], down[:, 0, 0:FB], b1, ALU.add).then_inc(s_bias, 1)
                with dve.Fori(0, max(experts // 2, 1)) as i:
                    for s in range(slots):
                        e = i * slots + s
                        with dve.Fori(0, CHUNKS) as c:
                            step = e * CHUNKS + c
                            for u in range(units):
                                f, (at, n) = u // 2, HALVES[u % 2]
                                dve.wait_ge(s_h32, step * units + (u + 1) + AHEAD)
                                dve.tensor_tensor(hidden[:, 1, f, at:at + n], h32[:, u % 4, 0:n],
                                                  hidden[:, 0, f, at:at + n], ALU.subtract).then_inc(s_hidden, 1)
                            if experts > 1:
                                dve.wait_ge(s_high, step + 2)
                                piece = bass.ds(c * STRIDE, PIECE)
                                dve.scalar_tensor_tensor(out=w16[:, 1 - s, 1, piece], in0=w[:, piece], scalar=WS,
                                                         in1=w16[:, 1 - s, 0, piece], op0=ALU.mult,
                                                         op1=ALU.subtract).then_inc(s_low, 1)
                            for j in range(J):
                                t = c * J + j
                                dve.wait_ge(s_down, step * J + (j + 1))
                                dve.scalar_tensor_tensor(
                                    out=m.x[:, t, :], in0=down[0:R, j % 4, 0:C],
                                    scalar=1.0 / WS if gate is None else gate[:, t, bass.ds(e, 1)], in1=m.x[:, t, :],
                                    op0=ALU.mult, op1=ALU.add).then_inc(s_added, 1)


def mixer0(nc, m, a):
    with phase(nc, "mix") as ph:
        wx = ph.sb("wx", [128, CB, C])
        wo = ph.sb("wo", [128, CB, C])
        QV = X8 * KR + C
        wqv = ph.sb("wqv", [128, CB, QV])
        wk = ph.sb("wk", [128, CB, X8 * KR])
        mine = ph.sb("mine", [X8 * KR, X8, HD])
        mixed = ph.sb("mixed", [128, CB, COLS])
        k_cols = ph.sb("k_cols", [X8 * KR, N])
        q = ph.sb("q", [R, T * X8, KR])
        qstat = ph.sb("qstat", [R, T * X8])
        kmax = ph.sb("kmax", [X8 * KR, 1])
        ksums = ph.sb("ksums", [X8 * KR, CHUNKS])
        ksum = ph.sb("ksum", [X8 * KR, 1])
        ek = ph.sb("ek", [X8 * KR, COLS])
        ek_rows = ph.sb("ek_rows", [R, J, X8 * KR])
        kv = ph.sb("kv", [X8 * KR, C])
        kv_cols = ph.sb("kv_cols", [128, CB, X8 * KR])
        read = ph.sb("read", [X8 * KR, C])
        qc = ph.sb("qc", [R, J, X8 * KR])
        q_cols = ph.sb("q_cols", [X8 * KR, COLS])
        bank4 = ph.ps("bank4", [128, 4, 512])
        kbank = ph.ps("kbank", [X8 * KR, 2, 512])
        rbank = ph.ps("rbank", [R, 2, 512])
        s_w, s_zero, s_mask, s_bd = ph.sem("w"), ph.sem("zero"), ph.sem("mask"), ph.sem("bd")
        s_mix, s_mixed, s_k, s_kout, s_qv, s_qvout = (ph.sem(x) for x in ("mix", "mixed", "k", "kout", "qv", "qvout"))
        s_v, s_kmax, s_ek, s_ekt, s_ekr, s_kv, s_kvadd = (ph.sem(x) for x in ("v", "kmax", "ek", "ekt", "ekr", "kv", "kvadd"))
        s_kvm, s_kvt, s_kvc, s_read, s_readout = (ph.sem(x) for x in ("kvm", "kvt", "kvc", "read", "readout"))
        s_qmax, s_qexp, s_qc, s_qt, s_qcols, s_at, s_fx = (ph.sem(x) for x in ("qmax", "qexp", "qc", "qt", "qcols", "at", "fx"))
        s_act = ph.sem("act")
        bo, b2 = m.row["L0_mix_bo"], m.row["L0_mix_b2"]
        nbd = 3 * X8
        ph.ahead(s_ekr, s_ekt, s_fx, s_kout, s_kv, s_kvadd, s_mixed, s_qcols, s_qt, s_qv, s_qvout)
        with nc.Block() as block:

            @block.gpsimd
            def _(pool):
                pool.memset(wqv[:, :, :], 0.0).then_inc(s_zero, 1)
                pool.memset(wk[:, :, :], 0.0).then_inc(s_zero, 1)
                pool.memset(mine[:, :, :], 1.0).then_inc(s_mask, 1)
                pool.wait_ge(s_mask, 1)
                pool.affine_select(out=mine[:, :, :], in_=mine[:, :, :], compare_op=ALU.is_ge, fill=0.0, base=0,
                                   pattern=[[-KR, X8], [0, HD]], channel_multiplier=1).then_inc(s_mask, 1)
                pool.wait_ge(s_mask, 2)
                pool.affine_select(out=mine[:, :, :], in_=mine[:, :, :], compare_op=ALU.is_ge, fill=0.0,
                                   base=KR - 1, pattern=[[KR, X8], [0, HD]], channel_multiplier=-1)\
                    .then_inc(s_mask, 1)

            @block.sync
            def _(sp):
                sp.dma_start(wx[:, :, :], a["L0_mix_Wx"].rearrange("(b p) n -> p b n", p=128)).then_inc(s_w, 16)
                sp.dma_start(wo[:, :, :], a["L0_mix_Wo"].rearrange("(b p) n -> p b n", p=128)).then_inc(s_w, 16)
                sp.wait_ge(s_zero, 2)
                for h in range(X8):
                    p = slice(HD * (h % 4), HD * (h % 4) + HD)
                    sp.dma_start(wqv[p, h // 4, KR * h:KR * h + KR], a["L0_mix_Wq"]).then_inc(s_bd, 16)
                    sp.dma_start(wk[p, h // 4, KR * h:KR * h + KR], a["L0_mix_Wk"]).then_inc(s_bd, 16)
                    at = X8 * KR + HD * h
                    sp.dma_start(wqv[p, h // 4, at:at + HD], a["L0_mix_Wv"]).then_inc(s_bd, 16)

            @block.tensor
            def _(pe):
                pe.wait_ge(s_w, 32)
                pe.wait_ge(s_bd, 16 * nbd)
                pe.sem_inc(s_act, 1)
                with pe.Fori(0, CHUNKS) as c:
                    for u in range(4):
                        o, (at, n) = u // 2, HALVES[u % 2]
                        if u == 0:
                            pe.wait_ge(s_mixed, c * 4 + AHEAD)
                        for b in range(CB):
                            ins = pe.matmul(bank4[:, u, 0:n], wx[:, b, o * 128:(o + 1) * 128],
                                            m.z_cols[:, b, bass.ds(c * COLS + at, n)],
                                            start=(b == 0), stop=(b == CB - 1))
                        ins.then_inc(s_mix, 1)
                    pe.wait_ge(s_mixed, c * 4 + 4 + AHEAD)
                    pe.wait_ge(s_kout, c * 2 + AHEAD)
                    for u, (at, n) in enumerate(HALVES):
                        for b in range(CB):
                            ins = pe.matmul(kbank[:, u, 0:n], wk[:, b, :], mixed[:, b, at:at + n],
                                            start=(b == 0), stop=(b == CB - 1))
                        ins.then_inc(s_k, 1)
                    for j in range(J):
                        pe.wait_ge(s_qvout, (c * J + (j - 1) if j else c * J) + AHEAD)
                        for b in range(CB):
                            ins = pe.matmul(rbank[:, j % 2, 0:QV], mixed[:, b, j * R:(j + 1) * R], wqv[:, b, :],
                                            start=(b == 0), stop=(b == CB - 1))
                        ins.then_inc(s_qv, 1)
                with pe.Fori(0, CHUNKS) as c:
                    pe.wait_ge(s_ek, c + 1)
                    pe.wait_ge(s_ekr, c + AHEAD)
                    pe.wait_ge(s_qvout, CHUNKS * J + AHEAD)
                    pe.sem_inc(s_act, 1)
                    for j in range(J):
                        ins = pe.transpose(rbank[:, 0, j * X8 * KR:(j + 1) * X8 * KR], ek[:, j * R:(j + 1) * R],
                                           m.ident[0:X8 * KR, 0:X8 * KR])
                    ins.then_inc(s_ekt, 1)
                    pe.wait_ge(s_ekr, c + 1 + AHEAD)
                    pe.wait_ge(s_kvadd, c + AHEAD)
                    for j in range(J):
                        ins = pe.matmul(kbank[:, 0, 0:C], ek_rows[:, j, :], m.y[:, c * J + j, :],
                                        start=(j == 0), stop=(j == J - 1))
                    ins.then_inc(s_kv, 1)
                pe.wait_ge(s_kvm, 1)
                for b in range(CB):
                    ins = pe.transpose(bank4[:, 0, b * X8 * KR:(b + 1) * X8 * KR], kv[:, b * 128:(b + 1) * 128],
                                       m.ident[0:X8 * KR, 0:X8 * KR])
                ins.then_inc(s_kvt, 1)
                pe.wait_ge(s_kvc, 1)
                for b in range(CB):
                    ins = pe.matmul(kbank[:, 1, 0:C], kv_cols[:, b, :], wo[:, b, :], start=(b == 0), stop=(b == CB - 1))
                ins.then_inc(s_read, 1)
                pe.wait_ge(s_readout, 1)
                with pe.Fori(0, CHUNKS) as c:
                    pe.wait_ge(s_qc, c + 1)
                    pe.wait_ge(s_qcols, c + AHEAD)
                    for j in range(J):
                        ins = pe.transpose(bank4[0:X8 * KR, j // 4, (j % 4) * R:(j % 4 + 1) * R], qc[:, j, :],
                                           m.ident[0:R, 0:R])
                    ins.then_inc(s_qt, 1)
                    pe.wait_ge(s_qcols, c + 1 + AHEAD)
                    for j in range(J):
                        pe.wait_ge(s_fx, (c * J + (j - 1) if j else c * J) + AHEAD)
                        pe.matmul(rbank[:, j % 2, 0:C], q_cols[:, j * R:(j + 1) * R], read[:, :],
                                  start=True, stop=True).then_inc(s_at, 1)

            @block.scalar
            def _(act):
                with act.Fori(0, CHUNKS) as c:
                    for u in range(4):
                        o, (at, n) = u // 2, HALVES[u % 2]
                        act.wait_ge(s_mix, c * 4 + (u + 1))
                        if u == 0:
                            act.wait_ge(s_qv, c * J + AHEAD)
                        act.activation(mixed[:, o, at:at + n], bank4[:, u, 0:n], ACT.Identity,
                                       bias=m.col["L0_mix_bx"][:, o:o + 1]).then_inc(s_mixed, 1)
                    for u, (at, n) in enumerate(HALVES):
                        act.wait_ge(s_k, c * 2 + (u + 1))
                        act.activation(k_cols[:, bass.ds(c * COLS + at, n)], kbank[:, u, 0:n], ACT.Copy)\
                            .then_inc(s_kout, 1)
                act.wait_ge(s_kmax, 1)
                with act.Fori(0, CHUNKS) as c:
                    act.wait_ge(s_ekt, c + AHEAD)
                    act.activation(ek[:, :], k_cols[:, bass.ds(c * COLS, COLS)], ACT.Exp, bias=kmax[:, :],
                                   accum_out=ksums[:, bass.ds(c, 1)]).then_inc(s_ek, 1)
                act.wait_ge(s_qmax, 1)
                act.activation(q[:, :, :], q[:, :, :], ACT.Exp).then_inc(s_qexp, 1)

            @block.vector
            def _(dve):
                v = Chain(dve, s_v)
                q_t = q[:, :, :].rearrange("p (t h) k -> p t (h k)", t=T)
                with dve.Fori(0, CHUNKS) as c:
                    for j in range(J):
                        dve.wait_ge(s_qv, c * J + (j + 1) + AHEAD)
                        dve.tensor_copy(q_t[:, c * J + j, :], rbank[:, j % 2, 0:X8 * KR])
                        dve.tensor_copy(m.y[:, c * J + j, :], rbank[:, j % 2, X8 * KR:QV]).then_inc(s_qvout, 1)
                dve.wait_ge(s_kout, 2 * CHUNKS + AHEAD)
                v.link(dve.tensor_reduce(kmax[:, :], k_cols[:, :], AX_X, ALU.max))
                dve.tensor_scalar(kmax[:, :], kmax[:, :], -1.0, None, ALU.mult).then_inc(s_kmax, 1)
                dve.wait_ge(s_qvout, T + AHEAD)
                v.link(dve.tensor_reduce(qstat[:, :], q[:, :, :], AX_X, ALU.max))
                v.link(dve.tensor_tensor(q[:, :, :], q[:, :, :], repeat_last(qstat[:, :], KR), ALU.subtract))
                v.done(s_qmax)
                v.link(dve.memset(kv[:, :], 0.0))
                with dve.Fori(0, CHUNKS) as c:
                    v.enter(c, 1)
                    dve.wait_ge(s_ekt, c + 1 + AHEAD)
                    dve.wait_ge(s_kv, c + AHEAD)
                    dve.tensor_copy(ek_rows[:, :, :].rearrange("p j k -> p (j k)"), rbank[:, 0, 0:J * X8 * KR])\
                        .then_inc(s_ekr, 1)
                    dve.wait_ge(s_kv, c + 1 + AHEAD)
                    v.link(dve.tensor_tensor(kv[:, :], kv[:, :], kbank[:, 0, 0:C], ALU.add))
                    dve.sem_inc(s_kvadd, 1)
                v.leave(CHUNKS)
                dve.wait_ge(s_mask, 3)
                dve.tensor_tensor(kv[:, :], kv[:, :], mine[:, :, :].rearrange("p h d -> p (h d)"), ALU.mult)\
                    .then_inc(s_kvm, 1)
                dve.wait_ge(s_kvt, 1)
                dve.tensor_copy(kv_cols[:, :, :].rearrange("p b k -> p (b k)"), bank4[:, 0, 0:CB * X8 * KR])\
                    .then_inc(s_kvc, 1)
                v.link(dve.tensor_reduce(ksum[:, :], ksums[:, :], AX_X, ALU.add))
                v.link(dve.reciprocal(ksum[:, :], ksum[:, :]))
                dve.wait_ge(s_read, 1)
                dve.tensor_scalar(read[:, :], kbank[:, 1, 0:C], ksum[:, :], None, ALU.mult).then_inc(s_readout, 1)
                dve.wait_ge(s_qexp, 1)
                v.link(dve.tensor_reduce(qstat[:, :], q[:, :, :], AX_X, ALU.add))
                v.link(dve.reciprocal(qstat[:, :], qstat[:, :]))
                with dve.Fori(0, CHUNKS) as c:
                    v.enter(c, 3 * J)
                    dve.wait_ge(s_qt, c + AHEAD)
                    dve.tensor_tensor(qc[:, :, :].rearrange("p j (h k) -> p (j h) k", k=KR),
                                      q[:, bass.ds(c * J * X8, J * X8), :],
                                      repeat_last(qstat[:, bass.ds(c * J * X8, J * X8)], KR), ALU.mult)\
                        .then_inc(s_qc, 1)
                    dve.wait_ge(s_qt, c + 1 + AHEAD)
                    dve.tensor_copy(q_cols[:, 0:4 * R], bank4[0:X8 * KR, 0, 0:4 * R])
                    dve.tensor_copy(q_cols[:, 4 * R:5 * R], bank4[0:X8 * KR, 1, 0:R]).then_inc(s_qcols, 1)
                    for j in range(J):
                        y = m.y[:, c * J + j, :]
                        x = m.x[:, c * J + j, :]
                        dve.wait_ge(s_at, c * J + (j + 1))
                        dve.tensor_tensor(y, rbank[:, j % 2, 0:C], bo, ALU.add).then_inc(s_fx, 1)
                        dve.wait_ge(s_fx, c * J + (j + 1) + AHEAD)
                        v.link(dve.tensor_tensor(y, y, m.z[:, c * J + j, :], ALU.add))
                        v.link(dve.tensor_tensor(x, x, y, ALU.add))
                        v.link(dve.tensor_tensor(x, x, b2, ALU.add))
                v.leave(CHUNKS)


def router(nc, m, name, Wr, br, top2, bias2, bias_row=None):
    with phase(nc, name) as ph:
        wr = ph.sb("wr", [128, CB, X8])
        b2 = ph.sb("b2", [X8, C])
        wr16 = ph.sb("wr16", [128, 2, CB, X8], F16)
        stat = ph.sb("stat", [R, 2, T])
        work = ph.sb("work", [R, 2, T, X8])
        prefer = ph.sb("prefer", [R, X8])
        gc = ph.sb("gc", [R, J, X8])
        g_cols = ph.sb("g_cols", [X8, COLS])
        score = ph.ps("score", [R, J, X8])
        turned = ph.ps("turned", [X8, 2, 512])
        bank = ph.ps("bank", [R, 2, 512])
        s_w, s_split, s_score, s_read, s_exp, s_gone, s_v = (ph.sem(x) for x in ("w", "split", "score", "read", "exp", "gone", "v"))
        s_gc, s_turned, s_gcols, s_prod, s_added, s_pace = (ph.sem(x) for x in ("gc", "turned", "gcols", "prod", "added", "pace"))
        s_prefer = ph.sem("prefer")
        gate = m.gate
        ph.ahead(s_added, s_gcols, s_prod, s_read, s_score, s_turned)
        with nc.Block() as block:

            @block.sync
            def _(sp):
                sp.dma_start(wr[:, :, :], Wr.rearrange("(b p) n -> p b n", p=128)).then_inc(s_w, 16)
                sp.dma_start(b2[:, :], bias2).then_inc(s_w, 16)

            @block.gpsimd
            def _(pool):
                pool.iota(prefer[:, :], pattern=[[-1, X8]], base=X8, channel_multiplier=0,
                          allow_small_or_imprecise_dtypes=True).then_inc(s_prefer, 1)

            @block.scalar
            def _(act):
                act.wait_ge(s_w, 32)
                act.activation(wr16[:, 0, :, :], wr[:, :, :], ACT.Copy, scale=WS).then_inc(s_split, 1)
                act.wait_ge(s_exp, 1)
                act.activation(gate[:, :, :], gate[:, :, :], ACT.Exp).then_inc(s_gone, 1)

            @block.tensor
            def _(pe):
                pe.wait_ge(s_split, 2)
                with pe.Fori(0, CHUNKS) as c:
                    pe.wait_ge(s_read, c + AHEAD)
                    for j in range(J):
                        ins = product(pe, score[:, j, :], lambda k, b: m.zc[:, k, b, bass.ds(c * COLS + j * R, R)],
                                      lambda k, b: wr16[:, k, b, :])
                    ins.then_inc(s_score, 1)
                with pe.Fori(0, CHUNKS) as c:
                    pe.wait_ge(s_gc, c + 1)
                    pe.wait_ge(s_gcols, c + AHEAD)
                    pe.sem_inc(s_pace, 1)
                    for j in range(J):
                        ins = pe.transpose(turned[:, j // 4, (j % 4) * R:(j % 4 + 1) * R], gc[:, j, :],
                                           m.ident[0:R, 0:R])
                    ins.then_inc(s_turned, 1)
                    pe.wait_ge(s_gcols, c + 1 + AHEAD)
                    for j in range(J):
                        pe.wait_ge(s_added, (c * J + (j - 1) if j else c * J) + AHEAD)
                        pe.matmul(bank[:, j % 2, 0:C], g_cols[:, j * R:(j + 1) * R], b2[:, :],
                                  start=True, stop=True).then_inc(s_prod, 1)

            @block.vector
            def _(dve):
                v = Chain(dve, s_v)
                dve.wait_ge(s_split, 1)
                dve.scalar_tensor_tensor(out=wr16[:, 1, :, :], in0=wr[:, :, :], scalar=WS, in1=wr16[:, 0, :, :],
                                         op0=ALU.mult, op1=ALU.subtract).then_inc(s_split, 1)
                with dve.Fori(0, CHUNKS) as c:
                    dve.wait_ge(s_score, c + 1 + AHEAD)
                    some = gate[:, bass.ds(c * J, J), :]
                    if br is None:
                        ins = dve.tensor_scalar(some, score[:, :, :], 1.0 / WS, None, ALU.mult)
                    else:
                        ins = dve.scalar_tensor_tensor(out=some, in0=score[:, :, :], scalar=1.0 / WS,
                                                       in1=repeat_mid(br, J), op0=ALU.mult, op1=ALU.add)
                    ins.then_inc(s_read, 1)
                dve.wait_ge(s_read, CHUNKS + AHEAD)
                v.link(dve.tensor_reduce(stat[:, 0, :], gate[:, :, :], AX_X, ALU.max))
                v.link(dve.tensor_tensor(gate[:, :, :], gate[:, :, :], repeat_last(stat[:, 0, :], X8), ALU.subtract))
                v.done(s_exp)
                dve.wait_ge(s_gone, 1)
                v.link(dve.tensor_reduce(stat[:, 0, :], gate[:, :, :], AX_X, ALU.add))
                v.link(dve.reciprocal(stat[:, 0, :], stat[:, 0, :]))
                v.link(dve.tensor_tensor(gate[:, :, :], gate[:, :, :], repeat_last(stat[:, 0, :], X8), ALU.mult))
                if top2:
                    left, pick = work[:, 0, :, :], work[:, 1, :, :]
                    v.link(dve.tensor_copy(left, gate[:, :, :]))
                    dve.wait_ge(s_prefer, 1)
                    for _ in range(2):
                        v.link(dve.tensor_reduce(stat[:, 0, :], left, AX_X, ALU.max))
                        v.link(dve.tensor_tensor(pick, left, repeat_last(stat[:, 0, :], X8), ALU.is_equal))
                        v.link(dve.tensor_tensor(pick, pick, repeat_mid(prefer[:, :], T), ALU.mult))
                        v.link(dve.tensor_reduce(stat[:, 1, :], pick, AX_X, ALU.max))
                        v.link(dve.tensor_tensor(pick, pick, repeat_last(stat[:, 1, :], X8), ALU.is_equal))
                        v.link(dve.scalar_tensor_tensor(out=left, in0=pick, scalar=-4.0, in1=left,
                                                        op0=ALU.mult, op1=ALU.add))
                    v.link(dve.tensor_scalar(pick, left, -1.0, None, ALU.is_lt))
                    v.link(dve.tensor_tensor(gate[:, :, :], gate[:, :, :], pick, ALU.mult))
                    v.link(dve.tensor_reduce(stat[:, 0, :], gate[:, :, :], AX_X, ALU.add))
                    v.link(dve.reciprocal(stat[:, 0, :], stat[:, 0, :]))
                    v.link(dve.tensor_tensor(gate[:, :, :], gate[:, :, :], repeat_last(stat[:, 0, :], X8), ALU.mult))
                with dve.Fori(0, CHUNKS) as c:
                    if bias_row is not None:
                        v.enter(c, 1)
                        dve.wait_ge(s_added, c * J + AHEAD)
                        chunk = m.x[:, bass.ds(c * J, J), :]
                        v.link(dve.tensor_tensor(chunk, chunk, repeat_mid(bias_row, J), ALU.add))
                    dve.wait_ge(s_turned, c + AHEAD)
                    dve.tensor_copy(gc[:, :, :], gate[:, bass.ds(c * J, J), :]).then_inc(s_gc, 1)
                    dve.wait_ge(s_turned, c + 1 + AHEAD)
                    dve.wait_ge(s_prod, c * J + AHEAD)
                    dve.tensor_copy(g_cols[:, 0:4 * R], turned[:, 0, 0:4 * R])
                    dve.tensor_copy(g_cols[:, 4 * R:5 * R], turned[:, 1, 0:R]).then_inc(s_gcols, 1)
                    for j in range(J):
                        x = m.x[:, c * J + j, :]
                        dve.wait_ge(s_prod, c * J + (j + 1) + AHEAD)
                        dve.tensor_tensor(x, x, bank[:, j % 2, 0:C], ALU.add).then_inc(s_added, 1)
                if bias_row is not None:
                    v.leave(CHUNKS)
                dve.wait_ge(s_turned, CHUNKS + AHEAD)
                v.link(dve.tensor_scalar(gate[:, :, :], gate[:, :, :], 1.0 / WS, None, ALU.mult))


def experts0(nc, m, a):
    with phase(nc, "ex0") as ph:
        NV = X8 * CB
        WALL = 3 * CB * C
        PIECE = -(-WALL // CHUNKS)
        STRIDE = (WALL - PIECE) // (CHUNKS - 1)
        w = ph.sb("w", [128, WALL])
        w16 = ph.sb("w16", [128, 2, 2, WALL], F16)
        scale = ph.sb("scale", [128, 2, NV])
        shift = ph.sb("shift", [128, 2, NV])
        now = ph.sb("now", [128, 2, 2, CB])
        bn_eps = ph.sb("bn_eps", [128, 1])
        h32 = ph.sb("h32", [128, 4, HALVES[0][1]])
        h1 = ph.sb("h1", [128, 2, CB, COLS], F16)
        h2 = ph.sb("h2", [128, 2, CB, COLS], F16)
        up = ph.ps("up", [128, 4, 512])
        down = ph.ps("down", [R, 4, 512])
        s_w, s_high, s_low, s_now = (ph.sem(x) for x in ("w", "high", "low", "now"))
        s_eps, s_sd, s_bn, s_v = (ph.sem(x) for x in ("eps", "sd", "bn", "v"))
        s_up, s_h32, s_h, s_down, s_added, s_pace = (ph.sem(x) for x in ("up", "h32", "h", "down", "added", "pace"))
        col = m.col
        ph.ahead(s_added, s_down, s_h32, s_h)

        def part(s, k, layer, b, at, n):
            start = (layer * CB + b) * C + at
            return w16[:, s, k, start:start + n]

        with nc.Block() as block:

            @block.sync
            def _(sp):
                def load(e):
                    for k, W in enumerate((a["L0_ffn_W1"], a["L0_ffn_W2"], a["L0_ffn_Wo"])):
                        sp.dma_start(w[:, k * CB * C:(k + 1) * CB * C].rearrange("p (b n) -> p b n", b=CB),
                                     W[bass.ds(e, 1), :, :].rearrange("e (b p) n -> p (e b) n", p=128))\
                            .then_inc(s_w, 16)

                load(0)
                sp.wait_ge(s_low, 1)
                load(1)
                with sp.Fori(1, X8) as e:
                    sp.wait_ge(s_low, e * CHUNKS + 1)
                    load((e + 1) % X8)
                sp.wait_ge(s_w, 48 * (X8 + 1))

            @block.tensor
            def _(pe):
                with pe.Fori(0, X8 // 2) as i:
                    for s in range(2):
                        e = i * 2 + s
                        pe.wait_ge(s_low, e * CHUNKS + 1)
                        pe.sem_inc(s_pace, 1)
                        with pe.Fori(0, CHUNKS) as c:
                            step = e * CHUNKS + c
                            for u in range(8):
                                layer, (at, n), o = u // 4, HALVES[u // 2 % 2], u % 2
                                if u < 4:
                                    pe.wait_ge(s_h32, step * 8 + max(u - 3, 0) + AHEAD)
                                elif u == 4 or u == 6:
                                    pe.wait_ge(s_h, step * 8 + (u - 2) + AHEAD)
                                product(pe, up[:, u % 4, 0:n], lambda k, b: part(s, k, layer, b, o * 128, 128),
                                        (lambda k, b: m.zc[:, k, b, bass.ds(c * COLS + at, n)]) if layer == 0 else
                                        (lambda k, b: h1[:, k, b, at:at + n])).then_inc(s_up, 1)
                            for j in range(J):
                                if j == 0:
                                    pe.wait_ge(s_added, step * J + AHEAD)
                                    pe.wait_ge(s_h, step * 8 + 6 + AHEAD)
                                elif j == 2:
                                    pe.wait_ge(s_h, step * 8 + 8 + AHEAD)
                                elif j == 4:
                                    pe.wait_ge(s_added, step * J + 1 + AHEAD)
                                product(pe, down[:, j % 4, 0:C], lambda k, b: h2[:, k, b, j * R:(j + 1) * R],
                                        lambda k, b: part(s, k, 2, b, 0, C)).then_inc(s_down, 1)

            @block.scalar
            def _(act):
                act.wait_ge(s_eps, 1)
                act.activation(scale[:, 0, :], col["L0_ffn_v1"], ACT.Sqrt, bias=bn_eps[:, :])
                act.activation(scale[:, 1, :], col["L0_ffn_v2"], ACT.Sqrt, bias=bn_eps[:, :]).then_inc(s_sd, 1)
                act.wait_ge(s_w, 48)
                act.activation(w16[:, 0, 0, :], w[:, :], ACT.Copy, scale=WS).then_inc(s_high, 1)
                act.wait_ge(s_bn, 1)
                with act.Fori(0, X8 // 2) as i:
                    for s in range(2):
                        e = i * 2 + s
                        act.wait_ge(s_h, e * (8 * CHUNKS) + AHEAD)
                        act.sem_inc(s_pace, 1)
                        act.activation(now[:, 0, :, :], scale[:, :, bass.ds(e * CB, CB)], ACT.Copy).then_inc(s_now, 1)
                        act.activation(now[:, 1, :, :], shift[:, :, bass.ds(e * CB, CB)], ACT.Copy).then_inc(s_now, 1)
                        act.wait_ge(s_now, e * 2 + 2)
                        with act.Fori(0, CHUNKS) as c:
                            step = e * CHUNKS + c
                            for u in range(8):
                                layer, (at, n), o = u // 4, HALVES[u // 2 % 2], u % 2
                                to = h1 if layer == 0 else h2
                                act.wait_ge(s_up, step * 8 + (u + 1))
                                act.wait_ge(s_h, step * 8 + max(u - 3, 0) + AHEAD)
                                if u == 4:
                                    act.wait_ge(s_down, step * J + AHEAD)
                                for into in (h32[:, u % 4, 0:n], to[:, 0, o, at:at + n]):
                                    ins = act.activation(into, up[:, u % 4, 0:n], ACT.Relu,
                                                         bias=now[:, 1, layer, o:o + 1],
                                                         scale=now[:, 0, layer, o:o + 1])
                                ins.then_inc(s_h32, 1)
                            act.wait_ge(s_w, (e + 2) * 48)
                            act.sem_inc(s_pace, 1)
                            piece = bass.ds(c * STRIDE, PIECE)
                            act.activation(w16[:, 1 - s, 0, piece], w[:, piece], ACT.Copy, scale=WS)\
                                .then_inc(s_high, 1)

            @block.vector
            def _(dve):
                v = Chain(dve, s_v)
                dve.memset(bn_eps[:, :], 1e-3).then_inc(s_eps, 1)
                dve.wait_ge(s_sd, 1)
                v.link(dve.reciprocal(scale[:, :, :], scale[:, :, :]))
                for k in range(2):
                    b, g, be, mean = (col[f"L0_ffn_{x}{k + 1}"] for x in ("b", "g", "be", "m"))
                    v.link(dve.tensor_tensor(scale[:, k, :], scale[:, k, :], g, ALU.mult))
                    v.link(dve.tensor_tensor(shift[:, k, :], b, mean, ALU.subtract))
                    v.link(dve.tensor_tensor(shift[:, k, :], shift[:, k, :], scale[:, k, :], ALU.mult))
                    v.link(dve.tensor_tensor(shift[:, k, :], shift[:, k, :], be, ALU.add))
                v.link(dve.tensor_scalar(scale[:, :, :], scale[:, :, :], 1.0 / WS, None, ALU.mult))
                v.done(s_bn)
                dve.wait_ge(s_high, 1)
                dve.scalar_tensor_tensor(out=w16[:, 0, 1, :], in0=w[:, :], scalar=WS, in1=w16[:, 0, 0, :],
                                         op0=ALU.mult, op1=ALU.subtract).then_inc(s_low, 1)
                with dve.Fori(0, X8 // 2) as i:
                    for s in range(2):
                        e = i * 2 + s
                        with dve.Fori(0, CHUNKS) as c:
                            step = e * CHUNKS + c
                            for u in range(8):
                                layer, (at, n), o = u // 4, HALVES[u // 2 % 2], u % 2
                                to = h1 if layer == 0 else h2
                                dve.wait_ge(s_h32, step * 8 + (u + 1) + AHEAD)
                                dve.tensor_tensor(to[:, 1, o, at:at + n], h32[:, u % 4, 0:n],
                                                  to[:, 0, o, at:at + n], ALU.subtract).then_inc(s_h, 1)
                            dve.wait_ge(s_high, step + 2)
                            piece = bass.ds(c * STRIDE, PIECE)
                            dve.scalar_tensor_tensor(out=w16[:, 1 - s, 1, piece], in0=w[:, piece], scalar=WS,
                                                     in1=w16[:, 1 - s, 0, piece], op0=ALU.mult,
                                                     op1=ALU.subtract).then_inc(s_low, 1)
                            for j in range(J):
                                t = c * J + j
                                dve.wait_ge(s_down, step * J + (j + 1) + AHEAD)
                                dve.scalar_tensor_tensor(out=m.x[:, t, :], in0=down[:, j % 4, 0:C],
                                                         scalar=m.gate[:, t, bass.ds(e, 1)], in1=m.x[:, t, :],
                                                         op0=ALU.mult, op1=ALU.add).then_inc(s_added, 1)




def turned_weights(nc, m, a):
    plan = [("wq", a["L1_gnn_Wq"], C, C, 1), ("wk", a["L1_gnn_Wk"], C, C, 1), ("wv", a["L1_gnn_Wv"], C, C, 1),
            ("wp", a["L1_gnn_Wp"], C, C, 1), ("w1", a["L1_gnn_W1"], F, C, 1), ("w2", a["L1_gnn_W2"], C, F, 1),
            ("conv", a["L1_mix_w_qkv"].rearrange("o i k -> o (i k)"), 3 * C, C, 5),
            ("res", a["L1_mix_w_res"].rearrange("o i k -> o (i k)"), C, 2 * C, 1)]
    m.turned = {name: nc.dram_tensor(f"turned_{name}", [k, n], F32).ap() for name, _, n, k, _ in plan}
    blocks = [(name, W, o, k, taps) for name, W, n, k, taps in plan for o in range(n // 128)]
    with phase(nc, "tw") as ph:
        wide = max(k * taps for _, _, _, k, taps in plan)
        rows = ph.sb("rows", [128, 2, wide])
        cols = ph.sb("cols", [128, 2, FB, 128])
        bank = ph.ps("bank", [128, 2, FB, 128])
        s_in = [ph.sem(f"in{s}") for s in range(2)]
        s_out = [ph.sem(f"out{s}") for s in range(2)]
        s_turned, s_cols = ph.sem("turned"), ph.sem("cols")
        with nc.Block() as block:

            @block.sync
            def _(sp):
                for i, (name, W, o, k, taps) in enumerate(blocks):
                    if i >= 2:
                        sp.wait_ge(s_turned, i - 1)
                    sp.dma_start(rows[:, i % 2, 0:k * taps], W[o * 128:(o + 1) * 128, :]).then_inc(s_in[i % 2], 16)

            @block.tensor
            def _(pe):
                for i, (name, W, o, k, taps) in enumerate(blocks):
                    pe.wait_ge(s_in[i % 2], 16 * (i // 2 + 1))
                    if i >= 2:
                        pe.wait_ge(s_cols, i - 1)
                    taken = rows[:, i % 2, 0:k * taps].rearrange("p (i k) -> p i k", k=taps)[:, :, taps // 2]
                    for b in range(k // 128):
                        ins = pe.transpose(bank[:, i % 2, b, :], taken[:, b * 128:(b + 1) * 128], m.ident[:, :])
                    ins.then_inc(s_turned, 1)

            @block.vector
            def _(dve):
                for i, (name, W, o, k, taps) in enumerate(blocks):
                    kb = k // 128
                    dve.wait_ge(s_turned, i + 1)
                    if i >= 2:
                        dve.wait_ge(s_out[i % 2], 16 * (i // 2))
                    dve.tensor_copy(cols[:, i % 2, 0:kb, :], bank[:, i % 2, 0:kb, :]).then_inc(s_cols, 1)

            @block.scalar
            def _(act):
                for i, (name, W, o, k, taps) in enumerate(blocks):
                    kb = k // 128
                    act.wait_ge(s_cols, i + 1)
                    act.dma_start(m.turned[name].rearrange("(b p) n -> p b n", p=128)[:, :, o * 128:(o + 1) * 128],
                                  cols[:, i % 2, 0:kb, :]).then_inc(s_out[i % 2], 16)
                n = len(blocks)
                act.wait_ge(s_out[0], 16 * ((n + 1) // 2))
                act.wait_ge(s_out[1], 16 * (n // 2))


def query_rows(nc, m, a):
    with phase(nc, "qkv") as ph:
        w = ph.sb("w", [128, CB, 3 * C])
        zc = ph.sb("zc", [128, CB, COLS])
        out = ph.sb("out", [R, J, 3 * C])
        bias = ph.sb("bias", [R, 3 * C])
        prod = ph.ps("prod", [R, 2, 2, 512])
        s_w, s_bias, s_zc, s_prod, s_out, s_stored = (ph.sem(x) for x in ("w", "bias", "zc", "prod", "out", "stored"))
        ph.ahead(s_out, s_prod, s_stored)
        with nc.Block() as block:

            @block.sync
            def _(sp):
                for i, name in enumerate(("wq", "wk", "wv")):
                    sp.dma_start(w[:, :, i * C:(i + 1) * C], m.turned[name].rearrange("(b p) n -> p b n", p=128))\
                        .then_inc(s_w, 16)
                with sp.Fori(0, CHUNKS) as c:
                    sp.wait_ge(s_out, (c + 1) * J + AHEAD)
                    sp.dma_start(m.gather_q.rearrange("(t p) n -> p t n", p=R)[:, bass.ds(c * J, J), :],
                                 out[:, :, 0:C]).then_inc(s_stored, 16)
                    sp.dma_start(m.gather_kv.rearrange("(t p) n -> p t n", p=R)[:, bass.ds(c * J, J), :],
                                 out[:, :, C:3 * C]).then_inc(s_stored, 16)
                sp.wait_ge(s_stored, 32 * CHUNKS + AHEAD)

            @block.scalar
            def _(act):
                with act.Fori(0, CHUNKS) as c:
                    act.wait_ge(s_prod, c * J + AHEAD)
                    act.activation(zc[:, :, :], m.z_cols[:, :, bass.ds(c * COLS, COLS)], ACT.Copy).then_inc(s_zc, 1)

            @block.tensor
            def _(pe):
                pe.wait_ge(s_w, 48)
                with pe.Fori(0, CHUNKS) as c:
                    pe.wait_ge(s_zc, c + 1)
                    for j in range(J):
                        pe.wait_ge(s_out, (c * J + (j - 1) if j else c * J) + AHEAD)
                        for k, (at, n) in enumerate(((0, 512), (512, 256))):
                            for b in range(CB):
                                ins = pe.matmul(prod[:, j % 2, k, 0:n], zc[:, b, j * R:(j + 1) * R], w[:, b, at:at + n],
                                                start=(b == 0), stop=(b == CB - 1))
                        ins.then_inc(s_prod, 1)

            @block.vector
            def _(dve):
                for i, name in enumerate(("q", "k", "v")):
                    dve.tensor_copy(bias[:, i * C:(i + 1) * C], m.row[f"L1_gnn_b{name}"]).then_inc(s_bias, 1)
                dve.wait_ge(s_bias, 3)
                with dve.Fori(0, CHUNKS) as c:
                    dve.wait_ge(s_stored, c * 32 + AHEAD)
                    for j in range(J):
                        dve.wait_ge(s_prod, c * J + (j + 1) + AHEAD)
                        dve.tensor_tensor(out[:, j, 0:512], prod[:, j % 2, 0, :], bias[:, 0:512], ALU.add)
                        dve.tensor_tensor(out[:, j, 512:768], prod[:, j % 2, 1, 0:256], bias[:, 512:768], ALU.add)\
                            .then_inc(s_out, 1)


def attention_sum(nc, m):
    with phase(nc, "as") as ph:
        W = C + X8
        index = ph.sb("index", [R, SLOTS, 2, J], I32)
        gq = ph.sb("gq", [R, SLOTS, J, C])
        gkv = ph.sb("gkv", [R, SLOTS, J, 2 * C])
        score = ph.sb("score", [R, J * X8])
        node_no = m.z_cols[0:R, 0, :]
        spread = m.z_cols[0:R, 1, 0:J * W].rearrange("p (j w) -> p j w", j=J)
        hot = m.z_cols[0:R, 1, J * W:J * W + J * R].rearrange("p (j r) -> p j r", j=J)
        s_node = ph.sem("node")
        summed = ph.sb("summed", [R, T, W])
        none = ph.sb("none", [R, T, X8])
        total = ph.ps("total", [R, 512])
        s_index, s_got = ph.sem("index"), [ph.sem(f"got{s}") for s in range(SLOTS)]
        s_hot, s_total, s_added, s_zero, s_pace = (ph.sem(x) for x in ("hot", "total", "added", "zero", "pace"))
        s_v, s_score, s_exp, s_spread = (ph.sem(x) for x in ("v", "score", "exp", "spread"))
        with nc.Block() as block:

            def bounds(eng, g):
                first = eng.value_load(m.group_table[0:1, bass.ds(g, 1)], min_val=0, max_val=T - 1)
                count = eng.value_load(m.group_table[0:1, bass.ds(g + G, 1)], min_val=1, max_val=T)
                before = eng.value_load(m.group_table[0:1, bass.ds(g + 2 * G, 1)], min_val=0, max_val=T * G)
                return first, count, before

            @block.gpsimd
            def _(pool):
                pool.iota(node_no[:, :], pattern=[[1, N]], base=0, channel_multiplier=0,
                          allow_small_or_imprecise_dtypes=True).then_inc(s_node, 1)
                with pool.Fori(0, G // SLOTS) as i:
                    for s in range(SLOTS):
                        pool.wait_ge(s_index, i * SLOTS + (s + 1))
                        pool.sem_inc(s_pace, 1)
                        for j in range(J):
                            for into, table, k in ((gkv, m.gather_kv, 0), (gq, m.gather_q, 1)):
                                pool.indirect_dma_start(
                                    out=into[:, s, j, :], out_offset=None, in_=table,
                                    in_offset=bass.IndirectOffsetOnAxis(ap=index[:, s, k, j:j + 1], axis=0)
                                ).then_inc(s_got[s], 16)

            @block.scalar
            def _(act):
                ex = spread[:, :, C:W]
                with act.Fori(0, G) as g:
                    act.wait_ge(s_score, g + 1)
                    act.activation(ex, score[:, :].rearrange("p (j h) -> p j h", j=J), ACT.Exp).then_inc(s_exp, 1)

            @block.vector
            def _(dve):
                v = Chain(dve, s_v)
                dve.memset(summed[:, :, :], 0.0).then_inc(s_zero, 1)
                dve.wait_ge(s_zero, 1)
                dve.wait_ge(s_node, 1)
                for s in range(SLOTS):
                    dve.tensor_copy(index[:, s, 0, :], m.edge_src[:, s, :])
                    dve.tensor_copy(index[:, s, 1, :], m.edge_dsti[:, s, :]).then_inc(s_index, 1)
                with dve.Fori(0, G // SLOTS) as i:
                    v.enter(i, SLOTS * 3)
                    for s in range(SLOTS):
                        g = i * SLOTS + s
                        dve.wait_ge(s_got[s], (i + 1) * (32 * J))
                        kk, vv = gkv[:, s, :, 0:C], gkv[:, s, :, C:2 * C]
                        v.link(dve.tensor_tensor(gq[:, s, :, :], gq[:, s, :, :], kk, ALU.mult))
                        v.link(dve.tensor_reduce(score[:, :], gq[:, s, :, :].rearrange("p j (h d) -> p (j h) d", h=X8),
                                                 AX_X, ALU.add))
                        v.link(dve.tensor_scalar(score[:, :], score[:, :], HD ** -0.5, 10.0, ALU.mult, ALU.min))
                        dve.tensor_scalar(score[:, :], score[:, :], -10.0, None, ALU.max).then_inc(s_score, 1)
                        dve.wait_ge(s_exp, g + 1)
                        dve.tensor_tensor(spread[:, :, 0:C].rearrange("p j (h d) -> p j h d", h=X8),
                                          vv.rearrange("p j (h d) -> p j h d", h=X8),
                                          repeat_last(spread[:, :, C:W], HD), ALU.mult).then_inc(s_spread, 1)
                        first, count, before = bounds(dve, g)
                        with dve.Fori(0, count) as k:
                            tile = dve.snap(nc.s_assert_within(first + k, 0, T - 1))
                            dve.tensor_tensor(hot[:, :, :],
                                              repeat_mid(node_no[:, bass.ds(tile * R, R)], J),
                                              repeat_last(m.edge_dst[:, g, :], R), ALU.is_equal).then_inc(s_hot, 1)
                            dve.wait_ge(s_total, before + k + 1)
                            dve.tensor_tensor(summed[:, tile, :], summed[:, tile, :], total[:, 0:W],
                                              ALU.add).then_inc(s_added, 1)
                            dve.wait_ge(s_added, before + k + 1)
                        dve.wait_ge(s_spread, g + 1)
                        for k, table in enumerate((m.edge_src, m.edge_dsti)):
                            ins = dve.tensor_copy(index[:, s, k, :],
                                                  table[:, bass.ds(g + SLOTS, 1), :].rearrange("p a j -> p (a j)"))
                        ins.then_inc(s_index, 1)
                v.leave(G // SLOTS)
                den = summed[:, :, C:W]
                v.link(dve.tensor_scalar(none[:, :, :], den, 0.0, None, ALU.is_equal))
                v.link(dve.tensor_tensor(none[:, :, :], none[:, :, :], den, ALU.add))
                v.link(dve.reciprocal(none[:, :, :], none[:, :, :]))
                with dve.Fori(0, T) as t:
                    dve.tensor_tensor(m.y[:, t, :].rearrange("p (h d) -> p h d", h=X8),
                                      summed[:, t, 0:C].rearrange("p (h d) -> p h d", h=X8),
                                      repeat_last(none[:, t, :], HD), ALU.mult).then_inc(s_zero, 1)
                dve.wait_ge(s_zero, T + 1)

            @block.tensor
            def _(pe):
                with pe.Fori(0, G) as g:
                    first, count, before = bounds(pe, g)
                    pe.wait_ge(s_spread, g + 1)
                    pe.sem_inc(s_pace, 1)
                    with pe.Fori(0, count) as k:
                        pe.wait_ge(s_hot, before + k + 1)
                        for j in range(J):
                            ins = pe.matmul(total[:, 0:W], hot[:, j, :], spread[:, j, :],
                                            start=(j == 0), stop=(j == J - 1))
                        ins.then_inc(s_total, 1)


def attention_out(nc, m):
    with phase(nc, "ao") as ph:
        w = ph.sb("w", [128, CB, C])
        rows = ph.sb("rows", [R, J, C])
        cols = ph.sb("cols", [128, J, CB, R])
        turned = ph.ps("turned", [128, 2, 512])
        bank = ph.ps("bank", [R, 2, 512])
        s_w, s_rows, s_turned, s_cols, s_prod, s_y, s_v = (ph.sem(x) for x in ("w", "rows", "turned", "cols", "prod", "y", "v"))
        bp, b2 = m.row["L1_gnn_bp"], m.row["L1_gnn_b2"]
        ph.ahead(s_cols, s_prod, s_turned, s_y)
        with nc.Block() as block:

            @block.sync
            def _(sp):
                sp.dma_start(w[:, :, :], m.turned["wp"].rearrange("(b p) n -> p b n", p=128)).then_inc(s_w, 16)

            @block.scalar
            def _(act):
                with act.Fori(0, CHUNKS) as c:
                    act.wait_ge(s_turned, c * J + AHEAD)
                    act.activation(rows[:, :, :], m.y[:, bass.ds(c * J, J), :], ACT.Copy).then_inc(s_rows, 1)
                    for j in range(J):
                        act.wait_ge(s_turned, c * J + (j + 1) + AHEAD)
                        if j == 0:
                            act.wait_ge(s_prod, c * J + AHEAD)
                        act.activation(cols[:, j, :, :].rearrange("p b r -> p (b r)"), turned[:, j % 2, 0:CB * R],
                                       ACT.Copy).then_inc(s_cols, 1)

            @block.tensor
            def _(pe):
                pe.wait_ge(s_w, 16)
                with pe.Fori(0, CHUNKS) as c:
                    pe.wait_ge(s_rows, c + 1)
                    for j in range(J):
                        pe.wait_ge(s_cols, (c * J + (j - 1) if j else c * J) + AHEAD)
                        for b in range(CB):
                            ins = pe.transpose(turned[:, j % 2, b * R:(b + 1) * R], rows[:, j, b * 128:(b + 1) * 128],
                                               m.ident[0:R, 0:R])
                        ins.then_inc(s_turned, 1)
                    for j in range(J):
                        pe.wait_ge(s_cols, c * J + (j + 1) + AHEAD)
                        pe.wait_ge(s_y, (c * J + (j - 1) if j else c * J) + AHEAD)
                        for b in range(CB):
                            ins = pe.matmul(bank[:, j % 2, 0:C], cols[:, j, b, :], w[:, b, :],
                                            start=(b == 0), stop=(b == CB - 1))
                        ins.then_inc(s_prod, 1)

            @block.vector
            def _(dve):
                v = Chain(dve, s_v)
                with dve.Fori(0, CHUNKS) as c:
                    v.enter(c, 3 * J)
                    for j in range(J):
                        x, y, z = (k[:, c * J + j, :] for k in (m.x, m.y, m.z))
                        dve.wait_ge(s_prod, c * J + (j + 1) + AHEAD)
                        dve.tensor_tensor(y, bank[:, j % 2, 0:C], bp, ALU.add).then_inc(s_y, 1)
                        dve.wait_ge(s_y, c * J + (j + 1) + AHEAD)
                        v.link(dve.tensor_tensor(y, y, z, ALU.add))
                        v.link(dve.tensor_tensor(x, x, y, ALU.add))
                        v.link(dve.tensor_tensor(x, x, b2, ALU.add))
                v.leave(CHUNKS)

C3 = 3 * C
OB = C3 // 128
CAT = 2 * C3
GW = 3 * HD
GN = CAT // GW
CO = GN * HD
BALL = 0.99999
MIN_NORM = 1e-15


def ball_log_rows(nc, m):
    with phase(nc, "bl") as ph:
        square = ph.sb("square", [R, C])
        n2 = ph.sb("n2", [R, T])
        norm, inv, c_, u, w, lnw, one = (ph.sb(x, [R, T]) for x in ("norm", "inv", "c", "u", "w", "lnw", "one"))
        rows = ph.sb("rows", [R, J, C])
        turned = ph.ps("turned", [128, J, 512])
        s_sq, s_norm, s_w, s_ln, s_v = (ph.sem(x) for x in ("sq", "norm", "w", "ln", "v"))
        s_rows, s_turned, s_out, s_pace = (ph.sem(x) for x in ("rows", "turned", "out", "pace"))
        ph.ahead(s_out, s_sq, s_turned)
        with nc.Block() as block:

            @block.scalar
            def _(act):
                with act.Fori(0, T) as t:
                    act.wait_ge(s_sq, t + AHEAD)
                    act.sem_inc(s_pace, 1)
                    act.activation(square[:, :], m.z[:, t, :], ACT.Square, accum_out=n2[:, bass.ds(t, 1)])\
                        .then_inc(s_sq, 1)
                act.wait_ge(s_sq, T + AHEAD)
                act.activation(norm[:, :], n2[:, :], ACT.Sqrt).then_inc(s_norm, 1)
                act.wait_ge(s_w, 1)
                act.activation(lnw[:, :], w[:, :], ACT.Ln).then_inc(s_ln, 1)
                with act.Fori(0, CHUNKS) as c:
                    for j in range(J):
                        act.wait_ge(s_turned, c * J + (j + 1) + AHEAD)
                        act.activation(m.z_cols[:, :, bass.ds(c * COLS + j * R, R)],
                                       turned[:, j, 0:CB * R].rearrange("p (b r) -> p b r", b=CB), ACT.Copy)\
                            .then_inc(s_out, 1)

            @block.vector
            def _(dve):
                v = Chain(dve, s_v)
                dve.wait_ge(s_norm, 1)
                v.link(dve.tensor_scalar(norm[:, :], norm[:, :], MIN_NORM, None, ALU.max))
                v.link(dve.reciprocal(inv[:, :], norm[:, :]))
                v.link(dve.tensor_scalar(c_[:, :], norm[:, :], BALL, None, ALU.min))
                v.link(dve.tensor_scalar(u[:, :], c_[:, :], -1.0, 1.0, ALU.mult, ALU.add))
                v.link(dve.reciprocal(u[:, :], u[:, :]))
                v.link(dve.scalar_tensor_tensor(out=u[:, :], in0=u[:, :], scalar=2.0, in1=c_[:, :],
                                                op0=ALU.mult, op1=ALU.mult))
                v.link(dve.tensor_scalar(w[:, :], u[:, :], 1.0, None, ALU.add))
                v.done(s_w)
                v.link(dve.tensor_scalar(one[:, :], w[:, :], 1.0, None, ALU.is_equal))
                v.link(dve.scalar_tensor_tensor(out=c_[:, :], in0=w[:, :], scalar=-1.0, in1=one[:, :],
                                                op0=ALU.add, op1=ALU.add))
                v.link(dve.reciprocal(c_[:, :], c_[:, :]))
                dve.wait_ge(s_ln, 1)
                v.link(dve.tensor_tensor(lnw[:, :], lnw[:, :], one[:, :], ALU.add))
                v.link(dve.tensor_tensor(lnw[:, :], lnw[:, :], c_[:, :], ALU.mult))
                v.link(dve.tensor_tensor(lnw[:, :], lnw[:, :], u[:, :], ALU.mult))
                v.link(dve.scalar_tensor_tensor(out=inv[:, :], in0=lnw[:, :], scalar=0.5, in1=inv[:, :],
                                                op0=ALU.mult, op1=ALU.mult))
                with dve.Fori(0, CHUNKS) as c:
                    dve.wait_ge(s_turned, c * J + AHEAD)
                    for j in range(J):
                        dve.tensor_scalar(rows[:, j, :], m.z[:, c * J + j, :], inv[:, bass.ds(c * J + j, 1)], None,
                                          ALU.mult).then_inc(s_rows, 1)

            @block.tensor
            def _(pe):
                with pe.Fori(0, CHUNKS) as c:
                    pe.wait_ge(s_out, c * J + AHEAD)
                    for j in range(J):
                        pe.wait_ge(s_rows, c * J + (j + 1))
                        for b in range(CB):
                            ins = pe.transpose(turned[:, j, b * R:(b + 1) * R], rows[:, j, b * 128:(b + 1) * 128],
                                               m.ident[0:R, 0:R])
                        ins.then_inc(s_turned, 1)


def ball_mixer(nc, m, a):
    import math
    reach = math.atanh(BALL)
    with phase(nc, "bm") as ph:
        wc = ph.sb("wc", [128, CB, C3])
        fx = ph.sb("fx", [128, J, C])
        pw = fx[:, 0, 0:OB * HD].rearrange("p (o i) -> p o i", o=OB)
        diag = fx[:, 1, 0:128]
        mine = fx[:, 2, 0:128].rearrange("p (g i) -> p g i", i=HD)
        branch = ph.sb("branch", [128, OB, 128])
        wr = ph.sb("wr", [128, CO // 128, C])
        y = ph.sb("y", [128, OB, N])
        junk = ph.sb("junk", [128, C3])
        stats = junk[:, 0:OB * CHUNKS * 12].rearrange("p (o n k) -> p o n k", o=OB, k=6)
        mv = ph.sb("mv", [128, OB, 2])
        scale = ph.sb("scale", [128, OB])
        shift = ph.sb("shift", [128, OB])
        act_c = ph.sb("act_c", [128, 2, OB, R])
        cat = [m.z_cols[0:R, j // 2, (j % 2) * CAT:(j % 2 + 1) * CAT] for j in range(J - 1)]
        cat.append(wc[0:R, :, :].rearrange("p b n -> p (b n)"))
        cat = [k.rearrange("p (w c) -> p w c", w=2) for k in cat]
        s2 = ph.sb("s2", [R, 4, J])
        nr = ph.sb("nr", [R, 9, J])
        qk = ph.sb("qk", [R, GN, 2 * HD])
        val = ph.sb("val", [R, 2, GN, HD])
        ratio = ph.sb("ratio", [R, GN, HD])
        ksum = ph.sb("ksum", [R, GN])
        o_cols = ph.sb("o_cols", [128, CO // 128, R])
        up = ph.ps("up", [128, 6, 512])
        obank = ph.ps("obank", [128, 512])
        fbank = ph.ps("fbank", [R, 512])
        s_w, s_mask, s_diag, s_turn, s_both = (ph.sem(x) for x in ("w", "mask", "diag", "turn", "both"))
        s_up, s_y, s_stats, s_sd, s_bn, s_v, s_pace = (ph.sem(x) for x in ("up", "y", "stats", "sd", "bn", "v", "pace"))
        s_act, s_cat, s_catr, s_catsq, s_used, s_sum, s_norm = (
            ph.sem(x) for x in ("act", "cat", "catr", "catsq", "used", "sum", "norm"))
        s_o, s_ot, s_oc, s_osq, s_f, s_raw, s_norm2 = (ph.sem(x) for x in ("o", "ot", "oc", "osq", "f", "raw", "norm2"))
        s_fx, s_fxsq, s_tanh, s_done, s_a, s_sq4 = (ph.sem(x) for x in ("fx", "fxsq", "tanh", "done", "a", "sq4"))
        units = OB * len(HALVES)
        col = m.col
        ph.ahead(s_cat, s_catr, s_oc, s_ot, s_raw, s_y, s_done, s_norm2)
        with nc.Block() as block:

            @block.gpsimd
            def _(pool):
                pool.memset(mine[:, :, :], 1.0).then_inc(s_mask, 1)
                pool.wait_ge(s_mask, 1)
                pool.affine_select(out=mine[:, :, :], in_=mine[:, :, :], compare_op=ALU.is_ge, fill=0.0, base=0,
                                   pattern=[[-HD, 4], [0, HD]], channel_multiplier=1).then_inc(s_mask, 1)
                pool.wait_ge(s_mask, 2)
                pool.affine_select(out=mine[:, :, :], in_=mine[:, :, :], compare_op=ALU.is_ge, fill=0.0,
                                   base=HD - 1, pattern=[[HD, 4], [0, HD]], channel_multiplier=-1).then_inc(s_mask, 1)

            @block.sync
            def _(sp):
                sp.dma_start(pw[:, :, :], a["L1_mix_w_pw"].rearrange("(b p) i k -> p b (i k)", p=128)).then_inc(s_w, 16)
                sp.dma_start(wc[:, :, :], m.turned["conv"].rearrange("(b p) n -> p b n", p=128)).then_inc(s_w, 16)
                sp.dma_start(wr[:, :, :], m.turned["res"].rearrange("(b p) n -> p b n", p=128)).then_inc(s_w, 16)

            @block.tensor
            def _(pe):
                for o in range(OB):
                    pe.wait_ge(s_diag, o + 1)
                    pe.transpose(obank[:, 0:128], diag[:, :], m.ident[:, :]).then_inc(s_turn, 1)
                pe.wait_ge(s_both, OB)
                pe.wait_ge(s_w, 48)
                pe.sem_inc(s_pace, 1)
                with pe.Fori(0, CHUNKS) as c:
                    for u in range(units):
                        o, (at, n) = u // 2, HALVES[u % 2]
                        pe.wait_ge(s_y, (c * units + (u - 3) if u > 3 else c * units) + AHEAD)
                        for b in range(CB):
                            ins = pe.matmul(up[:, u % 4, 0:n], wc[:, b, o * 128:(o + 1) * 128],
                                            m.z_cols[:, b, bass.ds(c * COLS + at, n)],
                                            start=(b == 0), stop=(b == CB - 1))
                        ins.then_inc(s_up, 1)

                def join(t, j):
                    pe.wait_ge(s_act, t + 1)
                    pe.wait_ge(s_catr, t - min(j, 1) + AHEAD)
                    for o in range(OB):
                        bank, at = j % 2 * 3 + o // 2, (o % 2) * 256
                        pe.transpose(up[0:R, bank, at:at + 128], act_c[:, j % 2, o, :], m.ident[:, :])
                        ins = pe.matmul(up[0:R, bank, at + 128:at + 256], act_c[:, j % 2, o, :], branch[:, o, :],
                                        start=True, stop=True)
                    ins.then_inc(s_cat, 1)

                def chunk(c, more):
                    for j in range(J):
                        t = c * J + j
                        pe.wait_ge(s_o, t + 1)
                        pe.wait_ge(s_oc, t + AHEAD)
                        rows = val[:, j % 2, :, :].rearrange("p g d -> p (g d)")
                        for b in range(CO // 128):
                            ins = pe.transpose(obank[:, b * R:(b + 1) * R], rows[:, b * 128:(b + 1) * 128],
                                               m.ident[0:R, 0:R])
                        ins.then_inc(s_ot, 1)
                        if more:
                            join((c + 1) * J + j, j)
                        pe.wait_ge(s_oc, t + 1 + AHEAD)
                        pe.wait_ge(s_raw, t + AHEAD)
                        for b in range(CO // 128):
                            ins = pe.matmul(fbank[:, 0:C], o_cols[:, b, :], wr[:, b, :],
                                            start=(b == 0), stop=(b == CO // 128 - 1))
                        ins.then_inc(s_f, 1)

                for j in range(J):
                    join(j, j)
                with pe.Fori(0, CHUNKS - 1) as c:
                    chunk(c, True)
                chunk(CHUNKS - 1, False)

            @block.scalar
            def _(act):
                with act.Fori(0, CHUNKS) as c:
                    for u in range(units):
                        o, (at, n) = u // 2, HALVES[u % 2]
                        act.wait_ge(s_up, c * units + (u + 1))
                        act.activation(y[:, o, bass.ds(c * COLS + at, n)], up[:, u % 4, 0:n], ACT.Copy)\
                            .then_inc(s_y, 1)
                act.wait_ge(s_stats, 1)
                act.activation(scale[:, :], mv[:, :, 1], ACT.Sqrt, bias=m.eps[:, :]).then_inc(s_sd, 1)
                act.wait_ge(s_bn, 1)
                a_ = Chain(act, s_a)

                def relu(t, j):
                    act.wait_ge(s_cat, t - min(j, 1) + AHEAD)
                    act.sem_inc(s_pace, 1)
                    for o in range(OB):
                        ins = act.activation(act_c[:, j % 2, o, :], y[:, o, bass.ds(t * R, R)], ACT.Relu,
                                             bias=shift[:, o:o + 1], scale=scale[:, o:o + 1])
                    ins.then_inc(s_act, 1)

                def read(t, j):
                    act.wait_ge(s_cat, t + 1 + AHEAD)
                    bank = up[0:R, j % 2 * 3:j % 2 * 3 + 3, :].rearrange("p a (b w c) -> p (a b) w c", b=2, w=2)
                    act.activation(cat[j].rearrange("p w (o c) -> p o w c", o=OB), bank, ACT.Copy)\
                        .then_inc(s_catr, 1)
                    act.wait_ge(s_catr, t + 1 + AHEAD)
                    for k in range(2):
                        a_.link(act.activation(junk[0:R, :], cat[j][:, k, :], ACT.Square, accum_out=s2[:, k, j:j + 1]))
                    act.sem_inc(s_catsq, 1)

                def chunk(c, more):
                    act.wait_ge(s_sum, c + 1)
                    act.activation(nr[:, 0:2, :], s2[:, 0:2, :], ACT.Sqrt).then_inc(s_norm, 1)
                    if more:
                        relu((c + 1) * J, 0)
                    for j in range(J):
                        t = c * J + j
                        act.wait_ge(s_ot, t + 1 + AHEAD)
                        if j:
                            act.wait_ge(s_f, t)
                        act.activation(o_cols[:, :, :].rearrange("p b r -> p (b r)"), obank[:, 0:CO // 128 * R],
                                       ACT.Copy).then_inc(s_oc, 1)
                        if more and j < J - 1:
                            relu((c + 1) * J + j + 1, j + 1)
                        a_.link(act.activation(junk[0:R, 0:CO], val[:, j % 2, :, :].rearrange("p g d -> p (g d)"),
                                               ACT.Square, accum_out=s2[:, 2, j:j + 1]))
                        act.sem_inc(s_osq, 1)
                        if more:
                            act.wait_ge(s_used, t + 1)
                            read((c + 1) * J + j, j)
                        act.wait_ge(s_f, t + 1)
                        if j == 0:
                            act.wait_ge(s_done, c + AHEAD)
                        act.activation(fx[0:R, j, :], fbank[:, 0:C], ACT.Copy).then_inc(s_raw, 1)
                    act.wait_ge(s_osq, (c + 1) * J)
                    act.activation(nr[:, 2, :], s2[:, 2, :], ACT.Sqrt).then_inc(s_norm2, 1)
                    for j in range(J):
                        act.wait_ge(s_fx, c * J + (j + 1))
                        a_.link(act.activation(junk[0:R, 0:C], fx[0:R, j, :], ACT.Square, accum_out=s2[:, 3, j:j + 1]))
                    a_.link(act.activation(nr[:, 3, :], s2[:, 3, :], ACT.Sqrt))
                    act.activation(nr[:, 4, :], nr[:, 3, :], ACT.Tanh).then_inc(s_tanh, 1)

                relu(0, 0)
                for j in range(J):
                    if j < J - 1:
                        relu(j + 1, j + 1)
                    read(j, j)
                with act.Fori(0, CHUNKS - 1) as c:
                    a_.enter(c, 4 * J + 1)
                    chunk(c, True)
                a_.leave(CHUNKS - 1)
                chunk(CHUNKS - 1, False)

            @block.vector
            def _(dve):
                v = Chain(dve, s_v)
                dve.wait_ge(s_w, 48)
                dve.wait_ge(s_mask, 3)
                for o in range(OB):
                    if o:
                        dve.wait_ge(s_turn, o)
                    dve.tensor_tensor(diag[:, :].rearrange("p (g i) -> p g i", i=HD), repeat_mid(pw[:, o, :], 4),
                                      mine[:, :, :], ALU.mult).then_inc(s_diag, 1)
                    dve.wait_ge(s_turn, o + 1)
                    dve.tensor_scalar(branch[:, o, :], obank[:, 0:128], col["L1_mix_w_dw"][:, o:o + 1], None,
                                      ALU.mult).then_inc(s_both, 1)
                with dve.Fori(0, CHUNKS) as c:
                    for u in range(units):
                        o, (at, n) = u // 2, HALVES[u % 2]
                        dve.wait_ge(s_y, c * units + (u + 1) + AHEAD)
                        ins = dve.bn_stats(stats[:, o, c * 2 + u % 2, :], y[:, o, bass.ds(c * COLS + at, n)])
                        ins.then_inc(s_sq4, 1)
                dve.wait_ge(s_sq4, CHUNKS * units)
                for o in range(OB):
                    ins = dve.bn_aggr(mv[:, o, :], stats[:, o, :, :].rearrange("p n k -> p (n k)"))
                v.link(ins)
                v.done(s_stats)
                dve.wait_ge(s_sd, 1)
                v.link(dve.reciprocal(scale[:, :], scale[:, :]))
                v.link(dve.tensor_tensor(scale[:, :], scale[:, :], col["L1_mix_bn_gamma"], ALU.mult))
                v.link(dve.tensor_tensor(shift[:, :], mv[:, :, 0], scale[:, :], ALU.mult))
                v.link(dve.tensor_tensor(shift[:, :], col["L1_mix_bn_beta"], shift[:, :], ALU.subtract))
                v.done(s_bn)

                def radial(n, k):
                    v.link(dve.tensor_scalar(nr[:, n, :], nr[:, n, :], MIN_NORM, None, ALU.max))
                    v.link(dve.reciprocal(nr[:, k, :], nr[:, n, :]))
                    v.link(dve.scalar_tensor_tensor(out=nr[:, k, :], in0=nr[:, n, :], scalar=reach,
                                                    in1=nr[:, k, :], op0=ALU.min, op1=ALU.mult))

                with dve.Fori(0, CHUNKS) as c:
                    v.enter(c, 9 + 5 * J + 6)
                    dve.wait_ge(s_catsq, (c + 1) * J)
                    v.link(dve.tensor_tensor(s2[:, 1, :], s2[:, 0, :], s2[:, 1, :], ALU.add))
                    v.done(s_sum)
                    dve.wait_ge(s_norm, c + 1)
                    radial(0, 5)
                    v.link(dve.tensor_tensor(nr[:, 1, :], nr[:, 1, :], nr[:, 5, :], ALU.mult))
                    radial(1, 6)
                    v.link(dve.tensor_tensor(nr[:, 6, :], nr[:, 6, :], nr[:, 5, :], ALU.mult))
                    for j in range(J):
                        t = c * J + j
                        groups = cat[j].rearrange("p a c -> p (a c)").rearrange("p (g w) -> p g w", w=GW)
                        gamma = nr[:, 6, j:j + 1]
                        out = val[:, j % 2, :, :]
                        dve.wait_ge(s_ot, t - min(j, 1) + AHEAD)
                        if j > 1:
                            dve.wait_ge(s_osq, t - 1)
                        elif j == 0:
                            dve.wait_ge(s_norm2, c + AHEAD)
                        dve.tensor_scalar(out, groups[:, :, 2 * HD:GW], gamma, None, ALU.mult)
                        v.link(dve.tensor_scalar(qk[:, :, :], groups[:, :, 0:2 * HD], gamma, 0.0, ALU.mult, ALU.max))
                        v.done(s_used)
                        v.link(dve.tensor_scalar(ratio[:, :, :], out, 1e-15, None, ALU.add))
                        dve.reciprocal(ratio[:, :, :], ratio[:, :, :])
                        dve.tensor_reduce(ksum[:, :], qk[:, :, HD:2 * HD], AX_X, ALU.add)
                        v.link(dve.tensor_tensor(out, out, qk[:, :, 0:HD], ALU.mult))
                        v.link(dve.tensor_tensor(ratio[:, :, :], ratio[:, :, :], out, ALU.mult))
                        v.link(dve.tensor_tensor(out, ratio[:, :, :], repeat_last(ksum[:, :], HD), ALU.mult))
                        v.done(s_o)
                    dve.wait_ge(s_norm2, c + 1 + AHEAD)
                    radial(2, 7)
                    for j in range(J):
                        dve.wait_ge(s_raw, c * J + (j + 1) + AHEAD)
                        dve.scalar_tensor_tensor(out=fx[0:R, j, :], in0=fx[0:R, j, :], scalar=nr[:, 7, j:j + 1],
                                                 in1=m.row["L1_mix_b_res"], op0=ALU.mult, op1=ALU.add)\
                            .then_inc(s_fx, 1)
                    dve.wait_ge(s_tanh, c + 1)
                    v.link(dve.tensor_scalar(nr[:, 3, :], nr[:, 3, :], MIN_NORM, None, ALU.max))
                    v.link(dve.reciprocal(nr[:, 3, :], nr[:, 3, :]))
                    v.link(dve.scalar_tensor_tensor(out=nr[:, 8, :], in0=nr[:, 4, :], scalar=BALL, in1=nr[:, 3, :],
                                                    op0=ALU.min, op1=ALU.mult))
                    for j in range(J):
                        t = c * J + j
                        ins = dve.scalar_tensor_tensor(out=m.x[:, t, :], in0=fx[0:R, j, :], scalar=nr[:, 8, j:j + 1],
                                                       in1=m.x[:, t, :], op0=ALU.mult, op1=ALU.add)
                    ins.then_inc(s_done, 1)
                v.leave(CHUNKS)


class Memory:
    pass


def graph_layers(nc, a, out):
    m = Memory()
    with ExitStack() as stack:
        def sb(name, shape, dt=F32):
            return stack.enter_context(nc.sbuf_tensor(name, shape, dt))

        m.ident = sb("ident", [128, 128])
        m.ones = sb("ones", [128, 128])
        m.eps = sb("eps", [128, 1])
        m.before = sb("before", [G, G])
        m.row_no = sb("row_no", [128, R])
        m.tile_starts = sb("tile_starts", [G, T - 1])
        m.edge_dst = sb("edge_dst", [R, G, J])
        m.edge_dsti = sb("edge_dsti", [R, G + SLOTS, J], I32)
        m.edge_src = sb("edge_src", [R, G + SLOTS, J], I32)
        m.group_table = sb("group_table", [1, 3 * G], I32)
        m.degree = sb("degree", [R, T])
        m.degree_s = sb("degree_s", [R, 2, T])
        m.inv_sqrt_degree = sb("inv_sqrt_degree", [R, T])
        m.x = sb("x_rows", [R, T, C])
        m.colvec = sb("colvec", [128, 384])
        m.rowvec = sb("rowvec", [R, 10, C])
        m.gate = sb("gate", [R, T, X8])
        m.z = sb("z_rows", [R, T, C])
        m.ident16 = sb("ident16", [128, 128], F16)
        z_flat = sb("z_flat", [128, CB * N])
        m.z_cols = z_flat[:, :].rearrange("p (b n) -> p b n", b=CB)
        m.zc = z_flat[:, :].bitcast(F16).rearrange("p (k b n) -> p k b n", k=2, b=CB)
        m.gather_q = nc.dram_tensor("gather_q", [N, C], F32).ap()
        m.gather_kv = nc.dram_tensor("gather_kv", [N, 2 * C], F32).ap()
        m.gather0 = nc.dram_tensor("gather0", [N, 2 * C], F16).ap()
        y_stack = ExitStack()

        def take_y(turn):
            m.y = y_stack.enter_context(nc.sbuf_tensor(f"y_rows{turn}", [R, T, C], F32))

        def free_y():
            y_stack.close()

        take_y(0)
        with nc.semaphore("x_in") as s_x, nc.Block() as block:

            @block.sync
            def _(sp):
                sp.dma_start(m.x[:, :, :], a["x"].rearrange("(t p) n -> p t n", p=R)).then_inc(s_x, 16)
                sp.wait_ge(s_x, 16)

            @block.gpsimd
            def _(pool):
                pool.memset(m.edge_src[:, :, :], 0)
                pool.memset(m.edge_dsti[:, :, :], 0)

        constants(nc, m)
        edge_tables(nc, m, a["src"], a["dst"])
        layernorm(nc, m, "ln0", m.x, m.z)
        scaled_rows(nc, m, a["L0_gnn_W"])
        load_vectors(nc, m, a)
        message_sum(nc, m)
        col = m.col
        layernorm_cols(nc, m, "ln1", m.z, None, [(m.z_cols, col["L0_mix_ln1_g"], col["L0_mix_ln1_b"])])
        mixer0(nc, m, a)
        layernorm(nc, m, "ln2", m.y)
        feed_forward(nc, m, "ff0", 1, lambda e: a["L0_mix_W1"], col["L0_mix_b1"], lambda e: a["L0_mix_W2"],
                     gain=col["L0_mix_ln2_g"], bias_in=col["L0_mix_ln2_b"])
        layernorm(nc, m, "ln3", m.x)
        router(nc, m, "ro0", a["L0_ffn_Wr"], m.row["L0_ffn_br"], False, a["L0_ffn_bo"])
        experts0(nc, m, a)
        layernorm_cols(nc, m, "ln4", m.x, m.z, [(m.z_cols, None, None)])
        turned_weights(nc, m, a)
        query_rows(nc, m, a)
        ball_log_rows(nc, m)
        free_y()
        ball_mixer(nc, m, a)
        take_y(1)
        attention_sum(nc, m)
        attention_out(nc, m)
        layernorm(nc, m, "ln5", m.y)
        feed_forward(nc, m, "ff1", 1, lambda e: m.turned["w1"], col["L1_gnn_b1"], lambda e: m.turned["w2"],
                     gain=col["L1_gnn_ln_g"], bias_in=col["L1_gnn_ln_b"])
        free_y()
        layernorm(nc, m, "ln6", m.x)
        router(nc, m, "ro1", a["L1_ffn_Wr"], None, True, a["L1_ffn_b2p"], m.row["L1_ffn_b2s"])
        feed_forward(nc, m, "ff2", 1, lambda e: a["L1_ffn_W1s"], col["L1_ffn_b1s"], lambda e: a["L1_ffn_W2s"])
        expert = lambda W: lambda e: W[bass.ds(e, 1), :, :].rearrange("e k n -> (e k) n")
        feed_forward(nc, m, "ff3", X8, expert(a["L1_ffn_W1p"]), col["L1_ffn_b1p"], expert(a["L1_ffn_W2p"]), m.gate)
        with nc.semaphore("out") as s_out, nc.Block() as block:

            @block.sync
            def _(sp):
                sp.dma_start(out.rearrange("(t p) n -> p t n", p=R), m.x[:, :, :]).then_inc(s_out, 16)
                sp.wait_ge(s_out, 16)


def kernel(**inputs):
    import numpy as np
    from concourse import bacc
    from concourse.bass_utils import run_bass_kernel_spmd

    nc = bacc.Bacc("TRN2", target_bir_lowering=False, num_devices=1)
    arrays, a = {}, {}
    for name, given in inputs.items():
        array = np.ascontiguousarray(given)
        arrays[f"in_{name}"] = array
        a[name] = nc.dram_tensor(f"in_{name}", array.shape, mybir.dt.from_np(array.dtype),
                                          kind="ExternalInput").ap()
    out = nc.dram_tensor("out", (N, C), F32, kind="ExternalOutput").ap()
    graph_layers(nc, a, out)
    return run_bass_kernel_spmd(nc, [arrays], core_ids=[0]).results[0]["out"]
```

```python
from contextlib import ExitStack, contextmanager

import concourse.bass as bass
from concourse import mybir

F32 = mybir.dt.float32
F16 = mybir.dt.float16
BF16 = mybir.dt.bfloat16
I32 = mybir.dt.int32
I16 = mybir.dt.int16
ALU = mybir.AluOpType
ACT = mybir.ActivationFunctionType
AX_X = mybir.AxisListType.X

N = 3125
C = 256
CB = C // 128
R = 125
T = N // R
J = 5
CHUNKS = T // J
COLS = J * R
HALVES = ((0, 313), (313, 312))
E = 50000
G = E // (J * R)
GP = G + 3
ET = E // R
SLOTS = 4
F = 4 * C
FB = F // 128
X8 = 8
HD = C // X8
KR = 4
EPS = 1e-5
WS = 64.0
LAG = 2
RING = 4
AHEAD = 1
RNE = 12582912.0


class Chain:

    def __init__(self, eng, sem):
        self.eng, self.sem, self.base, self.n = eng, sem, 0, 0

    def link(self, ins):
        self.n += 1
        ins.then_inc(self.sem, 1)
        self.eng.wait_ge(self.sem, self.base + self.n)

    def done(self, sem):
        self.eng.sem_inc(sem, 1)

    def enter(self, i, steps):
        self.start, self.steps = self.n, steps
        self.base = i * steps

    def leave(self, trips):
        assert self.n - self.start == self.steps, self.n - self.start
        self.base = 0
        self.n = self.start + self.steps * trips


class Phase:

    def __init__(self, nc, name, stack):
        self.nc, self.name, self.stack, self.sems = nc, name, stack, []

    def sb(self, name, shape, dt=F32):
        return self.stack.enter_context(self.nc.sbuf_tensor(f"{self.name}_{name}", shape, dt))

    def ps(self, name, shape, dt=F32):
        return self.stack.enter_context(self.nc.psum_tensor(f"{self.name}_{name}", shape, dt))

    def sem(self, name):
        self.sems.append(self.nc.alloc_semaphore(f"{self.name}_{name}"))
        return self.sems[-1]

    def ahead(self, *sems):
        for sem in dict.fromkeys(sems):
            self.nc.gpsimd.sem_inc(sem, AHEAD * sems.count(sem))


@contextmanager
def phase(nc, name):
    with ExitStack() as stack:
        ph = Phase(nc, name, stack)
        yield ph
        nc.clear_and_free_semaphores(ph.sems)
        nc.all_engine_barrier()


def repeat_last(ap, n):
    return ap.unsqueeze(len(ap.shape)).broadcast_to([*ap.shape, n])


def repeat_mid(ap, n):
    return ap.unsqueeze(1).broadcast_to([ap.shape[0], n, *ap.shape[1:]])


def constants(nc, m):
    with phase(nc, "cst") as ph:
        s_set, s_fill = ph.sem("set"), ph.sem("fill")
        with nc.Block() as block:

            @block.gpsimd
            def _(pool):
                pool.memset(m.ident[:, :], 0.0).then_inc(s_fill, 1)
                pool.memset(m.ones[:, :], 1.0).then_inc(s_set, 1)
                pool.memset(m.eps[:, :], EPS).then_inc(s_set, 1)
                pool.memset(m.ident16[:, :], 0.0).then_inc(s_fill, 1)
                pool.memset(m.before[:, :], 1.0).then_inc(s_fill, 1)
                pool.iota(m.row_no[:, :], pattern=[[1, R]], base=0, channel_multiplier=0,
                          allow_small_or_imprecise_dtypes=True).then_inc(s_set, 1)
                pool.iota(m.tile_starts[:, :], pattern=[[R, T - 1]], base=R, channel_multiplier=0,
                          allow_small_or_imprecise_dtypes=True).then_inc(s_set, 1)
                pool.wait_ge(s_fill, 3)
                pool.affine_select(out=m.ident[:, :], in_=m.ident[:, :], compare_op=ALU.not_equal, fill=1.0,
                                   base=0, pattern=[[-1, 128]], channel_multiplier=1).then_inc(s_set, 1)
                pool.affine_select(out=m.ident16[:, :], in_=m.ident16[:, :], compare_op=ALU.not_equal, fill=1.0,
                                   base=0, pattern=[[-1, 128]], channel_multiplier=1).then_inc(s_set, 1)
                pool.affine_select(out=m.before[:, :], in_=m.before[:, :], compare_op=ALU.is_gt, fill=0.0,
                                   base=0, pattern=[[1, G + 1]], channel_multiplier=-1).then_inc(s_set, 1)
                pool.wait_ge(s_set, 7)


def edge_tables(nc, m, src, dst):
    with phase(nc, "edg") as ph:
        raw = ph.sb("raw", [G, 2, J * R], I32)
        rawf = ph.sb("rawf", [G, 2, J * R])
        ends = ph.sb("ends", [G, 2])
        below = ph.sb("below", [G, 2, T - 1])
        span = ph.sb("span", [G, 2])
        last = ph.sb("last", [G, 2])
        packed = ph.sb("packed", [1, GP])
        tileno = ph.sb("tileno", [R, ET])
        rowno = ph.sb("rowno", [R, ET])
        tileb = ph.sb("tileb", [R, ET], BF16)
        rowb = ph.sb("rowb", [R, ET], BF16)
        nob = ph.sb("nob", [R, R], BF16)
        SET = 20
        hot_row = ph.sb("hot_row", [R, 2, SET, R], BF16)
        hot_tile = ph.sb("hot_tile", [R, 2, SET, T], BF16)
        turned = ph.ps("turned", [R, 2, 512])
        rows = ph.ps("rows", [1, 512])
        count = ph.ps("count", [R, 512])
        s_in, s_f, s_turned, s_span, s_rows = (ph.sem(x) for x in ("in", "f", "turned", "span", "rows"))
        s_hot, s_count, s_v = ph.sem("hot"), ph.sem("count"), ph.sem("v")
        with nc.Block() as block:

            @block.sync
            def _(sp):
                sp.dma_start(raw[:, 0, :], dst.rearrange("(g e) -> g e", g=G)).then_inc(s_in, 16)
                sp.dma_start(raw[:, 1, :], src.rearrange("(g e) -> g e", g=G)).then_inc(s_in, 16)

            @block.vector
            def _(dve):
                v = Chain(dve, s_v)
                dve.wait_ge(s_in, 32)
                dve.tensor_copy(rawf[:, :, :], raw[:, :, :]).then_inc(s_f, 1)
                dve.wait_ge(s_f, 1)
                dve.tensor_reduce(ends[:, 0:1], rawf[:, 0, :], AX_X, ALU.min)
                v.link(dve.tensor_reduce(ends[:, 1:2], rawf[:, 0, :], AX_X, ALU.max))
                for k in range(2):
                    last_ins = dve.tensor_scalar(below[:, k, :], m.tile_starts[:, :], ends[:, k:k + 1], None, ALU.is_le)
                v.link(last_ins)
                v.link(dve.tensor_reduce(last[:, :], below[:, :, :], AX_X, ALU.add))
                dve.tensor_copy(span[:, 0:1], last[:, 0:1])
                v.link(dve.tensor_tensor(span[:, 1:2], last[:, 1:2], last[:, 0:1], ALU.subtract))
                dve.tensor_scalar(span[:, 1:2], span[:, 1:2], 1.0, None, ALU.add).then_inc(s_span, 1)
                dve.wait_ge(s_turned, 1)
                dve.tensor_copy(m.edge_dst[:, :, :],
                                turned[:, 0, 0:J * G].rearrange("p (j g) -> p g j", j=J))
                v.link(dve.tensor_copy(m.edge_src[:, 0:G, :],
                                       turned[:, 1, 0:J * G].rearrange("p (j g) -> p g j", j=J)))
                dve.wait_ge(s_rows, 1)
                dve.memset(packed[:, G:GP], 32.0)
                v.link(dve.tensor_copy(packed[:, 0:G], rows[:, 0:G]))
                v.link(dve.scalar_tensor_tensor(out=packed[:, 0:G], in0=rows[:, G:2 * G], scalar=32.0,
                                                in1=packed[:, 0:G], op0=ALU.mult, op1=ALU.add))
                v.link(dve.scalar_tensor_tensor(out=packed[:, 0:G + 1], in0=rows[:, 2 * G:3 * G + 1], scalar=1024.0,
                                                in1=packed[:, 0:G + 1], op0=ALU.mult, op1=ALU.add))
                for g in range(G + 1, GP):
                    v.link(dve.tensor_scalar(packed[:, g:g + 1], packed[:, g - 1:g], 1024.0, None, ALU.add))
                v.link(dve.tensor_copy(m.group_table[:, :], packed[:, :]))
                flat = m.edge_dst[:, :, :].rearrange("p g j -> p (g j)")
                v.link(dve.tensor_scalar(tileno[:, :], flat, 1.0 / R, 0.5 / R - 0.5, ALU.mult, ALU.add))
                v.link(dve.tensor_scalar(tileno[:, :], tileno[:, :], RNE, RNE, ALU.add, ALU.subtract))
                v.link(dve.scalar_tensor_tensor(out=rowno[:, :], in0=tileno[:, :], scalar=-float(R), in1=flat,
                                                op0=ALU.mult, op1=ALU.add))
                dve.tensor_copy(tileb[:, :], tileno[:, :])
                dve.tensor_copy(rowb[:, :], rowno[:, :])
                v.link(dve.tensor_copy(nob[:, :], m.row_no[0:R, :]))
                def one_hots(at, s):
                    dve.tensor_tensor(hot_row[:, s, :, :], repeat_mid(nob[:, :], SET),
                                      repeat_last(rowb[:, bass.ds(at, SET)], R), ALU.is_equal)
                    dve.tensor_tensor(hot_tile[:, s, :, :], repeat_mid(nob[:, 0:T], SET),
                                      repeat_last(tileb[:, bass.ds(at, SET)], T), ALU.is_equal).then_inc(s_hot, 1)

                for s in range(2):
                    one_hots(s * SET, s)
                with dve.Fori(1, ET // SET // 2) as i:
                    for s in range(2):
                        dve.wait_ge(s_count, i * 2 + (s - 1))
                        one_hots(i * (2 * SET) + s * SET, s)
                dve.wait_ge(s_count, ET // SET)
                v.link(dve.tensor_copy(m.degree[:, :], count[:, 0:T]))
                v.link(dve.tensor_scalar(m.degree_s[:, 0, :], m.degree[:, :], 1.0, None, ALU.max))
                dve.tensor_scalar(m.degree_s[:, 1, :], m.degree[:, :], 1.0, None, ALU.min).then_inc(s_span, 1)
                dve.wait_ge(s_rows, 2)
                v.link(dve.reciprocal(m.degree_s[:, 0, :], m.degree_s[:, 0, :]))
                v.link(dve.tensor_tensor(m.inv_sqrt_degree[:, :], m.degree_s[:, 0, :], m.degree_s[:, 1, :], ALU.mult))

            @block.scalar
            def _(act):
                act.wait_ge(s_span, 2)
                act.activation(m.degree_s[:, 0, :], m.degree_s[:, 0, :], ACT.Sqrt).then_inc(s_rows, 1)

            @block.tensor
            def _(pe):
                pe.wait_ge(s_f, 1)
                for k in range(2):
                    for j in range(J):
                        last_ins = pe.transpose(turned[:, k, j * G:(j + 1) * G], rawf[:, k, j * R:(j + 1) * R],
                                                m.ident[0:G, 0:G])
                last_ins.then_inc(s_turned, 1)
                pe.wait_ge(s_span, 1)
                pe.matmul(rows[:, 0:G], span[:, 0:1], m.ident[0:G, 0:G], start=True, stop=True)
                pe.matmul(rows[:, G:2 * G], span[:, 1:2], m.ident[0:G, 0:G], start=True, stop=True)
                pe.matmul(rows[:, 2 * G:3 * G + 1], span[:, 1:2], m.before[:, 0:G + 1], start=True, stop=True)\
                    .then_inc(s_rows, 1)

                def add(s, first, last_step):
                    for k in range(SET):
                        ins = pe.matmul(count[:, 0:T], hot_row[:, s, k, :], hot_tile[:, s, k, :],
                                        start=(first and k == 0), stop=(last_step and k == SET - 1))
                    ins.then_inc(s_count, 1)

                pe.wait_ge(s_hot, 1)
                add(0, True, False)
                pe.wait_ge(s_hot, 2)
                add(1, False, False)
                with pe.Fori(1, ET // SET // 2 - 1) as i:
                    for s in range(2):
                        pe.wait_ge(s_hot, i * 2 + (s + 1))
                        add(s, False, False)
                for s in range(2):
                    pe.wait_ge(s_hot, ET // SET - 1 + s)
                    add(s, False, s == 1)


def join_stats(v, stats, mv):
    dve = v.eng
    a_mean, b_mean = stats[:, :, 1], stats[:, :, 4]
    v.link(dve.tensor_tensor(mv[:, 0, :], a_mean, b_mean, ALU.subtract))
    v.link(dve.scalar_tensor_tensor(out=mv[:, 1, :], in0=mv[:, 0, :], scalar=C / 4.0, in1=mv[:, 0, :],
                                    op0=ALU.mult, op1=ALU.mult))
    v.link(dve.tensor_tensor(mv[:, 1, :], mv[:, 1, :], stats[:, :, 2], ALU.add))
    v.link(dve.tensor_tensor(mv[:, 1, :], mv[:, 1, :], stats[:, :, 5], ALU.add))
    v.link(dve.tensor_tensor(mv[:, 0, :], a_mean, b_mean, ALU.add))
    v.link(dve.tensor_scalar(mv[:, 0, :], mv[:, 0, :], 0.5, None, ALU.mult))
    v.link(dve.tensor_scalar(mv[:, 1, :], mv[:, 1, :], 1.0 / C, None, ALU.mult))


def layernorm(nc, m, name, source, rows_out=None):
    with phase(nc, name) as ph:
        stats = ph.sb("stats", [R, T, 6])
        mv = ph.sb("mv", [R, 2, T])
        sd = ph.sb("sd", [R, T])
        z32 = ph.sb("z32", [R, J, C])
        z16 = ph.sb("z16", [R, J, 2, C], F16)
        turned = ph.ps("turned", [128, J, 2, 2 * CB, 128], F16)
        s_stats, s_mv, s_sd, s_v = (ph.sem(x) for x in ("stats", "mv", "sd", "v"))
        s_z32, s_high, s_low, s_turned, s_out, s_pace = (
            ph.sem(x) for x in ("z32", "high", "low", "turned", "out", "pace"))
        ph.ahead(s_turned, s_out, s_low)

        def normed(c, j):
            return z32[:, j, :] if rows_out is None else rows_out[:, c * J + j, :]

        with nc.Block() as block:

            @block.vector
            def _(dve):
                v = Chain(dve, s_v)
                with dve.Fori(0, CHUNKS) as c:
                    for j in range(J):
                        ins = dve.bn_stats(stats[:, c * J + j, :], source[:, c * J + j, :])
                    ins.then_inc(s_stats, 1)
                dve.wait_ge(s_stats, CHUNKS)
                join_stats(v, stats, mv)
                v.done(s_mv)
                dve.wait_ge(s_sd, 1)
                v.link(dve.reciprocal(sd[:, :], sd[:, :]))
                with dve.Fori(0, CHUNKS) as c:
                    dve.wait_ge(s_low, c * J + AHEAD)
                    for j in range(J):
                        dve.tensor_scalar(normed(c, j), source[:, c * J + j, :], mv[:, 0, bass.ds(c * J + j, 1)],
                                          sd[:, bass.ds(c * J + j, 1)], ALU.subtract, ALU.mult).then_inc(s_z32, 1)
                    for j in range(J):
                        dve.wait_ge(s_high, c * J + (j + 1))
                        dve.tensor_tensor(z16[:, j, 1, :], normed(c, j), z16[:, j, 0, :], ALU.subtract)\
                            .then_inc(s_low, 1)

            @block.scalar
            def _(act):
                act.wait_ge(s_mv, 1)
                act.activation(sd[:, :], mv[:, 1, :], ACT.Sqrt, bias=m.eps[0:R, :]).then_inc(s_sd, 1)
                with act.Fori(0, CHUNKS) as c:
                    act.wait_ge(s_turned, c * J + AHEAD)
                    for j in range(J):
                        act.wait_ge(s_z32, c * J + (j + 1))
                        act.sem_inc(s_pace, 1)
                        act.activation(z16[:, j, 0, :], normed(c, j), ACT.Copy).then_inc(s_high, 1)
                    for j in range(J):
                        act.wait_ge(s_turned, c * J + (j + 1) + AHEAD)
                        act.activation(m.zc[:, :, :, bass.ds(c * COLS + j * R, R)].rearrange("p k b r -> p (k b) r"),
                                       turned[:, j, 0, :, 0:R], ACT.Copy).then_inc(s_out, 1)

            @block.tensor
            def _(pe):
                with pe.Fori(0, CHUNKS) as c:
                    pe.wait_ge(s_out, c * J + AHEAD)
                    for j in range(J):
                        pe.wait_ge(s_low, c * J + (j + 1) + AHEAD)
                        for k in range(2):
                            for b in range(CB):
                                ins = pe.transpose(turned[:, j, 0, k * CB + b, 0:R], z16[:, j, k, b * 128:(b + 1) * 128],
                                                   m.ident16[0:R, 0:R])
                        ins.then_inc(s_turned, 1)


def layernorm_cols(nc, m, name, source, rows_out, cols):
    with phase(nc, name) as ph:
        stats = ph.sb("stats", [R, T, 6])
        mv = ph.sb("mv", [R, 2, T])
        sd = ph.sb("sd", [R, T])
        normed = ph.sb("normed", [R, J, C])
        turned = ph.ps("turned", [128, J, 512])
        s_stats, s_mv, s_sd, s_v = (ph.sem(x) for x in ("stats", "mv", "sd", "v"))
        s_normed, s_turned, s_free, s_done, s_rows = (ph.sem(x) for x in ("normed", "turned", "free", "done", "rows"))
        with nc.Block() as block:

            @block.vector
            def _(dve):
                v = Chain(dve, s_v)
                with dve.Fori(0, CHUNKS) as c:
                    for j in range(J):
                        ins = dve.bn_stats(stats[:, c * J + j, :], source[:, c * J + j, :])
                    ins.then_inc(s_stats, 1)
                dve.wait_ge(s_stats, CHUNKS)
                join_stats(v, stats, mv)
                v.done(s_mv)
                dve.wait_ge(s_sd, 1)
                v.link(dve.reciprocal(sd[:, :], sd[:, :]))
                with dve.Fori(0, CHUNKS) as c:
                    for j in range(J):
                        dve.wait_ge(s_free, c * J + (j + 1))
                        dve.tensor_scalar(normed[:, j, :], source[:, c * J + j, :], mv[:, 0, bass.ds(c * J + j, 1)],
                                          sd[:, bass.ds(c * J + j, 1)], ALU.subtract, ALU.mult).then_inc(s_normed, 1)

            @block.gpsimd
            def _(pool):
                if rows_out is not None:
                    with pool.Fori(0, CHUNKS) as c:
                        for j in range(J):
                            pool.wait_ge(s_normed, c * J + (j + 1))
                            pool.tensor_copy(rows_out[:, c * J + j, :], normed[:, j, :]).then_inc(s_rows, 1)

            @block.scalar
            def _(act):
                act.wait_ge(s_mv, 1)
                act.activation(sd[:, :], mv[:, 1, :], ACT.Sqrt, bias=m.eps[0:R, :]).then_inc(s_sd, 1)
                act.sem_inc(s_free, J)
                with act.Fori(0, CHUNKS) as c:
                    for j in range(J):
                        act.wait_ge(s_turned, c * J + (j + 1))
                        at = c * COLS + j * R
                        n = 0
                        for target, gain, shift in cols:
                            if gain is None:
                                ins = act.activation(target[:, :, bass.ds(at, R)],
                                                     turned[:, j, 0:CB * R].rearrange("p (b r) -> p b r", b=CB),
                                                     ACT.Copy)
                            else:
                                for b in range(CB):
                                    ins = act.activation(target[:, b, bass.ds(at, R)], turned[:, j, b * R:(b + 1) * R],
                                                         ACT.Identity, bias=shift[:, b:b + 1], scale=gain[:, b:b + 1])
                        ins.then_inc(s_done, 1)
                        if rows_out is not None:
                            act.wait_ge(s_rows, c * J + (j + 1))
                        act.wait_ge(s_done, c * J + (j + 1))
                        act.sem_inc(s_free, 1)

            @block.tensor
            def _(pe):
                with pe.Fori(0, CHUNKS) as c:
                    for j in range(J):
                        pe.wait_ge(s_normed, c * J + (j + 1))
                        for b in range(CB):
                            ins = pe.transpose(turned[:, j, b * R:(b + 1) * R], normed[:, j, b * 128:(b + 1) * 128],
                                               m.ident[0:R, 0:R])
                        ins.then_inc(s_turned, 1)


def product(pe, out, left, right):
    terms = [(0, 0), (1, 0), (0, 1)]
    todo = [(k, n, b) for b in range(CB) for k, n in terms]
    for i, (k, n, b) in enumerate(todo):
        ins = pe.matmul(out, left(k, b), right(n, b), start=(i == 0), stop=(i == len(todo) - 1))
    return ins


def scaled_rows(nc, m, W):
    with phase(nc, "hs") as ph:
        w = ph.sb("w", [128, CB, C])
        w16 = ph.sb("w16", [128, 2, CB, C], F16)
        out32 = ph.sb("out32", [R, J, C])
        out = ph.sb("out", [R, J, 2, C], F16)
        prod = ph.ps("prod", [R, J, 512])
        s_w, s_split, s_prod, s_out, s_high, s_low, s_stored = (
            ph.sem(x) for x in ("w", "split", "prod", "out", "high", "low", "stored"))
        ph.ahead(s_stored, s_out, s_low)
        with nc.Block() as block:

            @block.sync
            def _(sp):
                sp.dma_start(w[:, :, :], W.rearrange("(b p) n -> p b n", p=128)).then_inc(s_w, 16)
                with sp.Fori(0, CHUNKS) as c:
                    sp.wait_ge(s_low, (c + 1) * J + AHEAD)
                    sp.dma_start(m.gather0.rearrange("(t p) n -> p t n", p=R)[:, bass.ds(c * J, J), :],
                                 out[:, :, :, :].rearrange("p j k n -> p j (k n)")).then_inc(s_stored, 16)
                sp.wait_ge(s_stored, 16 * CHUNKS + AHEAD)

            @block.scalar
            def _(act):
                act.wait_ge(s_w, 16)
                act.activation(w16[:, 0, :, :], w[:, :, :], ACT.Copy, scale=WS).then_inc(s_split, 1)
                with act.Fori(0, CHUNKS) as c:
                    act.wait_ge(s_stored, c * 16 + AHEAD)
                    for j in range(J):
                        act.wait_ge(s_out, c * J + (j + 1) + AHEAD)
                        act.activation(out[:, j, 0, :], out32[:, j, :], ACT.Copy).then_inc(s_high, 1)

            @block.tensor
            def _(pe):
                pe.wait_ge(s_split, 2)
                with pe.Fori(0, CHUNKS) as c:
                    pe.wait_ge(s_out, c * J + AHEAD)
                    for j in range(J):
                        product(pe, prod[:, j, 0:C], lambda k, b: m.zc[:, k, b, bass.ds(c * COLS + j * R, R)],
                                lambda k, b: w16[:, k, b, :]).then_inc(s_prod, 1)

            @block.vector
            def _(dve):
                dve.wait_ge(s_split, 1)
                dve.scalar_tensor_tensor(out=w16[:, 1, :, :], in0=w[:, :, :], scalar=WS, in1=w16[:, 0, :, :],
                                         op0=ALU.mult, op1=ALU.subtract).then_inc(s_split, 1)
                with dve.Fori(0, CHUNKS) as c:
                    dve.wait_ge(s_low, c * J + AHEAD)
                    for j in range(J):
                        dve.wait_ge(s_prod, c * J + (j + 1))
                        dve.tensor_scalar(out32[:, j, :], prod[:, j, 0:C], m.inv_sqrt_degree[:, bass.ds(c * J + j, 1)],
                                          1.0 / WS, ALU.mult, ALU.mult).then_inc(s_out, 1)
                    for j in range(J):
                        dve.wait_ge(s_high, c * J + (j + 1))
                        if j == 0:
                            dve.wait_ge(s_stored, c * 16 + AHEAD)
                        dve.tensor_tensor(out[:, j, 1, :], out32[:, j, :], out[:, j, 0, :], ALU.subtract)\
                            .then_inc(s_low, 1)


def group_bounds(eng, m, g):
    packed = eng.value_load(m.group_table[0:1, bass.ds(g, 1)], min_val=0, max_val=31 + 1024 * (T * G + 3))
    first = eng.snap(packed & 31, min_val=0, max_val=T - 1)
    count = eng.snap((packed >> 5) & 31, min_val=1, max_val=T)
    before = eng.snap(packed >> 10, min_val=0, max_val=T * G + 2)
    return first, count, before


class Adder:

    def __init__(self, nc, dve, name, summed, total, s_total, s_added):
        self.nc, self.dve, self.summed, self.total = nc, dve, summed, total
        self.s_total, self.s_added = s_total, s_added
        self.tiles = [dve.alloc_register(f"{name}_tile{n}") for n in range(LAG)]
        for register in self.tiles:
            dve.reg_mov(register, 0)

    def add(self, visit, tile):
        dve = self.dve
        oldest = dve.snap(self.tiles[0], min_val=0, max_val=T - 1)
        into = self.summed[:, oldest, :]
        fresh = self.total[:, dve.snap((visit + (RING - LAG)) % RING), 0:self.summed.shape[2]]
        for n in range(LAG - 1):
            dve.reg_mov(self.tiles[n], self.tiles[n + 1])
        dve.reg_mov(self.tiles[-1], tile)
        dve.wait_ge(self.s_total, visit + 1)
        dve.wait_ge(self.s_added, visit + LAG)
        dve.tensor_tensor(into, into, fresh, ALU.add).then_inc(self.s_added, 1)

    def finish(self, visits, s_pace):
        for n in range(LAG):
            self.add(visits + n, 0)
        self.dve.wait_ge(self.s_added, visits + 2 * LAG)
        self.dve.sem_inc(s_pace, 1)


class Turner:

    def __init__(self, nc, m, a, ph):
        plan = [("wq", a["L1_gnn_Wq"], C, C, 1), ("wk", a["L1_gnn_Wk"], C, C, 1), ("wv", a["L1_gnn_Wv"], C, C, 1),
                ("wp", a["L1_gnn_Wp"], C, C, 1), ("w1", a["L1_gnn_W1"], F, C, 1), ("w2", a["L1_gnn_W2"], C, F, 1),
                ("conv", a["L1_mix_w_qkv"].rearrange("o i k -> o (i k)"), 3 * C, C, 5),
                ("res", a["L1_mix_w_res"].rearrange("o i k -> o (i k)"), C, 2 * C, 1)]
        m.turned = {name: nc.dram_tensor(f"turned_{name}", [k, n], F32).ap() for name, _, n, k, _ in plan}
        self.m = m
        self.blocks = [(name, W, o, k, taps) for name, W, n, k, taps in plan for o in range(n // 128)]
        wide = max(k * taps for _, _, _, k, taps in plan)
        self.rows = ph.sb("rows", [128, 2, wide])
        self.cols = ph.sb("cols", [128, 2, FB, 128])
        self.bank = ph.ps("bank", [128, 2, FB, 128])
        self.s_in = [ph.sem(f"in{s}") for s in range(2)]
        self.s_out = [ph.sem(f"out{s}") for s in range(2)]
        self.s_turned, self.s_cols = ph.sem("turned"), ph.sem("cols")

    def load(self, sp):
        for i, (name, W, o, k, taps) in enumerate(self.blocks):
            if i >= 2:
                sp.wait_ge(self.s_turned, i - 1)
            sp.dma_start(self.rows[:, i % 2, 0:k * taps], W[o * 128:(o + 1) * 128, :])\
                .then_inc(self.s_in[i % 2], 16)

    def turn(self, pe, part, parts):
        n = len(self.blocks)
        for i in range(n * part // parts, n * (part + 1) // parts):
            name, W, o, k, taps = self.blocks[i]
            pe.wait_ge(self.s_in[i % 2], 16 * (i // 2 + 1))
            if i >= 2:
                pe.wait_ge(self.s_cols, i - 1)
            taken = self.rows[:, i % 2, 0:k * taps].rearrange("p (i k) -> p i k", k=taps)[:, :, taps // 2]
            for b in range(k // 128):
                ins = pe.transpose(self.bank[:, i % 2, b, :], taken[:, b * 128:(b + 1) * 128], self.m.ident[:, :])
            ins.then_inc(self.s_turned, 1)

    def store(self, act):
        for i, (name, W, o, k, taps) in enumerate(self.blocks):
            kb = k // 128
            act.wait_ge(self.s_turned, i + 1)
            if i >= 2:
                act.wait_ge(self.s_out[i % 2], 16 * (i // 2))
            act.activation(self.cols[:, i % 2, 0:kb, :], self.bank[:, i % 2, 0:kb, :], ACT.Copy)\
                .then_inc(self.s_cols, 1)
            act.wait_ge(self.s_cols, i + 1)
            act.dma_start(self.m.turned[name].rearrange("(b p) n -> p b n", p=128)[:, :, o * 128:(o + 1) * 128],
                          self.cols[:, i % 2, 0:kb, :]).then_inc(self.s_out[i % 2], 16)
        n = len(self.blocks)
        act.wait_ge(self.s_out[0], 16 * ((n + 1) // 2))
        act.wait_ge(self.s_out[1], 16 * (n // 2))


def message_sum(nc, m, a):
    with phase(nc, "ms") as ph:
        index = ph.sb("index", [R, SLOTS, J], I32)
        got = ph.sb("got", [R, SLOTS, J, 2 * C], F16)
        hot = ph.sb("hot", [R, RING, J, R], F16)
        node_no = ph.sb("node_no", [R, N])
        s_node = ph.sem("node")
        summed = ph.sb("summed", [R, T, C])
        total = ph.ps("total", [R, RING, 512])
        s_index, s_got = ph.sem("index"), [ph.sem(f"got{s}") for s in range(SLOTS)]
        s_hot, s_total, s_added, s_zero = (ph.sem(x) for x in ("hot", "total", "added", "zero"))
        s_pace = ph.sem("pace")
        ph.ahead(*[s_total, s_added] * LAG)
        turner = Turner(nc, m, a, ph)
        with nc.Block() as block:

            @block.sync
            def _(sp):
                turner.load(sp)

            @block.scalar
            def _(act):
                turner.store(act)

            @block.gpsimd
            def _(pool):
                pool.iota(node_no[:, :], pattern=[[1, N]], base=0, channel_multiplier=0,
                          allow_small_or_imprecise_dtypes=True).then_inc(s_node, 1)
                with pool.Fori(0, G // SLOTS) as i:
                    for s in range(SLOTS):
                        pool.wait_ge(s_index, i * SLOTS + (s + 1))
                        pool.sem_inc(s_pace, 1)
                        for j in range(J):
                            pool.indirect_dma_start(
                                out=got[:, s, j, :], out_offset=None, in_=m.gather0,
                                in_offset=bass.IndirectOffsetOnAxis(ap=index[:, s, j:j + 1], axis=0)
                            ).then_inc(s_got[s], 16)

            @block.vector
            def _(dve):
                dve.memset(summed[:, :, :], 0.0).then_inc(s_zero, 1)
                dve.memset(total[:, :, :], 0.0).then_inc(s_zero, 1)
                dve.wait_ge(s_zero, 2)
                dve.wait_ge(s_node, 1)
                for s in range(SLOTS - 1):
                    dve.tensor_copy(index[:, s, :], m.edge_src[:, s, :]).then_inc(s_index, 1)
                adder = Adder(nc, dve, "ms", summed, total, s_total, s_added)
                with dve.Fori(0, G // SLOTS) as i:
                    for s in range(SLOTS):
                        g = i * SLOTS + s
                        first, count, before = group_bounds(dve, m, g)
                        with dve.Fori(0, count) as k:
                            visit = dve.snap(before + k)
                            tile = dve.snap(nc.s_assert_within(first + k, 0, T - 1))
                            dve.tensor_tensor(hot[:, visit % RING, :, :],
                                              repeat_mid(node_no[:, bass.ds(tile * R, R)], J),
                                              repeat_last(m.edge_dst[:, g, :], R), ALU.is_equal)\
                                .then_inc(s_hot, 1)
                            adder.add(visit, tile)
                        free = (s - 1) % SLOTS
                        dve.wait_ge(s_total, before + LAG)
                        dve.sem_inc(s_pace, 1)
                        nxt = m.edge_src[:, bass.ds(g + SLOTS - 1, 1), :].rearrange("p a j -> p (a j)")
                        dve.tensor_copy(index[:, free, :], nxt).then_inc(s_index, 1)
                adder.finish(dve.snap(before + count), s_pace)
                with dve.Fori(0, CHUNKS) as c:
                    for j in range(J):
                        t = c * J + j
                        dve.scalar_tensor_tensor(out=m.x[:, t, :], in0=summed[:, t, :],
                                                 scalar=m.inv_sqrt_degree[:, bass.ds(t, 1)], in1=m.x[:, t, :],
                                                 op0=ALU.mult, op1=ALU.add).then_inc(s_zero, 1)

            @block.tensor
            def _(pe):
                pe.wait_ge(s_zero, 2)
                PARTS = 5
                each = G // SLOTS // PARTS
                for part in range(PARTS):
                    with pe.Fori(part * each, (part + 1) * each) as i:
                        for s in range(SLOTS):
                            g = i * SLOTS + s
                            first, count, before = group_bounds(pe, m, g)
                            pe.wait_ge(s_got[s], (i + 1) * (16 * J))
                            pe.sem_inc(s_pace, 1)
                            with pe.Fori(0, count) as k:
                                visit = pe.snap(before + k)
                                pe.wait_ge(s_hot, visit + 1)
                                pe.wait_ge(s_added, visit + 1)
                                for j in range(J):
                                    for p in range(2):
                                        ins = pe.matmul(total[:, visit % RING, 0:C], hot[:, visit % RING, j, :],
                                                        got[:, s, j, p * C:(p + 1) * C],
                                                        start=(j + p == 0), stop=(j + p == J))
                                ins.then_inc(s_total, 1)
                    turner.turn(pe, part, PARTS)


def load_vectors(nc, m, a):
    plan, at = [], 0
    blocks = {}
    for name in ("L0_mix_ln1_g", "L0_mix_ln1_b", "L0_mix_bx", "L0_mix_ln2_g", "L0_mix_ln2_b", "L0_mix_b1",
                 "L0_ffn_b1", "L0_ffn_g1", "L0_ffn_be1", "L0_ffn_m1", "L0_ffn_v1",
                 "L0_ffn_b2", "L0_ffn_g2", "L0_ffn_be2", "L0_ffn_m2", "L0_ffn_v2",
                 "L1_gnn_ln_g", "L1_gnn_ln_b", "L1_gnn_b1", "L1_mix_bn_gamma", "L1_mix_bn_beta",
                 "L1_mix_w_dw", "L1_ffn_b1s", "L1_ffn_b1p"):
        ap = a[name]
        if name == "L1_mix_w_dw":
            ap = ap.rearrange("c a k -> (c a) k")[:, 2:3].rearrange("(b p) k -> b (p k)", p=128)
        elif len(ap.shape) == 2:
            ap = ap.rearrange("e (b p) -> (e b) p", p=128)
        else:
            ap = ap.rearrange("(b p) -> b p", p=128)
        n = ap.shape[0]
        blocks[name] = (at, n)
        done = 0
        while done < n:
            k = min(n - done, 128 - at % 128)
            plan.append((at // 128, at % 128, k, ap[done:done + k, :]))
            at += k
            done += k
    total = -(-at // 128)
    rows = [("L0_mix_bo", C), ("L0_mix_b2", C), ("L0_ffn_br", X8), ("L1_gnn_bq", C), ("L1_gnn_bk", C),
            ("L1_gnn_bv", C), ("L1_gnn_bp", C), ("L1_gnn_b2", C), ("L1_mix_b_res", C), ("L1_ffn_b2s", C)]
    with phase(nc, "vec") as ph:
        stack = ph.sb("stack", [128, total, 128])
        turned = ph.ps("turned", [128, total, 128])
        s_in, s_row, s_turned, s_zero = ph.sem("in"), ph.sem("row"), ph.sem("turned"), ph.sem("zero")
        with nc.Block() as block:

            @block.sync
            def _(sp):
                sp.wait_ge(s_zero, 1)
                for b, p, k, ap in plan:
                    sp.dma_start(stack[p:p + k, b, :], ap, allow_slow_non_contiguous=True).then_inc(s_in, 16)
                for i, (name, n) in enumerate(rows):
                    sp.dma_start(m.rowvec[:, i, 0:n], a[name].unsqueeze(0).broadcast_to([R, n])).then_inc(s_row, 16)
                sp.wait_ge(s_row, 16 * len(rows))

            @block.tensor
            def _(pe):
                pe.wait_ge(s_in, 16 * len(plan))
                for b in range(total):
                    ins = pe.transpose(turned[:, b, :], stack[:, b, :], m.ident[:, :])
                ins.then_inc(s_turned, 1)

            @block.vector
            def _(dve):
                dve.memset(stack[:, :, :], 0.0).then_inc(s_zero, 1)
                dve.wait_ge(s_turned, 1)
                dve.tensor_copy(m.colvec[:, 0:total * 128].rearrange("p (b c) -> p b c", b=total), turned[:, :, :])\
                    .then_inc(s_zero, 1)
                dve.wait_ge(s_zero, 2)
    m.col = {name: m.colvec[:, at:at + n] for name, (at, n) in blocks.items()}
    m.row = {name: m.rowvec[:, i, 0:n] for i, (name, n) in enumerate(rows)}


def feed_forward(nc, m, name, experts, W1, b1, W2, gate=None, gain=None, bias_in=None):
    slots = min(experts, 2)
    WALL = CB * F + FB * C
    PIECE = -(-WALL // CHUNKS)
    STRIDE = (WALL - PIECE) // (CHUNKS - 1)
    with phase(nc, name) as ph:
        w = ph.sb("w", [128, WALL])
        w16 = ph.sb("w16", [128, slots, 2, WALL], F16)
        hidden = ph.sb("hidden", [128, 2, FB, COLS], F16)
        h32 = ph.sb("h32", [128, 4, HALVES[0][1]])
        bias = ph.sb("bias", [128, FB])
        gain_s = ph.sb("gain_s", [128, CB])
        up = ph.ps("up", [128, 4, 512])
        down = ph.ps("down", [128, 4, 512])
        s_w, s_high, s_low, s_gain, s_through, s_bias, s_pace = (
            ph.sem(x) for x in ("w", "high", "low", "gain", "through", "bias", "pace"))
        s_up, s_h32, s_hhigh, s_hidden, s_down, s_added = (
            ph.sem(x) for x in ("up", "h32", "hhigh", "hidden", "down", "added"))
        ph.ahead(s_h32, s_hidden, s_down, s_added)
        units = FB * len(HALVES)
        w1_32 = w[:, 0:CB * F].rearrange("p (b n) -> p b n", b=CB)

        def part(s, k, layer, b, at, n):
            start = b * F + at if layer == 0 else CB * F + b * C + at
            return w16[:, s, k, start:start + n]

        with nc.Block() as block:

            @block.sync
            def _(sp):
                def load(e):
                    sp.dma_start(w1_32, W1(e).rearrange("(b p) n -> p b n", p=128)).then_inc(s_w, 16)
                    sp.dma_start(w[:, CB * F:].rearrange("p (b n) -> p b n", b=FB),
                                 W2(e).rearrange("(b p) n -> p b n", p=128)).then_inc(s_w, 16)

                load(0)
                if experts > 1:
                    sp.wait_ge(s_low, 1)
                    load(1)
                    with sp.Fori(1, experts) as e:
                        sp.wait_ge(s_low, e * CHUNKS + 1)
                        load((e + 1) % experts)
                    sp.wait_ge(s_w, 32 * (experts + 1))

            @block.tensor
            def _(pe):
                if bias_in is not None:
                    pe.wait_ge(s_w, 32)
                    for f in range(FB):
                        for b in range(CB):
                            ins = pe.matmul(down[:, 0, f:f + 1], w1_32[:, b, f * 128:(f + 1) * 128],
                                            bias_in[:, b:b + 1], start=(b == 0), stop=(b == CB - 1))
                    ins.then_inc(s_through, 1)
                    pe.wait_ge(s_bias, 1)
                with pe.Fori(0, max(experts // 2, 1)) as i:
                    for s in range(slots):
                        e = i * slots + s
                        pe.wait_ge(s_low, e * CHUNKS + 1)
                        pe.sem_inc(s_pace, 1)
                        with pe.Fori(0, CHUNKS) as c:
                            step = e * CHUNKS + c
                            for u in range(units):
                                f, (at, n) = u // 2, HALVES[u % 2]
                                pe.wait_ge(s_h32, step * units + max(u - 3, 0) + AHEAD)
                                product(pe, up[:, u % 4, 0:n], lambda k, b: part(s, k, 0, b, f * 128, 128),
                                        lambda k, b: m.zc[:, k, b, bass.ds(c * COLS + at, n)]).then_inc(s_up, 1)
                            for j in range(J):
                                if j == 0 or j == 4:
                                    pe.wait_ge(s_added, step * J + j // 4 + AHEAD)
                                for f in range(FB):
                                    if j == 0:
                                        pe.wait_ge(s_hidden, step * units + 2 * (f + 1) + AHEAD)
                                    for n, (k, r) in enumerate(((0, 0), (1, 0), (0, 1))):
                                        ins = pe.matmul(down[0:R, j % 4, 0:C], hidden[:, k, f, j * R:(j + 1) * R],
                                                        part(s, r, 1, f, 0, C), start=(f + n == 0),
                                                        stop=(f == FB - 1 and n == 2))
                                ins.then_inc(s_down, 1)

            @block.scalar
            def _(act):
                act.wait_ge(s_w, 32)
                if gain is None:
                    act.activation(w16[:, 0, 0, :], w[:, :], ACT.Copy, scale=WS).then_inc(s_high, 1)
                else:
                    act.wait_ge(s_gain, 1)
                    for b in range(CB):
                        act.activation(w16[:, 0, 0, b * F:(b + 1) * F], w[:, b * F:(b + 1) * F], ACT.Copy,
                                       scale=gain_s[:, b:b + 1])
                    act.activation(w16[:, 0, 0, CB * F:], w[:, CB * F:], ACT.Copy, scale=WS).then_inc(s_high, 1)
                    act.wait_ge(s_bias, 1)
                with act.Fori(0, max(experts // 2, 1)) as i:
                    for s in range(slots):
                        e = i * slots + s
                        if bias_in is None:
                            act.wait_ge(s_h32, e * (units * CHUNKS) + AHEAD)
                            act.sem_inc(s_pace, 1)
                            act.activation(bias[:, :], b1[:, bass.ds(e * FB, FB)], ACT.Copy).then_inc(s_bias, 1)
                            act.wait_ge(s_bias, e + 1)
                        with act.Fori(0, CHUNKS) as c:
                            step = e * CHUNKS + c
                            for u in range(units):
                                f, (at, n) = u // 2, HALVES[u % 2]
                                act.wait_ge(s_up, step * units + (u + 1))
                                act.wait_ge(s_hidden, step * units + max(u - 3, 0) + AHEAD)
                                act.activation(h32[:, u % 4, 0:n], up[:, u % 4, 0:n], ACT.Gelu,
                                               scale=1.0 / WS, bias=bias[:, f:f + 1]).then_inc(s_h32, 1)
                            if experts > 1:
                                act.wait_ge(s_w, (e + 2) * 32)
                                act.sem_inc(s_pace, 1)
                                piece = bass.ds(c * STRIDE, PIECE)
                                act.activation(w16[:, 1 - s, 0, piece], w[:, piece], ACT.Copy, scale=WS)\
                                    .then_inc(s_high, 1)

            @block.vector
            def _(dve):
                if gain is not None:
                    dve.tensor_scalar(gain_s[:, :], gain, WS, None, ALU.mult).then_inc(s_gain, 1)
                    dve.wait_ge(s_gain, 1)
                dve.wait_ge(s_high, 1)
                if gain is None:
                    ins = dve.scalar_tensor_tensor(out=w16[:, 0, 1, :], in0=w[:, :], scalar=WS, in1=w16[:, 0, 0, :],
                                                   op0=ALU.mult, op1=ALU.subtract)
                else:
                    for b in range(CB):
                        at = slice(b * F, (b + 1) * F)
                        dve.scalar_tensor_tensor(out=w16[:, 0, 1, at], in0=w[:, at], scalar=gain_s[:, b:b + 1],
                                                 in1=w16[:, 0, 0, at], op0=ALU.mult, op1=ALU.subtract)
                    ins = dve.scalar_tensor_tensor(out=w16[:, 0, 1, CB * F:], in0=w[:, CB * F:], scalar=WS,
                                                   in1=w16[:, 0, 0, CB * F:], op0=ALU.mult, op1=ALU.subtract)
                ins.then_inc(s_low, 1)
                if bias_in is not None:
                    dve.wait_ge(s_through, 1)
                    dve.tensor_tensor(bias[:, :], down[:, 0, 0:FB], b1, ALU.add).then_inc(s_bias, 1)
                with dve.Fori(0, max(experts // 2, 1)) as i:
                    for s in range(slots):
                        e = i * slots + s
                        with dve.Fori(0, CHUNKS) as c:
                            step = e * CHUNKS + c
                            for u in range(units):
                                f, (at, n) = u // 2, HALVES[u % 2]
                                full = h32[:, u % 4, 0:n]
                                dve.wait_ge(s_h32, step * units + (u + 1) + AHEAD)
                                if u == 0:
                                    dve.wait_ge(s_down, step * J + AHEAD)
                                dve.tensor_copy(hidden[:, 0, f, at:at + n], full).then_inc(s_hhigh, 1)
                                dve.wait_ge(s_hhigh, step * units + (u + 1))
                                dve.tensor_tensor(hidden[:, 1, f, at:at + n], full,
                                                  hidden[:, 0, f, at:at + n], ALU.subtract).then_inc(s_hidden, 1)
                            if experts > 1:
                                dve.wait_ge(s_high, step + 2)
                                piece = bass.ds(c * STRIDE, PIECE)
                                dve.scalar_tensor_tensor(out=w16[:, 1 - s, 1, piece], in0=w[:, piece], scalar=WS,
                                                         in1=w16[:, 1 - s, 0, piece], op0=ALU.mult,
                                                         op1=ALU.subtract).then_inc(s_low, 1)
                            for j in range(J):
                                t = c * J + j
                                dve.wait_ge(s_down, step * J + (j + 1) + AHEAD)
                                dve.scalar_tensor_tensor(
                                    out=m.x[:, t, :], in0=down[0:R, j % 4, 0:C],
                                    scalar=1.0 / WS if gate is None else gate[:, t, bass.ds(e, 1)], in1=m.x[:, t, :],
                                    op0=ALU.mult, op1=ALU.add).then_inc(s_added, 1)


def mixer0(nc, m, a):
    with phase(nc, "mix") as ph:
        wx = ph.sb("wx", [128, CB, C])
        wo = ph.sb("wo", [128, CB, C])
        QV = X8 * KR + C
        wqv = ph.sb("wqv", [128, CB, QV])
        wk = ph.sb("wk", [128, CB, X8 * KR])
        mine = ph.sb("mine", [X8 * KR, X8, HD])
        mixed = ph.sb("mixed", [128, CB, COLS])
        k_cols = ph.sb("k_cols", [X8 * KR, N])
        q = ph.sb("q", [R, T * X8, KR])
        qstat = ph.sb("qstat", [R, T * X8])
        kmax = ph.sb("kmax", [X8 * KR, 1])
        ksums = ph.sb("ksums", [X8 * KR, CHUNKS])
        ksum = ph.sb("ksum", [X8 * KR, 1])
        ek = ph.sb("ek", [X8 * KR, COLS])
        ek_rows = ph.sb("ek_rows", [R, J, X8 * KR])
        kv = ph.sb("kv", [X8 * KR, C])
        kv_cols = ph.sb("kv_cols", [128, CB, X8 * KR])
        read = ph.sb("read", [X8 * KR, C])
        qc = ph.sb("qc", [R, J, X8 * KR])
        q_cols = ph.sb("q_cols", [X8 * KR, COLS])
        bank4 = ph.ps("bank4", [128, 4, 512])
        kbank = ph.ps("kbank", [X8 * KR, 2, 512])
        rbank = ph.ps("rbank", [R, 2, 512])
        s_w, s_zero, s_mask, s_bd = ph.sem("w"), ph.sem("zero"), ph.sem("mask"), ph.sem("bd")
        s_mix, s_mixed, s_k, s_kout, s_qv, s_qvout = (ph.sem(x) for x in ("mix", "mixed", "k", "kout", "qv", "qvout"))
        s_v, s_kmax, s_ek, s_ekt, s_ekr, s_kv, s_kvadd = (ph.sem(x) for x in ("v", "kmax", "ek", "ekt", "ekr", "kv", "kvadd"))
        s_kvm, s_kvt, s_kvc, s_read, s_readout = (ph.sem(x) for x in ("kvm", "kvt", "kvc", "read", "readout"))
        s_qmax, s_qexp, s_qc, s_qt, s_qcols, s_at, s_fx = (ph.sem(x) for x in ("qmax", "qexp", "qc", "qt", "qcols", "at", "fx"))
        s_act, s_bias, s_added = ph.sem("act"), ph.sem("bias"), ph.sem("added")
        bo, b2 = m.row["L0_mix_bo"], m.row["L0_mix_b2"]
        nbd = 3 * X8
        ph.ahead(s_ekr, s_ekt, s_fx, s_kout, s_kv, s_kvadd, s_mixed, s_qcols, s_qt, s_qv, s_qvout)
        with nc.Block() as block:

            @block.gpsimd
            def _(pool):
                pool.memset(wqv[:, :, :], 0.0).then_inc(s_zero, 1)
                pool.memset(wk[:, :, :], 0.0).then_inc(s_zero, 1)
                pool.memset(mine[:, :, :], 1.0).then_inc(s_mask, 1)
                pool.wait_ge(s_mask, 1)
                pool.affine_select(out=mine[:, :, :], in_=mine[:, :, :], compare_op=ALU.is_ge, fill=0.0, base=0,
                                   pattern=[[-KR, X8], [0, HD]], channel_multiplier=1).then_inc(s_mask, 1)
                pool.wait_ge(s_mask, 2)
                pool.affine_select(out=mine[:, :, :], in_=mine[:, :, :], compare_op=ALU.is_ge, fill=0.0,
                                   base=KR - 1, pattern=[[KR, X8], [0, HD]], channel_multiplier=-1)\
                    .then_inc(s_mask, 1)
                with pool.Fori(0, CHUNKS) as c:
                    for rows, bias in ((m.z, bo), (m.x, b2)):
                        some = rows[:, bass.ds(c * J, J), :]
                        ins = pool.tensor_tensor(some, some, repeat_mid(bias, J), ALU.add)
                    ins.then_inc(s_bias, 1)

            @block.sync
            def _(sp):
                sp.dma_start(wx[:, :, :], a["L0_mix_Wx"].rearrange("(b p) n -> p b n", p=128)).then_inc(s_w, 16)
                sp.dma_start(wo[:, :, :], a["L0_mix_Wo"].rearrange("(b p) n -> p b n", p=128)).then_inc(s_w, 16)
                sp.wait_ge(s_zero, 2)
                for h in range(X8):
                    p = slice(HD * (h % 4), HD * (h % 4) + HD)
                    sp.dma_start(wqv[p, h // 4, KR * h:KR * h + KR], a["L0_mix_Wq"]).then_inc(s_bd, 16)
                    sp.dma_start(wk[p, h // 4, KR * h:KR * h + KR], a["L0_mix_Wk"]).then_inc(s_bd, 16)
                    at = X8 * KR + HD * h
                    sp.dma_start(wqv[p, h // 4, at:at + HD], a["L0_mix_Wv"]).then_inc(s_bd, 16)

            @block.tensor
            def _(pe):
                pe.wait_ge(s_w, 32)
                pe.wait_ge(s_bd, 16 * nbd)
                pe.sem_inc(s_act, 1)
                with pe.Fori(0, CHUNKS) as c:
                    for u in range(4):
                        o, (at, n) = u // 2, HALVES[u % 2]
                        if u == 0:
                            pe.wait_ge(s_mixed, c * 4 + AHEAD)
                        for b in range(CB):
                            ins = pe.matmul(bank4[:, u, 0:n], wx[:, b, o * 128:(o + 1) * 128],
                                            m.z_cols[:, b, bass.ds(c * COLS + at, n)],
                                            start=(b == 0), stop=(b == CB - 1))
                        ins.then_inc(s_mix, 1)
                    pe.wait_ge(s_mixed, c * 4 + 4 + AHEAD)
                    pe.wait_ge(s_kout, c * 2 + AHEAD)
                    for u, (at, n) in enumerate(HALVES):
                        for b in range(CB):
                            ins = pe.matmul(kbank[:, u, 0:n], wk[:, b, :], mixed[:, b, at:at + n],
                                            start=(b == 0), stop=(b == CB - 1))
                        ins.then_inc(s_k, 1)
                    for j in range(J):
                        pe.wait_ge(s_qvout, (c * J + (j - 1) if j else c * J) + AHEAD)
                        for b in range(CB):
                            ins = pe.matmul(rbank[:, j % 2, 0:QV], mixed[:, b, j * R:(j + 1) * R], wqv[:, b, :],
                                            start=(b == 0), stop=(b == CB - 1))
                        ins.then_inc(s_qv, 1)
                with pe.Fori(0, CHUNKS) as c:
                    pe.wait_ge(s_ek, c + 1)
                    pe.wait_ge(s_ekr, c + AHEAD)
                    pe.wait_ge(s_qvout, CHUNKS * J + AHEAD)
                    pe.sem_inc(s_act, 1)
                    for j in range(J):
                        ins = pe.transpose(rbank[:, 0, j * X8 * KR:(j + 1) * X8 * KR], ek[:, j * R:(j + 1) * R],
                                           m.ident[0:X8 * KR, 0:X8 * KR])
                    ins.then_inc(s_ekt, 1)
                    pe.wait_ge(s_ekr, c + 1 + AHEAD)
                    pe.wait_ge(s_kvadd, c + AHEAD)
                    for j in range(J):
                        ins = pe.matmul(kbank[:, 0, 0:C], ek_rows[:, j, :], m.y[:, c * J + j, :],
                                        start=(j == 0), stop=(j == J - 1))
                    ins.then_inc(s_kv, 1)
                pe.wait_ge(s_kvm, 1)
                for b in range(CB):
                    ins = pe.transpose(bank4[:, 0, b * X8 * KR:(b + 1) * X8 * KR], kv[:, b * 128:(b + 1) * 128],
                                       m.ident[0:X8 * KR, 0:X8 * KR])
                ins.then_inc(s_kvt, 1)
                pe.wait_ge(s_kvc, 1)
                for b in range(CB):
                    ins = pe.matmul(kbank[:, 1, 0:C], kv_cols[:, b, :], wo[:, b, :], start=(b == 0), stop=(b == CB - 1))
                ins.then_inc(s_read, 1)
                pe.wait_ge(s_readout, 1)
                with pe.Fori(0, CHUNKS) as c:
                    pe.wait_ge(s_qc, c + 1)
                    pe.wait_ge(s_qcols, c + AHEAD)
                    for j in range(J):
                        ins = pe.transpose(bank4[0:X8 * KR, j // 4, (j % 4) * R:(j % 4 + 1) * R], qc[:, j, :],
                                           m.ident[0:R, 0:R])
                    ins.then_inc(s_qt, 1)
                    pe.wait_ge(s_qcols, c + 1 + AHEAD)
                    for j in range(J):
                        pe.wait_ge(s_fx, (c * J + (j - 1) if j else c * J) + AHEAD)
                        pe.matmul(rbank[:, j % 2, 0:C], q_cols[:, j * R:(j + 1) * R], read[:, :],
                                  start=True, stop=True).then_inc(s_at, 1)

            @block.scalar
            def _(act):
                with act.Fori(0, CHUNKS) as c:
                    for u in range(4):
                        o, (at, n) = u // 2, HALVES[u % 2]
                        act.wait_ge(s_mix, c * 4 + (u + 1))
                        if u == 0:
                            act.wait_ge(s_qv, c * J + AHEAD)
                        act.activation(mixed[:, o, at:at + n], bank4[:, u, 0:n], ACT.Identity,
                                       bias=m.col["L0_mix_bx"][:, o:o + 1]).then_inc(s_mixed, 1)
                    for u, (at, n) in enumerate(HALVES):
                        act.wait_ge(s_k, c * 2 + (u + 1))
                        act.activation(k_cols[:, bass.ds(c * COLS + at, n)], kbank[:, u, 0:n], ACT.Copy)\
                            .then_inc(s_kout, 1)
                act.wait_ge(s_kmax, 1)
                with act.Fori(0, CHUNKS) as c:
                    act.wait_ge(s_ekt, c + AHEAD)
                    act.activation(ek[:, :], k_cols[:, bass.ds(c * COLS, COLS)], ACT.Exp, bias=kmax[:, :],
                                   accum_out=ksums[:, bass.ds(c, 1)]).then_inc(s_ek, 1)
                act.wait_ge(s_qmax, 1)
                act.activation(q[:, :, :], q[:, :, :], ACT.Exp).then_inc(s_qexp, 1)

            @block.vector
            def _(dve):
                v = Chain(dve, s_v)
                q_t = q[:, :, :].rearrange("p (t h) k -> p t (h k)", t=T)
                with dve.Fori(0, CHUNKS) as c:
                    for j in range(J):
                        dve.wait_ge(s_qv, c * J + (j + 1) + AHEAD)
                        dve.tensor_copy(q_t[:, c * J + j, :], rbank[:, j % 2, 0:X8 * KR])
                        dve.tensor_copy(m.y[:, c * J + j, :], rbank[:, j % 2, X8 * KR:QV]).then_inc(s_qvout, 1)
                dve.wait_ge(s_kout, 2 * CHUNKS + AHEAD)
                v.link(dve.tensor_reduce(kmax[:, :], k_cols[:, :], AX_X, ALU.max))
                dve.tensor_scalar(kmax[:, :], kmax[:, :], -1.0, None, ALU.mult).then_inc(s_kmax, 1)
                dve.wait_ge(s_qvout, T + AHEAD)
                v.link(dve.tensor_reduce(qstat[:, :], q[:, :, :], AX_X, ALU.max))
                v.link(dve.tensor_tensor(q[:, :, :], q[:, :, :], repeat_last(qstat[:, :], KR), ALU.subtract))
                v.done(s_qmax)
                v.link(dve.memset(kv[:, :], 0.0))
                with dve.Fori(0, CHUNKS) as c:
                    v.enter(c, 1)
                    dve.wait_ge(s_ekt, c + 1 + AHEAD)
                    dve.wait_ge(s_kv, c + AHEAD)
                    dve.tensor_copy(ek_rows[:, :, :].rearrange("p j k -> p (j k)"), rbank[:, 0, 0:J * X8 * KR])\
                        .then_inc(s_ekr, 1)
                    dve.wait_ge(s_kv, c + 1 + AHEAD)
                    v.link(dve.tensor_tensor(kv[:, :], kv[:, :], kbank[:, 0, 0:C], ALU.add))
                    dve.sem_inc(s_kvadd, 1)
                v.leave(CHUNKS)
                dve.wait_ge(s_mask, 3)
                dve.tensor_tensor(kv[:, :], kv[:, :], mine[:, :, :].rearrange("p h d -> p (h d)"), ALU.mult)\
                    .then_inc(s_kvm, 1)
                dve.wait_ge(s_kvt, 1)
                dve.tensor_copy(kv_cols[:, :, :].rearrange("p b k -> p (b k)"), bank4[:, 0, 0:CB * X8 * KR])\
                    .then_inc(s_kvc, 1)
                v.link(dve.tensor_reduce(ksum[:, :], ksums[:, :], AX_X, ALU.add))
                v.link(dve.reciprocal(ksum[:, :], ksum[:, :]))
                dve.wait_ge(s_read, 1)
                dve.tensor_scalar(read[:, :], kbank[:, 1, 0:C], ksum[:, :], None, ALU.mult).then_inc(s_readout, 1)
                dve.wait_ge(s_qexp, 1)
                v.link(dve.tensor_reduce(qstat[:, :], q[:, :, :], AX_X, ALU.add))
                v.link(dve.reciprocal(qstat[:, :], qstat[:, :]))
                with dve.Fori(0, CHUNKS) as c:
                    dve.wait_ge(s_qt, c + AHEAD)
                    dve.tensor_tensor(qc[:, :, :].rearrange("p j (h k) -> p (j h) k", k=KR),
                                      q[:, bass.ds(c * J * X8, J * X8), :],
                                      repeat_last(qstat[:, bass.ds(c * J * X8, J * X8)], KR), ALU.mult)\
                        .then_inc(s_qc, 1)
                    dve.wait_ge(s_qt, c + 1 + AHEAD)
                    dve.tensor_copy(q_cols[:, 0:4 * R], bank4[0:X8 * KR, 0, 0:4 * R])
                    dve.tensor_copy(q_cols[:, 4 * R:5 * R], bank4[0:X8 * KR, 1, 0:R]).then_inc(s_qcols, 1)
                    for j in range(J):
                        if j == 0:
                            dve.wait_ge(s_bias, c + 1)
                        dve.wait_ge(s_at, c * J + (j + 1))
                        dve.tensor_tensor(m.y[:, c * J + j, :], rbank[:, j % 2, 0:C], m.z[:, c * J + j, :], ALU.add)\
                            .then_inc(s_fx, 1)
                    dve.wait_ge(s_fx, (c + 1) * J + AHEAD)
                    x, y = (rows[:, bass.ds(c * J, J), :] for rows in (m.x, m.y))
                    dve.tensor_tensor(x, x, y, ALU.add).then_inc(s_added, 1)


def router(nc, m, name, Wr, br, top2, bias2, bias_row=None):
    with phase(nc, name) as ph:
        wr = ph.sb("wr", [128, CB, X8])
        b2 = ph.sb("b2", [X8, C])
        wr16 = ph.sb("wr16", [128, 2, CB, X8], F16)
        stat = ph.sb("stat", [R, 2, T])
        work = ph.sb("work", [R, 2, T, X8])
        prefer = ph.sb("prefer", [R, X8])
        gc = ph.sb("gc", [R, J, X8])
        g_cols = ph.sb("g_cols", [X8, COLS])
        score = ph.ps("score", [R, J, X8])
        turned = ph.ps("turned", [X8, 2, 512])
        bank = ph.ps("bank", [R, 3, 512])
        s_w, s_split, s_score, s_read, s_exp, s_gone, s_v = (ph.sem(x) for x in ("w", "split", "score", "read", "exp", "gone", "v"))
        s_gc, s_turned, s_gcols, s_prod, s_added, s_pace = (ph.sem(x) for x in ("gc", "turned", "gcols", "prod", "added", "pace"))
        s_prefer, s_bias = ph.sem("prefer"), ph.sem("bias")
        gate = m.gate
        ph.ahead(s_added, s_gcols, s_prod, s_read, s_score, s_turned)
        with nc.Block() as block:

            @block.sync
            def _(sp):
                sp.dma_start(wr[:, :, :], Wr.rearrange("(b p) n -> p b n", p=128)).then_inc(s_w, 16)
                sp.dma_start(b2[:, :], bias2).then_inc(s_w, 16)

            @block.gpsimd
            def _(pool):
                pool.iota(prefer[:, :], pattern=[[-1, X8]], base=X8, channel_multiplier=0,
                          allow_small_or_imprecise_dtypes=True).then_inc(s_prefer, 1)
                if bias_row is not None:
                    with pool.Fori(0, CHUNKS) as c:
                        chunk = m.x[:, bass.ds(c * J, J), :]
                        pool.tensor_tensor(chunk, chunk, repeat_mid(bias_row, J), ALU.add).then_inc(s_bias, 1)

            @block.scalar
            def _(act):
                act.wait_ge(s_w, 32)
                act.activation(wr16[:, 0, :, :], wr[:, :, :], ACT.Copy, scale=WS).then_inc(s_split, 1)
                act.wait_ge(s_exp, 1)
                act.activation(gate[:, :, :], gate[:, :, :], ACT.Exp).then_inc(s_gone, 1)

            @block.tensor
            def _(pe):
                pe.wait_ge(s_split, 2)
                with pe.Fori(0, CHUNKS) as c:
                    pe.wait_ge(s_read, c + AHEAD)
                    for j in range(J):
                        ins = product(pe, score[:, j, :], lambda k, b: m.zc[:, k, b, bass.ds(c * COLS + j * R, R)],
                                      lambda k, b: wr16[:, k, b, :])
                    ins.then_inc(s_score, 1)
                with pe.Fori(0, CHUNKS) as c:
                    pe.wait_ge(s_gc, c + 1)
                    pe.wait_ge(s_gcols, c + AHEAD)
                    pe.sem_inc(s_pace, 1)
                    for j in range(J):
                        ins = pe.transpose(turned[:, j // 4, (j % 4) * R:(j % 4 + 1) * R], gc[:, j, :],
                                           m.ident[0:R, 0:R])
                    ins.then_inc(s_turned, 1)
                    pe.wait_ge(s_gcols, c + 1 + AHEAD)
                    pe.wait_ge(s_added, c + AHEAD)
                    for j in range(J):
                        ins = pe.matmul(bank[:, j // 2, j % 2 * C:j % 2 * C + C], g_cols[:, j * R:(j + 1) * R], b2[:, :],
                                        start=True, stop=True)
                    ins.then_inc(s_prod, 1)

            @block.vector
            def _(dve):
                v = Chain(dve, s_v)
                dve.wait_ge(s_split, 1)
                dve.scalar_tensor_tensor(out=wr16[:, 1, :, :], in0=wr[:, :, :], scalar=WS, in1=wr16[:, 0, :, :],
                                         op0=ALU.mult, op1=ALU.subtract).then_inc(s_split, 1)
                with dve.Fori(0, CHUNKS) as c:
                    dve.wait_ge(s_score, c + 1 + AHEAD)
                    some = gate[:, bass.ds(c * J, J), :]
                    if br is None:
                        ins = dve.tensor_scalar(some, score[:, :, :], 1.0 / WS, None, ALU.mult)
                    else:
                        ins = dve.scalar_tensor_tensor(out=some, in0=score[:, :, :], scalar=1.0 / WS,
                                                       in1=repeat_mid(br, J), op0=ALU.mult, op1=ALU.add)
                    ins.then_inc(s_read, 1)
                dve.wait_ge(s_read, CHUNKS + AHEAD)
                v.link(dve.tensor_reduce(stat[:, 0, :], gate[:, :, :], AX_X, ALU.max))
                v.link(dve.tensor_tensor(gate[:, :, :], gate[:, :, :], repeat_last(stat[:, 0, :], X8), ALU.subtract))
                v.done(s_exp)
                dve.wait_ge(s_gone, 1)
                v.link(dve.tensor_reduce(stat[:, 0, :], gate[:, :, :], AX_X, ALU.add))
                v.link(dve.reciprocal(stat[:, 0, :], stat[:, 0, :]))
                v.link(dve.tensor_tensor(gate[:, :, :], gate[:, :, :], repeat_last(stat[:, 0, :], X8), ALU.mult))
                if top2:
                    left, pick = work[:, 0, :, :], work[:, 1, :, :]
                    v.link(dve.tensor_copy(left, gate[:, :, :]))
                    dve.wait_ge(s_prefer, 1)
                    for _ in range(2):
                        v.link(dve.tensor_reduce(stat[:, 0, :], left, AX_X, ALU.max))
                        v.link(dve.tensor_tensor(pick, left, repeat_last(stat[:, 0, :], X8), ALU.is_equal))
                        v.link(dve.tensor_tensor(pick, pick, repeat_mid(prefer[:, :], T), ALU.mult))
                        v.link(dve.tensor_reduce(stat[:, 1, :], pick, AX_X, ALU.max))
                        v.link(dve.tensor_tensor(pick, pick, repeat_last(stat[:, 1, :], X8), ALU.is_equal))
                        v.link(dve.scalar_tensor_tensor(out=left, in0=pick, scalar=-4.0, in1=left,
                                                        op0=ALU.mult, op1=ALU.add))
                    v.link(dve.tensor_scalar(pick, left, -1.0, None, ALU.is_lt))
                    v.link(dve.tensor_tensor(gate[:, :, :], gate[:, :, :], pick, ALU.mult))
                    v.link(dve.tensor_reduce(stat[:, 0, :], gate[:, :, :], AX_X, ALU.add))
                    v.link(dve.reciprocal(stat[:, 0, :], stat[:, 0, :]))
                    v.link(dve.tensor_tensor(gate[:, :, :], gate[:, :, :], repeat_last(stat[:, 0, :], X8), ALU.mult))
                with dve.Fori(0, CHUNKS) as c:
                    if bias_row is not None:
                        dve.wait_ge(s_bias, c + 1)
                    dve.wait_ge(s_turned, c + AHEAD)
                    dve.tensor_copy(gc[:, :, :], gate[:, bass.ds(c * J, J), :]).then_inc(s_gc, 1)
                    dve.wait_ge(s_turned, c + 1 + AHEAD)
                    dve.wait_ge(s_prod, c + AHEAD)
                    dve.tensor_copy(g_cols[:, 0:4 * R], turned[:, 0, 0:4 * R])
                    dve.tensor_copy(g_cols[:, 4 * R:5 * R], turned[:, 1, 0:R]).then_inc(s_gcols, 1)
                    x = m.x[:, bass.ds(c * J, J), :]
                    dve.wait_ge(s_prod, c + 1 + AHEAD)
                    dve.tensor_tensor(x, x, bank[:, :, :].rearrange("p b c -> p (b c)")[:, 0:J * C]
                                      .rearrange("p (j c) -> p j c", j=J), ALU.add).then_inc(s_added, 1)
                dve.wait_ge(s_turned, CHUNKS + AHEAD)
                v.link(dve.tensor_scalar(gate[:, :, :], gate[:, :, :], 1.0 / WS, None, ALU.mult))


def experts0(nc, m, a):
    with phase(nc, "ex0") as ph:
        NV = X8 * CB
        WALL = 3 * CB * C
        PIECE = -(-WALL // CHUNKS)
        STRIDE = (WALL - PIECE) // (CHUNKS - 1)
        w = ph.sb("w", [128, WALL])
        w16 = ph.sb("w16", [128, 2, 2, WALL], F16)
        scale = ph.sb("scale", [128, 2, NV])
        shift = ph.sb("shift", [128, 2, NV])
        now = ph.sb("now", [128, 2, 2, CB])
        bn_eps = ph.sb("bn_eps", [128, 1])
        h32 = ph.sb("h32", [128, 4, HALVES[0][1]])
        h1 = ph.sb("h1", [128, 2, CB, COLS], F16)
        h2 = ph.sb("h2", [128, 2, CB, COLS], F16)
        up = ph.ps("up", [128, 4, 512])
        down = ph.ps("down", [R, 4, 512])
        s_w, s_high, s_low, s_now = (ph.sem(x) for x in ("w", "high", "low", "now"))
        s_eps, s_sd, s_bn, s_v = (ph.sem(x) for x in ("eps", "sd", "bn", "v"))
        s_up, s_h32, s_hhigh, s_h, s_down, s_added, s_pace = (
            ph.sem(x) for x in ("up", "h32", "hhigh", "h", "down", "added", "pace"))
        col = m.col
        ph.ahead(s_added, s_down, s_h32, s_h)

        def part(s, k, layer, b, at, n):
            start = (layer * CB + b) * C + at
            return w16[:, s, k, start:start + n]

        with nc.Block() as block:

            @block.sync
            def _(sp):
                def load(e):
                    for k, W in enumerate((a["L0_ffn_W1"], a["L0_ffn_W2"], a["L0_ffn_Wo"])):
                        sp.dma_start(w[:, k * CB * C:(k + 1) * CB * C].rearrange("p (b n) -> p b n", b=CB),
                                     W[bass.ds(e, 1), :, :].rearrange("e (b p) n -> p (e b) n", p=128))\
                            .then_inc(s_w, 16)

                load(0)
                sp.wait_ge(s_low, 1)
                load(1)
                with sp.Fori(1, X8) as e:
                    sp.wait_ge(s_low, e * CHUNKS + 1)
                    load((e + 1) % X8)
                sp.wait_ge(s_w, 48 * (X8 + 1))

            @block.tensor
            def _(pe):
                with pe.Fori(0, X8 // 2) as i:
                    for s in range(2):
                        e = i * 2 + s
                        pe.wait_ge(s_low, e * CHUNKS + 1)
                        pe.sem_inc(s_pace, 1)
                        with pe.Fori(0, CHUNKS) as c:
                            step = e * CHUNKS + c
                            for u in range(8):
                                layer, (at, n), o = u // 4, HALVES[u // 2 % 2], u % 2
                                if u < 4:
                                    pe.wait_ge(s_h32, step * 8 + AHEAD)
                                elif u == 4 or u == 6:
                                    pe.wait_ge(s_h, step * 8 + (u - 2) + AHEAD)
                                product(pe, up[:, u % 4, 0:n], lambda k, b: part(s, k, layer, b, o * 128, 128),
                                        (lambda k, b: m.zc[:, k, b, bass.ds(c * COLS + at, n)]) if layer == 0 else
                                        (lambda k, b: h1[:, k, b, at:at + n])).then_inc(s_up, 1)
                            for j in range(J):
                                if j == 0:
                                    pe.wait_ge(s_added, step * J + AHEAD)
                                    pe.wait_ge(s_h, step * 8 + 6 + AHEAD)
                                elif j == 2:
                                    pe.wait_ge(s_h, step * 8 + 8 + AHEAD)
                                elif j == 4:
                                    pe.wait_ge(s_added, step * J + 1 + AHEAD)
                                product(pe, down[:, j % 4, 0:C], lambda k, b: h2[:, k, b, j * R:(j + 1) * R],
                                        lambda k, b: part(s, k, 2, b, 0, C)).then_inc(s_down, 1)

            @block.scalar
            def _(act):
                act.wait_ge(s_eps, 1)
                act.activation(scale[:, 0, :], col["L0_ffn_v1"], ACT.Sqrt, bias=bn_eps[:, :])
                act.activation(scale[:, 1, :], col["L0_ffn_v2"], ACT.Sqrt, bias=bn_eps[:, :]).then_inc(s_sd, 1)
                act.wait_ge(s_w, 48)
                act.activation(w16[:, 0, 0, :], w[:, :], ACT.Copy, scale=WS).then_inc(s_high, 1)
                act.wait_ge(s_bn, 1)
                with act.Fori(0, X8 // 2) as i:
                    for s in range(2):
                        e = i * 2 + s
                        act.wait_ge(s_h, e * (8 * CHUNKS) + AHEAD)
                        act.sem_inc(s_pace, 1)
                        act.activation(now[:, 0, :, :], scale[:, :, bass.ds(e * CB, CB)], ACT.Copy).then_inc(s_now, 1)
                        act.activation(now[:, 1, :, :], shift[:, :, bass.ds(e * CB, CB)], ACT.Copy).then_inc(s_now, 1)
                        act.wait_ge(s_now, e * 2 + 2)
                        with act.Fori(0, CHUNKS) as c:
                            step = e * CHUNKS + c
                            for u in range(8):
                                layer, (at, n), o = u // 4, HALVES[u // 2 % 2], u % 2
                                act.wait_ge(s_up, step * 8 + (u + 1))
                                act.wait_ge(s_h, step * 8 + max(u - 3, 0) + AHEAD)
                                act.activation(h32[:, u % 4, 0:n], up[:, u % 4, 0:n], ACT.Relu,
                                               bias=now[:, 1, layer, o:o + 1],
                                               scale=now[:, 0, layer, o:o + 1]).then_inc(s_h32, 1)
                            act.wait_ge(s_w, (e + 2) * 48)
                            act.sem_inc(s_pace, 1)
                            piece = bass.ds(c * STRIDE, PIECE)
                            act.activation(w16[:, 1 - s, 0, piece], w[:, piece], ACT.Copy, scale=WS)\
                                .then_inc(s_high, 1)

            @block.vector
            def _(dve):
                v = Chain(dve, s_v)
                dve.memset(bn_eps[:, :], 1e-3).then_inc(s_eps, 1)
                dve.wait_ge(s_sd, 1)
                v.link(dve.reciprocal(scale[:, :, :], scale[:, :, :]))
                for k in range(2):
                    b, g, be, mean = (col[f"L0_ffn_{x}{k + 1}"] for x in ("b", "g", "be", "m"))
                    v.link(dve.tensor_tensor(scale[:, k, :], scale[:, k, :], g, ALU.mult))
                    v.link(dve.tensor_tensor(shift[:, k, :], b, mean, ALU.subtract))
                    v.link(dve.tensor_tensor(shift[:, k, :], shift[:, k, :], scale[:, k, :], ALU.mult))
                    v.link(dve.tensor_tensor(shift[:, k, :], shift[:, k, :], be, ALU.add))
                v.link(dve.tensor_scalar(scale[:, :, :], scale[:, :, :], 1.0 / WS, None, ALU.mult))
                v.done(s_bn)
                dve.wait_ge(s_high, 1)
                dve.scalar_tensor_tensor(out=w16[:, 0, 1, :], in0=w[:, :], scalar=WS, in1=w16[:, 0, 0, :],
                                         op0=ALU.mult, op1=ALU.subtract).then_inc(s_low, 1)
                with dve.Fori(0, X8 // 2) as i:
                    for s in range(2):
                        e = i * 2 + s
                        with dve.Fori(0, CHUNKS) as c:
                            step = e * CHUNKS + c
                            for u in range(8):
                                layer, (at, n), o = u // 4, HALVES[u // 2 % 2], u % 2
                                to = h1 if layer == 0 else h2
                                full = h32[:, u % 4, 0:n]
                                dve.wait_ge(s_h32, step * 8 + (u + 1) + AHEAD)
                                if u == 4:
                                    dve.wait_ge(s_down, step * J + AHEAD)
                                dve.tensor_copy(to[:, 0, o, at:at + n], full).then_inc(s_hhigh, 1)
                                dve.wait_ge(s_hhigh, step * 8 + (u + 1))
                                dve.tensor_tensor(to[:, 1, o, at:at + n], full, to[:, 0, o, at:at + n],
                                                  ALU.subtract).then_inc(s_h, 1)
                            dve.wait_ge(s_high, step + 2)
                            piece = bass.ds(c * STRIDE, PIECE)
                            dve.scalar_tensor_tensor(out=w16[:, 1 - s, 1, piece], in0=w[:, piece], scalar=WS,
                                                     in1=w16[:, 1 - s, 0, piece], op0=ALU.mult,
                                                     op1=ALU.subtract).then_inc(s_low, 1)
                            for j in range(J):
                                t = c * J + j
                                dve.wait_ge(s_down, step * J + (j + 1) + AHEAD)
                                dve.scalar_tensor_tensor(out=m.x[:, t, :], in0=down[:, j % 4, 0:C],
                                                         scalar=m.gate[:, t, bass.ds(e, 1)], in1=m.x[:, t, :],
                                                         op0=ALU.mult, op1=ALU.add).then_inc(s_added, 1)




def query_rows(nc, m, a):
    with phase(nc, "qkv") as ph:
        w = ph.sb("w", [128, CB, 3 * C])
        w16 = ph.sb("w16", [128, 2, CB, 3 * C], F16)
        out = ph.sb("out", [R, 2, J, 3 * C])
        q16 = ph.sb("q16", [R, 2, J, 2, C], F16)
        bias = ph.sb("bias", [R, 3 * C])
        prod = ph.ps("prod", [R, 4, 2, 512])
        s_w, s_bias, s_split, s_prod, s_out = (ph.sem(x) for x in ("w", "bias", "split", "prod", "out"))
        s_stored = [ph.sem(f"stored{s}") for s in range(2)]
        s_high, s_low, s_pace = ph.sem("high"), ph.sem("low"), ph.sem("pace")
        ph.ahead(s_out, *s_stored)

        def every_chunk(eng, work):
            with eng.Fori(0, CHUNKS // 2) as i:
                for s in range(2):
                    work(i * 2 + s, i, s)
            work(CHUNKS - 1, CHUNKS // 2, 0)

        with nc.Block() as block:

            @block.sync
            def _(sp):
                for i, name in enumerate(("wq", "wk", "wv")):
                    sp.dma_start(w[:, :, i * C:(i + 1) * C], m.turned[name].rearrange("(b p) n -> p b n", p=128))\
                        .then_inc(s_w, 16)
                def work(c, i, s):
                    sp.wait_ge(s_low, (c + 1) * J)
                    sp.dma_start(m.gather_q.rearrange("(t p) n -> p t n", p=R)[:, bass.ds(c * J, J), :],
                                 q16[:, s, :, :, :].rearrange("p j k n -> p j (k n)")).then_inc(s_stored[s], 16)
                    sp.dma_start(m.gather_kv.rearrange("(t p) n -> p t n", p=R)[:, bass.ds(c * J, J), :],
                                 out[:, s, :, C:3 * C]).then_inc(s_stored[s], 16)

                every_chunk(sp, work)
                sp.wait_ge(s_stored[0], 32 * (CHUNKS - CHUNKS // 2) + AHEAD)
                sp.wait_ge(s_stored[1], 32 * (CHUNKS // 2) + AHEAD)

            @block.scalar
            def _(act):
                act.wait_ge(s_w, 48)
                act.activation(w16[:, 0, :, :], w[:, :, :], ACT.Copy, scale=WS).then_inc(s_split, 1)
                def work(c, i, s):
                    for j in range(J):
                        act.wait_ge(s_out, c * J + (j + 1) + AHEAD)
                        act.sem_inc(s_pace, 1)
                        act.activation(q16[:, s, j, 0, :], out[:, s, j, 0:C], ACT.Copy).then_inc(s_high, 1)

                every_chunk(act, work)

            @block.tensor
            def _(pe):
                pe.wait_ge(s_split, 2)
                def work(c, i, s):
                    for j in range(J):
                        pe.wait_ge(s_out, c * J + max(j - 3, 0) + AHEAD)
                        for k, (at, n) in enumerate(((0, 512), (512, 256))):
                            ins = product(pe, prod[:, j % 4, k, 0:n],
                                          lambda p, b: m.zc[:, p, b, bass.ds(c * COLS + j * R, R)],
                                          lambda p, b: w16[:, p, b, at:at + n])
                        ins.then_inc(s_prod, 1)

                every_chunk(pe, work)

            @block.vector
            def _(dve):
                for i, name in enumerate(("q", "k", "v")):
                    dve.tensor_copy(bias[:, i * C:(i + 1) * C], m.row[f"L1_gnn_b{name}"]).then_inc(s_bias, 1)
                dve.wait_ge(s_split, 1)
                dve.scalar_tensor_tensor(out=w16[:, 1, :, :], in0=w[:, :, :], scalar=WS, in1=w16[:, 0, :, :],
                                         op0=ALU.mult, op1=ALU.subtract).then_inc(s_split, 1)
                dve.wait_ge(s_bias, 3)
                def work(c, i, s):
                    dve.wait_ge(s_stored[s], i * 32 + AHEAD)
                    for j in range(J):
                        dve.wait_ge(s_prod, c * J + (j + 1))
                        for k, (at, n) in enumerate(((0, 512), (512, 256))):
                            ins = dve.scalar_tensor_tensor(out=out[:, s, j, at:at + n], in0=prod[:, j % 4, k, 0:n],
                                                           scalar=1.0 / WS, in1=bias[:, at:at + n],
                                                           op0=ALU.mult, op1=ALU.add)
                        ins.then_inc(s_out, 1)
                    for j in range(J):
                        dve.wait_ge(s_high, c * J + (j + 1))
                        dve.tensor_tensor(q16[:, s, j, 1, :], out[:, s, j, 0:C], q16[:, s, j, 0, :],
                                          ALU.subtract)\
                            .then_inc(s_low, 1)

                every_chunk(dve, work)


def attention_sum(nc, m, dst):
    with phase(nc, "as") as ph:
        PICKS = 4
        W = C + X8
        index = ph.sb("index", [R, SLOTS, J], I32)
        gkv = ph.sb("gkv", [R, SLOTS, J, 2 * C])
        q16 = m.y[:, :, :].rearrange("p t c -> p (t c)").bitcast(F16).rearrange("p (t k c) -> p t k c", t=T, k=2)
        dsts = ph.sb("dsts", [R, 2, J * R], I32)
        minus_node = ph.sb("minus_node", [R, T])
        at = 3 * J * W // 2
        apart = m.z_cols[0:R, 1, at:at + J * R // 2 + 1].bitcast(BF16)[:, 0:J * R]
        pick = ph.sb("pick", [R, PICKS, J * R], F16)
        zeros = ph.sb("zeros", [R, R], F16)
        score = ph.sb("score", [R, J * X8])
        half = N // 2 + 1
        node_no = m.z_cols[0:R, 0, 0:half].bitcast(I16)
        qk = m.z_cols[0:R, 0, half:half + J * C]
        parts_of = "p (k j w) -> p k j w"
        parts = [m.z_cols[0:R, 1, 0:3 * J * W // 2].bitcast(BF16).rearrange(parts_of, k=3, j=J),
                 ph.sb("parts", [R, 3 * J * W], BF16)[:, :].rearrange(parts_of, k=3, j=J)]
        weight = ph.sb("weight", [R, 2, J, X8])
        hot = ph.sb("hot", [R, RING, J, R], F16)
        summed = ph.sb("summed", [R, T, W])
        none = gkv[:, 0, 0, 0:T * X8].rearrange("p (t h) -> p t h", t=T)
        picked = ph.ps("picked", [R, 3, 512])
        total = ph.ps("total", [R, RING, 512])
        s_node, s_q, s_zero = ph.sem("node"), ph.sem("q"), ph.sem("zero")
        s_index, s_got = ph.sem("index"), [ph.sem(f"got{s}") for s in range(SLOTS)]
        s_dst, s_dfree = [ph.sem(f"dst{s}") for s in range(2)], ph.sem("dfree")
        s_apart, s_pick, s_pickv, s_picked, s_qk = (ph.sem(x) for x in ("apart", "pick", "pickv", "picked", "qk"))
        s_score, s_exp, s_spread, s_high, s_rest, s_mid, s_low = (
            ph.sem(x) for x in ("score", "exp", "spread", "high", "rest", "mid", "low"))
        s_hot, s_total, s_added, s_pace, s_v = (ph.sem(x) for x in ("hot", "total", "added", "pace", "v"))
        ph.ahead(s_pick, *[s_total, s_added] * LAG)
        ph.ahead(*[s_pickv] * PICKS)
        with nc.Block() as block:

            @block.gpsimd
            def _(pool):
                pool.iota(node_no[:, 0:N], pattern=[[1, N]], base=0, channel_multiplier=0,
                          allow_small_or_imprecise_dtypes=True).then_inc(s_node, 1)
                pool.iota(minus_node[:, :], pattern=[[-R, T]], base=0, channel_multiplier=-1,
                          allow_small_or_imprecise_dtypes=True).then_inc(s_node, 1)
                pool.memset(zeros[:, :], 0.0).then_inc(s_node, 1)

                def gather(s):
                    for j in range(J):
                        pool.indirect_dma_start(
                            out=gkv[:, s, j, :], out_offset=None, in_=m.gather_kv,
                            in_offset=bass.IndirectOffsetOnAxis(ap=index[:, s, j:j + 1], axis=0)
                        ).then_inc(s_got[s], 16)

                def low_part(g, s):
                    pool.wait_ge(s_mid, g + 1)
                    for own, part in ((gkv[:, s, :, C:2 * C], parts[s % 2][:, :, :, 0:C]),
                                      (weight[:, s % 2, :, :], parts[s % 2][:, :, :, C:W])):
                        ins = pool.tensor_tensor(part[:, 2, :, :], own, part[:, 1, :, :], ALU.subtract)
                    ins.then_inc(s_low, 1)

                pool.wait_ge(s_index, SLOTS)
                for s in range(SLOTS):
                    gather(s)
                low_part(0, 0)
                with pool.Fori(0, G // SLOTS) as i:
                    for s in range(SLOTS):
                        n = i * SLOTS + s
                        low_part(n + 1, (s + 1) % SLOTS)
                        pool.wait_ge(s_index, n + SLOTS + 1)
                        pool.sem_inc(s_pace, 1)
                        gather(s)

            @block.sync
            def _(sp):
                sp.dma_start(q16.rearrange("p t k c -> p t (k c)"),
                             m.gather_q.rearrange("(t p) n -> p t n", p=R)).then_inc(s_q, 16)

                def load(g, s):
                    sp.dma_start(dsts[:, s, :],
                                 dst[bass.ds(g * (J * R), J * R)].unsqueeze(0).broadcast_to([R, J * R]))\
                        .then_inc(s_dst[s], 16)

                for s in range(2):
                    load(s, s)
                with sp.Fori(0, G // 2 - 1) as i:
                    for s in range(2):
                        sp.wait_ge(s_dfree, i * 2 + (s + 1))
                        load(i * 2 + (s + 2), s)
                for g in range(G, GP):
                    sp.wait_ge(s_dfree, g - 1)
                    load(g - G, g % 2)

            @block.scalar
            def _(act):
                def one_hots(g, i, s, bounds):
                    first, count, before = bounds
                    act.wait_ge(s_dst[s], (i + 1) * 16)
                    act.sem_inc(s_pace, 1)
                    with act.Fori(0, count) as k:
                        visit = act.snap(before + k)
                        tile = act.snap(nc.s_assert_within(first + k, 0, T - 1))
                        act.wait_ge(s_pick, visit + AHEAD)
                        act.sem_inc(s_pace, 1)
                        act.activation(apart[:, :], dsts[:, s, :], ACT.Square,
                                       bias=minus_node[:, bass.ds(tile, 1)]).then_inc(s_apart, 1)
                        act.wait_ge(s_apart, visit + 1)
                        act.wait_ge(s_pickv, visit + 1)
                        act.sem_inc(s_pace, 1)
                        act.activation(pick[:, visit % PICKS, :], apart[:, :], ACT.Relu, bias=m.ones[0:R, 0:1],
                                       scale=-1.0).then_inc(s_pick, 1)
                    act.sem_inc(s_dfree, 1)

                def weights(g, p):
                    act.wait_ge(s_score, g + 1)
                    act.activation(weight[:, p, :, :], score[:, :].rearrange("p (j h) -> p j h", j=J), ACT.Exp)\
                        .then_inc(s_exp, 1)

                def part(g, s, k, after, done):
                    act.wait_ge(after, g + 1)
                    act.activation(parts[s % 2][:, k, :, 0:C], gkv[:, s, :, C:2 * C], ACT.Copy)
                    act.activation(parts[s % 2][:, k, :, C:W], weight[:, s % 2, :, :], ACT.Copy).then_inc(done, 1)

                act.wait_ge(s_node, 3)
                one_hots(0, 0, 0, group_bounds(act, m, 0))
                one_hots(1, 0, 1, group_bounds(act, m, 1))
                weights(0, 0)
                part(0, 0, 0, s_spread, s_high)
                one_hots(2, 1, 0, group_bounds(act, m, 2))
                with act.Fori(0, G // SLOTS) as i:
                    for s in range(SLOTS):
                        n = i * SLOTS + s
                        bounds = group_bounds(act, m, n + 3)
                        part(n, s, 1, s_rest, s_mid)
                        weights(n + 1, (s + 1) % 2)
                        part(n + 1, (s + 1) % SLOTS, 0, s_spread, s_high)
                        one_hots(n + 3, i * 2 + (s + 3) // 2, (s + 3) % 2, bounds)
                part(G, 0, 1, s_rest, s_mid)

            @block.tensor
            def _(pe):
                def pick_q(g, bounds):
                    first, count, before = bounds
                    if not isinstance(g, int) or g > 0:
                        pe.wait_ge(s_qk, g)
                        pe.sem_inc(s_pace, 1)
                    anything = q16[:, 0, :, :].rearrange("p k c -> p (k c)")
                    for b in range(3):
                        n = min(512, J * C - b * 512)
                        pe.matmul(picked[:, b, 0:n], zeros[:, :], anything[:, 0:n], start=True, stop=False)
                    with pe.Fori(0, count) as k:
                        visit = pe.snap(before + k)
                        tile = pe.snap(nc.s_assert_within(first + k, 0, T - 1))
                        pe.wait_ge(s_pick, visit + 1 + AHEAD)
                        pe.sem_inc(s_pace, 1)
                        for j in range(J):
                            at = j % 2 * C
                            for p in range(2):
                                ins = pe.matmul(picked[:, j // 2, at:at + C], pick[:, visit % PICKS, j * R:(j + 1) * R],
                                                q16[:, tile, p, :], start=False, stop=False)
                        ins.then_inc(s_pickv, 1)
                    for b in range(3):
                        ins = pe.matmul(picked[:, b, 0:1], zeros[:, :], anything[:, 0:1], start=False, stop=True)
                    ins.then_inc(s_picked, 1)

                pe.wait_ge(s_q, 16)
                pe.wait_ge(s_zero, 2)
                pe.wait_ge(s_node, 3)
                pick_q(0, group_bounds(pe, m, 0))
                pick_q(1, group_bounds(pe, m, 1))
                with pe.Fori(0, G // 2) as i:
                    for s in range(2):
                        n = i * 2 + s
                        ahead = group_bounds(pe, m, n + 2)
                        first, count, before = group_bounds(pe, m, n)
                        pick_q(n + 2, ahead)
                        pe.wait_ge(s_low, n + 1)
                        pe.sem_inc(s_pace, 1)
                        with pe.Fori(0, count) as k:
                            visit = pe.snap(before + k)
                            pe.wait_ge(s_hot, visit + 1)
                            pe.wait_ge(s_added, visit + 1)
                            pe.sem_inc(s_pace, 1)
                            for j in range(J):
                                for p in range(3):
                                    ins = pe.matmul(total[:, visit % RING, 0:W], hot[:, visit % RING, j, :],
                                                    parts[s][:, p, j, :], start=(j + p == 0), stop=(j + p == J + 1))
                            ins.then_inc(s_total, 1)

            @block.vector
            def _(dve):
                v = Chain(dve, s_v)

                def scores(g, i, s):
                    dve.wait_ge(s_got[s], (i + 1) * (16 * J))
                    dve.wait_ge(s_picked, g + 1)
                    dve.tensor_tensor(qk[:, :].rearrange("p (j c) -> p j c", j=J),
                                      picked[:, :, :].rearrange("p b c -> p (b c)")[:, 0:J * C]
                                      .rearrange("p (j c) -> p j c", j=J), gkv[:, s, :, 0:C], ALU.mult)\
                        .then_inc(s_qk, 1)
                    dve.wait_ge(s_qk, g + 1)
                    v.link(dve.tensor_reduce(score[:, :], qk[:, :].rearrange("p (k d) -> p k d", d=HD), AX_X, ALU.add))
                    v.link(dve.tensor_scalar(score[:, :], score[:, :], HD ** -0.5, 10.0, ALU.mult, ALU.min))
                    dve.tensor_scalar(score[:, :], score[:, :], -10.0, None, ALU.max).then_inc(s_score, 1)

                def weigh(g, s):
                    dve.wait_ge(s_exp, g + 1)
                    rows = gkv[:, s, :, C:2 * C].rearrange("p j (h d) -> p j h d", h=X8)
                    dve.tensor_tensor(rows, rows, repeat_last(weight[:, s % 2, :, :], HD), ALU.mult)\
                        .then_inc(s_spread, 1)

                def rest(g, s):
                    dve.wait_ge(s_high, g + 1)
                    for own, part in ((gkv[:, s, :, C:2 * C], parts[s % 2][:, 0, :, 0:C]),
                                      (weight[:, s % 2, :, :], parts[s % 2][:, 0, :, C:W])):
                        ins = dve.tensor_tensor(own, own, part, ALU.subtract)
                    ins.then_inc(s_rest, 1)

                def next_index(g, s):
                    nxt = m.edge_src[:, bass.ds(g + SLOTS, 1), :].rearrange("p a j -> p (a j)")
                    dve.tensor_copy(index[:, s, :], nxt).then_inc(s_index, 1)

                for s in range(SLOTS):
                    dve.tensor_copy(index[:, s, :], m.edge_src[:, s, :]).then_inc(s_index, 1)
                dve.memset(summed[:, :, :], 0.0).then_inc(s_zero, 1)
                dve.memset(total[:, :, :], 0.0).then_inc(s_zero, 1)
                dve.wait_ge(s_zero, 2)
                dve.wait_ge(s_node, 3)
                scores(0, 0, 0)
                weigh(0, 0)
                rest(0, 0)
                adder = Adder(nc, dve, "as", summed, total, s_total, s_added)
                with dve.Fori(0, G // SLOTS) as i:
                    v.enter(i, SLOTS * 2)
                    for s in range(SLOTS):
                        n = i * SLOTS + s
                        first, count, before = group_bounds(dve, m, n)
                        scores(n + 1, i + (s + 1) // SLOTS, (s + 1) % SLOTS)
                        dve.wait_ge(s_total, before + LAG)
                        dve.sem_inc(s_pace, 1)
                        weigh(n + 1, (s + 1) % SLOTS)
                        with dve.Fori(0, count) as k:
                            visit = dve.snap(before + k)
                            tile = dve.snap(nc.s_assert_within(first + k, 0, T - 1))
                            dve.tensor_tensor(hot[:, visit % RING, :, :],
                                              repeat_mid(node_no[:, bass.ds(tile * R, R)], J),
                                              repeat_last(m.edge_dst[:, n, :], R), ALU.is_equal)\
                                .then_inc(s_hot, 1)
                            adder.add(visit, tile)
                        dve.wait_ge(s_low, n + 1)
                        next_index(n, s)
                        rest(n + 1, (s + 1) % SLOTS)
                v.leave(G // SLOTS)
                adder.finish(dve.snap(before + count), s_pace)
                for s in range(SLOTS):
                    dve.wait_ge(s_got[s], (G // SLOTS + 1) * (16 * J))
                dve.wait_ge(s_low, G + 1)
                dve.wait_ge(s_picked, G + 2)
                den = summed[:, :, C:W]
                v.link(dve.tensor_scalar(none[:, :, :], den, 0.0, None, ALU.is_equal))
                v.link(dve.tensor_tensor(none[:, :, :], none[:, :, :], den, ALU.add))
                v.link(dve.reciprocal(none[:, :, :], none[:, :, :]))
                with dve.Fori(0, CHUNKS) as c:
                    for t in (c * J + j for j in range(J)):
                        dve.tensor_tensor(m.y[:, t, :].rearrange("p (h d) -> p h d", h=X8),
                                          summed[:, t, 0:C].rearrange("p (h d) -> p h d", h=X8),
                                          repeat_last(none[:, t, :], HD), ALU.mult).then_inc(s_zero, 1)
                dve.wait_ge(s_zero, T + 2)


def attention_out(nc, m):
    with phase(nc, "ao") as ph:
        w = ph.sb("w", [128, CB, C])
        rows = ph.sb("rows", [R, J, C])
        cols = ph.sb("cols", [128, J, CB, R])
        turned = ph.ps("turned", [128, 4, 512])
        bank = ph.ps("bank", [R, 4, 512])
        s_w, s_rows, s_turned, s_cols, s_prod, s_y, s_bias, s_added = (
            ph.sem(x) for x in ("w", "rows", "turned", "cols", "prod", "y", "bias", "added"))
        bp, b2 = m.row["L1_gnn_bp"], m.row["L1_gnn_b2"]
        ph.ahead(s_cols, s_prod, s_turned, s_y)
        with nc.Block() as block:

            @block.gpsimd
            def _(pool):
                with pool.Fori(0, CHUNKS) as c:
                    for rows_, bias in ((m.z, bp), (m.x, b2)):
                        some = rows_[:, bass.ds(c * J, J), :]
                        ins = pool.tensor_tensor(some, some, repeat_mid(bias, J), ALU.add)
                    ins.then_inc(s_bias, 1)

            @block.sync
            def _(sp):
                sp.dma_start(w[:, :, :], m.turned["wp"].rearrange("(b p) n -> p b n", p=128)).then_inc(s_w, 16)

            @block.scalar
            def _(act):
                with act.Fori(0, CHUNKS) as c:
                    act.wait_ge(s_turned, c * J + AHEAD)
                    act.activation(rows[:, :, :], m.y[:, bass.ds(c * J, J), :], ACT.Copy).then_inc(s_rows, 1)
                    for j in range(J):
                        act.wait_ge(s_turned, c * J + (j + 1) + AHEAD)
                        if j == 0:
                            act.wait_ge(s_prod, c * J + AHEAD)
                        act.activation(cols[:, j, :, :].rearrange("p b r -> p (b r)"), turned[:, j % 4, 0:CB * R],
                                       ACT.Copy).then_inc(s_cols, 1)

            @block.tensor
            def _(pe):
                pe.wait_ge(s_w, 16)
                with pe.Fori(0, CHUNKS) as c:
                    pe.wait_ge(s_rows, c + 1)
                    for j in range(J):
                        pe.wait_ge(s_cols, c * J + max(j - 3, 0) + AHEAD)
                        for b in range(CB):
                            ins = pe.transpose(turned[:, j % 4, b * R:(b + 1) * R], rows[:, j, b * 128:(b + 1) * 128],
                                               m.ident[0:R, 0:R])
                        ins.then_inc(s_turned, 1)
                    for j in range(J):
                        pe.wait_ge(s_cols, c * J + (j + 1) + AHEAD)
                        pe.wait_ge(s_y, c * J + max(j - 3, 0) + AHEAD)
                        for b in range(CB):
                            ins = pe.matmul(bank[:, j % 4, 0:C], cols[:, j, b, :], w[:, b, :],
                                            start=(b == 0), stop=(b == CB - 1))
                        ins.then_inc(s_prod, 1)

            @block.vector
            def _(dve):
                with dve.Fori(0, CHUNKS) as c:
                    for j in range(J):
                        if j == 0:
                            dve.wait_ge(s_bias, c + 1)
                        dve.wait_ge(s_prod, c * J + (j + 1) + AHEAD)
                        dve.tensor_tensor(m.y[:, c * J + j, :], bank[:, j % 4, 0:C], m.z[:, c * J + j, :], ALU.add)\
                            .then_inc(s_y, 1)
                    dve.wait_ge(s_y, (c + 1) * J + AHEAD)
                    x, y = (rows[:, bass.ds(c * J, J), :] for rows in (m.x, m.y))
                    dve.tensor_tensor(x, x, y, ALU.add).then_inc(s_added, 1)

C3 = 3 * C
OB = C3 // 128
CAT = 2 * C3
GW = 3 * HD
GN = CAT // GW
CO = GN * HD
BALL = 0.99999
MIN_NORM = 1e-15


def ball_log_rows(nc, m):
    with phase(nc, "bl") as ph:
        square = ph.sb("square", [R, J, C])
        n2 = ph.sb("n2", [R, T])
        norm, inv, c_, u, w, lnw, one = (ph.sb(x, [R, T]) for x in ("norm", "inv", "c", "u", "w", "lnw", "one"))
        rows = ph.sb("rows", [R, J, C])
        turned = ph.ps("turned", [128, J, 512])
        s_sq, s_norm, s_w, s_ln, s_v = (ph.sem(x) for x in ("sq", "norm", "w", "ln", "v"))
        s_rows, s_turned, s_out, s_pace = (ph.sem(x) for x in ("rows", "turned", "out", "pace"))
        ph.ahead(s_out, s_sq, s_turned)
        with nc.Block() as block:

            @block.scalar
            def _(act):
                with act.Fori(0, CHUNKS) as c:
                    for j in range(J):
                        act.wait_ge(s_sq, c * J + AHEAD)
                        act.sem_inc(s_pace, 1)
                        act.activation(square[:, j, :], m.z[:, c * J + j, :], ACT.Square,
                                       accum_out=n2[:, bass.ds(c * J + j, 1)]).then_inc(s_sq, 1)
                act.wait_ge(s_sq, T + AHEAD)
                act.activation(norm[:, :], n2[:, :], ACT.Sqrt).then_inc(s_norm, 1)
                act.wait_ge(s_w, 1)
                act.activation(lnw[:, :], w[:, :], ACT.Ln).then_inc(s_ln, 1)
                with act.Fori(0, CHUNKS) as c:
                    for j in range(J):
                        act.wait_ge(s_turned, c * J + (j + 1) + AHEAD)
                        act.activation(m.z_cols[:, :, bass.ds(c * COLS + j * R, R)],
                                       turned[:, j, 0:CB * R].rearrange("p (b r) -> p b r", b=CB), ACT.Copy)\
                            .then_inc(s_out, 1)

            @block.vector
            def _(dve):
                v = Chain(dve, s_v)
                dve.wait_ge(s_norm, 1)
                v.link(dve.tensor_scalar(norm[:, :], norm[:, :], MIN_NORM, None, ALU.max))
                v.link(dve.reciprocal(inv[:, :], norm[:, :]))
                v.link(dve.tensor_scalar(c_[:, :], norm[:, :], BALL, None, ALU.min))
                v.link(dve.tensor_scalar(u[:, :], c_[:, :], -1.0, 1.0, ALU.mult, ALU.add))
                v.link(dve.reciprocal(u[:, :], u[:, :]))
                v.link(dve.scalar_tensor_tensor(out=u[:, :], in0=u[:, :], scalar=2.0, in1=c_[:, :],
                                                op0=ALU.mult, op1=ALU.mult))
                v.link(dve.tensor_scalar(w[:, :], u[:, :], 1.0, None, ALU.add))
                v.done(s_w)
                v.link(dve.tensor_scalar(one[:, :], w[:, :], 1.0, None, ALU.is_equal))
                v.link(dve.scalar_tensor_tensor(out=c_[:, :], in0=w[:, :], scalar=-1.0, in1=one[:, :],
                                                op0=ALU.add, op1=ALU.add))
                v.link(dve.reciprocal(c_[:, :], c_[:, :]))
                dve.wait_ge(s_ln, 1)
                v.link(dve.tensor_tensor(lnw[:, :], lnw[:, :], one[:, :], ALU.add))
                v.link(dve.tensor_tensor(lnw[:, :], lnw[:, :], c_[:, :], ALU.mult))
                v.link(dve.tensor_tensor(lnw[:, :], lnw[:, :], u[:, :], ALU.mult))
                v.link(dve.scalar_tensor_tensor(out=inv[:, :], in0=lnw[:, :], scalar=0.5, in1=inv[:, :],
                                                op0=ALU.mult, op1=ALU.mult))
                with dve.Fori(0, CHUNKS) as c:
                    dve.wait_ge(s_turned, c * J + AHEAD)
                    for j in range(J):
                        dve.tensor_scalar(rows[:, j, :], m.z[:, c * J + j, :], inv[:, bass.ds(c * J + j, 1)], None,
                                          ALU.mult).then_inc(s_rows, 1)

            @block.tensor
            def _(pe):
                with pe.Fori(0, CHUNKS) as c:
                    pe.wait_ge(s_out, c * J + AHEAD)
                    for j in range(J):
                        pe.wait_ge(s_rows, c * J + (j + 1))
                        for b in range(CB):
                            ins = pe.transpose(turned[:, j, b * R:(b + 1) * R], rows[:, j, b * 128:(b + 1) * 128],
                                               m.ident[0:R, 0:R])
                        ins.then_inc(s_turned, 1)


def ball_mixer(nc, m, a):
    import math
    reach = math.atanh(BALL)
    with phase(nc, "bm") as ph:
        wc = ph.sb("wc", [128, CB, C3])
        fx = ph.sb("fx", [128, J, C])
        pw = fx[:, 0, 0:OB * HD].rearrange("p (o i) -> p o i", o=OB)
        diag = fx[:, 1, 0:128]
        mine = fx[:, 2, 0:128].rearrange("p (g i) -> p g i", i=HD)
        branch = ph.sb("branch", [128, OB, 128])
        wr = ph.sb("wr", [128, CO // 128, C])
        y = ph.sb("y", [128, OB, N])
        junk = ph.sb("junk", [128, C3])
        stats = junk[:, 0:OB * CHUNKS * 12].rearrange("p (o n k) -> p o n k", o=OB, k=6)
        mv = ph.sb("mv", [128, OB, 2])
        scale = ph.sb("scale", [128, OB])
        shift = ph.sb("shift", [128, OB])
        act_c = ph.sb("act_c", [128, 2, OB, R])
        cat = [m.z_cols[0:R, j // 2, (j % 2) * CAT:(j % 2 + 1) * CAT] for j in range(J - 1)]
        cat.append(wc[0:R, :, :].rearrange("p b n -> p (b n)"))
        cat = [k.rearrange("p (w c) -> p w c", w=2) for k in cat]
        s2 = ph.sb("s2", [R, 4, J])
        nr = ph.sb("nr", [R, 9, J])
        qk = ph.sb("qk", [R, GN, 2 * HD])
        val = ph.sb("val", [R, 2, GN, HD])
        ksum = ph.sb("ksum", [R, GN])
        o_cols = ph.sb("o_cols", [128, CO // 128, R])
        up = ph.ps("up", [128, 6, 512])
        obank = ph.ps("obank", [128, 512])
        fbank = ph.ps("fbank", [R, 512])
        s_w, s_mask, s_diag, s_turn, s_both = (ph.sem(x) for x in ("w", "mask", "diag", "turn", "both"))
        s_up, s_y, s_stats, s_sd, s_bn, s_v, s_pace = (ph.sem(x) for x in ("up", "y", "stats", "sd", "bn", "v", "pace"))
        s_act, s_cat, s_catr, s_catsq, s_used, s_sum, s_norm = (
            ph.sem(x) for x in ("act", "cat", "catr", "catsq", "used", "sum", "norm"))
        s_o, s_ot, s_oc, s_osq, s_f, s_raw, s_norm2 = (ph.sem(x) for x in ("o", "ot", "oc", "osq", "f", "raw", "norm2"))
        s_fx, s_tanh, s_done, s_a, s_sq4, s_summed = (
            ph.sem(x) for x in ("fx", "tanh", "done", "a", "sq4", "summed"))
        units = OB * len(HALVES)
        col = m.col
        ph.ahead(s_cat, s_catr, s_oc, s_ot, s_raw, s_y, s_done, s_norm2)
        with nc.Block() as block:

            @block.gpsimd
            def _(pool):
                pool.memset(mine[:, :, :], 1.0).then_inc(s_mask, 1)
                pool.wait_ge(s_mask, 1)
                pool.affine_select(out=mine[:, :, :], in_=mine[:, :, :], compare_op=ALU.is_ge, fill=0.0, base=0,
                                   pattern=[[-HD, 4], [0, HD]], channel_multiplier=1).then_inc(s_mask, 1)
                pool.wait_ge(s_mask, 2)
                pool.affine_select(out=mine[:, :, :], in_=mine[:, :, :], compare_op=ALU.is_ge, fill=0.0,
                                   base=HD - 1, pattern=[[HD, 4], [0, HD]], channel_multiplier=-1).then_inc(s_mask, 1)
                with pool.Fori(0, CHUNKS) as c:
                    for j in range(J):
                        pool.wait_ge(s_used, c * J + (j + 1))
                        out = val[:, j % 2, :, :]
                        pool.tensor_tensor(out, out, repeat_last(ksum[:, :], HD), ALU.mult).then_inc(s_summed, 1)

            @block.sync
            def _(sp):
                sp.dma_start(pw[:, :, :], a["L1_mix_w_pw"].rearrange("(b p) i k -> p b (i k)", p=128)).then_inc(s_w, 16)
                sp.dma_start(wc[:, :, :], m.turned["conv"].rearrange("(b p) n -> p b n", p=128)).then_inc(s_w, 16)
                sp.dma_start(wr[:, :, :], m.turned["res"].rearrange("(b p) n -> p b n", p=128)).then_inc(s_w, 16)

            @block.tensor
            def _(pe):
                for o in range(OB):
                    pe.wait_ge(s_diag, o + 1)
                    pe.transpose(obank[:, 0:128], diag[:, :], m.ident[:, :]).then_inc(s_turn, 1)
                pe.wait_ge(s_both, OB)
                pe.wait_ge(s_w, 48)
                pe.sem_inc(s_pace, 1)
                with pe.Fori(0, CHUNKS) as c:
                    for u in range(units):
                        o, (at, n) = u // 2, HALVES[u % 2]
                        pe.wait_ge(s_y, (c * units + (u - 3) if u > 3 else c * units) + AHEAD)
                        for b in range(CB):
                            ins = pe.matmul(up[:, u % 4, 0:n], wc[:, b, o * 128:(o + 1) * 128],
                                            m.z_cols[:, b, bass.ds(c * COLS + at, n)],
                                            start=(b == 0), stop=(b == CB - 1))
                        ins.then_inc(s_up, 1)

                def join(t, j):
                    pe.wait_ge(s_act, t + 1)
                    pe.wait_ge(s_catr, t - min(j, 1) + AHEAD)
                    for o in range(OB):
                        bank, at = j % 2 * 3 + o // 2, (o % 2) * 256
                        pe.transpose(up[0:R, bank, at:at + 128], act_c[:, j % 2, o, :], m.ident[:, :])
                        ins = pe.matmul(up[0:R, bank, at + 128:at + 256], act_c[:, j % 2, o, :], branch[:, o, :],
                                        start=True, stop=True)
                    ins.then_inc(s_cat, 1)

                def chunk(c, more):
                    for j in range(J):
                        t = c * J + j
                        pe.wait_ge(s_o, t + 1)
                        pe.wait_ge(s_oc, t + AHEAD)
                        rows = val[:, j % 2, :, :].rearrange("p g d -> p (g d)")
                        for b in range(CO // 128):
                            ins = pe.transpose(obank[:, b * R:(b + 1) * R], rows[:, b * 128:(b + 1) * 128],
                                               m.ident[0:R, 0:R])
                        ins.then_inc(s_ot, 1)
                        if more:
                            join((c + 1) * J + j, j)
                        pe.wait_ge(s_oc, t + 1 + AHEAD)
                        pe.wait_ge(s_raw, t + AHEAD)
                        for b in range(CO // 128):
                            ins = pe.matmul(fbank[:, 0:C], o_cols[:, b, :], wr[:, b, :],
                                            start=(b == 0), stop=(b == CO // 128 - 1))
                        ins.then_inc(s_f, 1)

                for j in range(J):
                    join(j, j)
                with pe.Fori(0, CHUNKS - 1) as c:
                    chunk(c, True)
                chunk(CHUNKS - 1, False)

            @block.scalar
            def _(act):
                with act.Fori(0, CHUNKS) as c:
                    for u in range(units):
                        o, (at, n) = u // 2, HALVES[u % 2]
                        act.wait_ge(s_up, c * units + (u + 1))
                        act.activation(y[:, o, bass.ds(c * COLS + at, n)], up[:, u % 4, 0:n], ACT.Copy)\
                            .then_inc(s_y, 1)
                act.wait_ge(s_stats, 1)
                act.activation(scale[:, :], mv[:, :, 1], ACT.Sqrt, bias=m.eps[:, :]).then_inc(s_sd, 1)
                act.wait_ge(s_bn, 1)
                a_ = Chain(act, s_a)

                def relu(t, j):
                    act.wait_ge(s_cat, t - min(j, 1) + AHEAD)
                    act.sem_inc(s_pace, 1)
                    for o in range(OB):
                        ins = act.activation(act_c[:, j % 2, o, :], y[:, o, bass.ds(t * R, R)], ACT.Relu,
                                             bias=shift[:, o:o + 1], scale=scale[:, o:o + 1])
                    ins.then_inc(s_act, 1)

                def read(t, j):
                    act.wait_ge(s_cat, t + 1 + AHEAD)
                    bank = up[0:R, j % 2 * 3:j % 2 * 3 + 3, :].rearrange("p a (b w c) -> p (a b) w c", b=2, w=2)
                    act.activation(cat[j].rearrange("p w (o c) -> p o w c", o=OB), bank, ACT.Copy)\
                        .then_inc(s_catr, 1)
                    act.wait_ge(s_catr, t + 1 + AHEAD)
                    for k in range(2):
                        a_.link(act.activation(junk[0:R, :], cat[j][:, k, :], ACT.Square, accum_out=s2[:, k, j:j + 1]))
                    act.sem_inc(s_catsq, 1)

                def chunk(c, more):
                    act.wait_ge(s_sum, c + 1)
                    act.activation(nr[:, 0:2, :], s2[:, 0:2, :], ACT.Sqrt).then_inc(s_norm, 1)
                    if more:
                        relu((c + 1) * J, 0)
                    for j in range(J):
                        t = c * J + j
                        act.wait_ge(s_ot, t + 1 + AHEAD)
                        if j:
                            act.wait_ge(s_f, t)
                        act.activation(o_cols[:, :, :].rearrange("p b r -> p (b r)"), obank[:, 0:CO // 128 * R],
                                       ACT.Copy).then_inc(s_oc, 1)
                        if more and j < J - 1:
                            relu((c + 1) * J + j + 1, j + 1)
                        a_.link(act.activation(junk[0:R, 0:CO], val[:, j % 2, :, :].rearrange("p g d -> p (g d)"),
                                               ACT.Square, accum_out=s2[:, 2, j:j + 1]))
                        act.sem_inc(s_osq, 1)
                        if more:
                            act.wait_ge(s_used, t + 1)
                            read((c + 1) * J + j, j)
                        act.wait_ge(s_f, t + 1)
                        if j == 0:
                            act.wait_ge(s_done, c + AHEAD)
                        act.activation(fx[0:R, j, :], fbank[:, 0:C], ACT.Copy).then_inc(s_raw, 1)
                    act.wait_ge(s_osq, (c + 1) * J)
                    act.activation(nr[:, 2, :], s2[:, 2, :], ACT.Sqrt).then_inc(s_norm2, 1)
                    for j in range(J):
                        act.wait_ge(s_fx, c * J + (j + 1))
                        a_.link(act.activation(junk[0:R, 0:C], fx[0:R, j, :], ACT.Square, accum_out=s2[:, 3, j:j + 1]))
                    a_.link(act.activation(nr[:, 3, :], s2[:, 3, :], ACT.Sqrt))
                    act.activation(nr[:, 4, :], nr[:, 3, :], ACT.Tanh).then_inc(s_tanh, 1)

                relu(0, 0)
                for j in range(J):
                    if j < J - 1:
                        relu(j + 1, j + 1)
                    read(j, j)
                with act.Fori(0, CHUNKS - 1) as c:
                    a_.enter(c, 4 * J + 1)
                    chunk(c, True)
                a_.leave(CHUNKS - 1)
                chunk(CHUNKS - 1, False)

            @block.vector
            def _(dve):
                v = Chain(dve, s_v)
                dve.wait_ge(s_w, 48)
                dve.wait_ge(s_mask, 3)
                for o in range(OB):
                    if o:
                        dve.wait_ge(s_turn, o)
                    dve.tensor_tensor(diag[:, :].rearrange("p (g i) -> p g i", i=HD), repeat_mid(pw[:, o, :], 4),
                                      mine[:, :, :], ALU.mult).then_inc(s_diag, 1)
                    dve.wait_ge(s_turn, o + 1)
                    dve.tensor_scalar(branch[:, o, :], obank[:, 0:128], col["L1_mix_w_dw"][:, o:o + 1], None,
                                      ALU.mult).then_inc(s_both, 1)
                with dve.Fori(0, CHUNKS) as c:
                    for u in range(units):
                        o, (at, n) = u // 2, HALVES[u % 2]
                        dve.wait_ge(s_y, c * units + (u + 1) + AHEAD)
                        ins = dve.bn_stats(stats[:, o, c * 2 + u % 2, :], y[:, o, bass.ds(c * COLS + at, n)])
                        ins.then_inc(s_sq4, 1)
                dve.wait_ge(s_sq4, CHUNKS * units)
                for o in range(OB):
                    ins = dve.bn_aggr(mv[:, o, :], stats[:, o, :, :].rearrange("p n k -> p (n k)"))
                v.link(ins)
                v.done(s_stats)
                dve.wait_ge(s_sd, 1)
                v.link(dve.reciprocal(scale[:, :], scale[:, :]))
                v.link(dve.tensor_tensor(scale[:, :], scale[:, :], col["L1_mix_bn_gamma"], ALU.mult))
                v.link(dve.tensor_tensor(shift[:, :], mv[:, :, 0], scale[:, :], ALU.mult))
                v.link(dve.tensor_tensor(shift[:, :], col["L1_mix_bn_beta"], shift[:, :], ALU.subtract))
                v.done(s_bn)

                def radial(n, k):
                    v.link(dve.tensor_scalar(nr[:, n, :], nr[:, n, :], MIN_NORM, None, ALU.max))
                    v.link(dve.reciprocal(nr[:, k, :], nr[:, n, :]))
                    v.link(dve.scalar_tensor_tensor(out=nr[:, k, :], in0=nr[:, n, :], scalar=reach,
                                                    in1=nr[:, k, :], op0=ALU.min, op1=ALU.mult))

                with dve.Fori(0, CHUNKS) as c:
                    v.enter(c, 9 + 6 * J + 6)
                    dve.wait_ge(s_catsq, (c + 1) * J)
                    v.link(dve.tensor_tensor(s2[:, 1, :], s2[:, 0, :], s2[:, 1, :], ALU.add))
                    v.done(s_sum)
                    dve.wait_ge(s_norm, c + 1)
                    radial(0, 5)
                    v.link(dve.tensor_tensor(nr[:, 1, :], nr[:, 1, :], nr[:, 5, :], ALU.mult))
                    radial(1, 6)
                    v.link(dve.tensor_tensor(nr[:, 6, :], nr[:, 6, :], nr[:, 5, :], ALU.mult))

                    for j in range(J):
                        t = c * J + j
                        groups = cat[j].rearrange("p a c -> p (a c)").rearrange("p (g w) -> p g w", w=GW)
                        gamma = nr[:, 6, j:j + 1]
                        out, turn = val[:, j % 2, :, :], qk[:, :, HD:2 * HD]
                        v.link(dve.tensor_scalar(qk[:, :, :], groups[:, :, 0:2 * HD], gamma, 0.0, ALU.mult, ALU.max))
                        v.link(dve.tensor_reduce(ksum[:, :], turn, AX_X, ALU.add))
                        v.link(dve.tensor_scalar(turn, groups[:, :, 2 * HD:GW], gamma, 1e-15, ALU.mult, ALU.add))
                        dve.wait_ge(s_ot, t - min(j, 1) + AHEAD)
                        if j > 1:
                            dve.wait_ge(s_osq, t - 1)
                        elif j == 0:
                            dve.wait_ge(s_norm2, c + AHEAD)
                        v.link(dve.scalar_tensor_tensor(out=out, in0=groups[:, :, 2 * HD:GW], scalar=gamma,
                                                        in1=qk[:, :, 0:HD], op0=ALU.mult, op1=ALU.mult))
                        v.done(s_used)
                        v.link(dve.reciprocal(turn, turn))
                        dve.wait_ge(s_summed, t + 1)
                        v.link(dve.tensor_tensor(out, out, turn, ALU.mult))
                        v.done(s_o)
                    dve.wait_ge(s_norm2, c + 1 + AHEAD)
                    radial(2, 7)
                    for j in range(J):
                        dve.wait_ge(s_raw, c * J + (j + 1) + AHEAD)
                        dve.scalar_tensor_tensor(out=fx[0:R, j, :], in0=fx[0:R, j, :], scalar=nr[:, 7, j:j + 1],
                                                 in1=m.row["L1_mix_b_res"], op0=ALU.mult, op1=ALU.add)\
                            .then_inc(s_fx, 1)
                    dve.wait_ge(s_tanh, c + 1)
                    v.link(dve.tensor_scalar(nr[:, 3, :], nr[:, 3, :], MIN_NORM, None, ALU.max))
                    v.link(dve.reciprocal(nr[:, 3, :], nr[:, 3, :]))
                    v.link(dve.scalar_tensor_tensor(out=nr[:, 8, :], in0=nr[:, 4, :], scalar=BALL, in1=nr[:, 3, :],
                                                    op0=ALU.min, op1=ALU.mult))
                    for j in range(J):
                        t = c * J + j
                        ins = dve.scalar_tensor_tensor(out=m.x[:, t, :], in0=fx[0:R, j, :], scalar=nr[:, 8, j:j + 1],
                                                       in1=m.x[:, t, :], op0=ALU.mult, op1=ALU.add)
                    ins.then_inc(s_done, 1)
                v.leave(CHUNKS)


class Memory:
    pass


def graph_layers(nc, a, out):
    m = Memory()
    with ExitStack() as stack:
        def sb(name, shape, dt=F32):
            return stack.enter_context(nc.sbuf_tensor(name, shape, dt))

        m.ident = sb("ident", [128, 128])
        m.ones = sb("ones", [128, 128])
        m.eps = sb("eps", [128, 1])
        m.before = sb("before", [G, G + 1])
        m.row_no = sb("row_no", [128, R])
        m.tile_starts = sb("tile_starts", [G, T - 1])
        m.edge_dst = sb("edge_dst", [R, G, J])
        m.edge_src = sb("edge_src", [R, G + SLOTS + 1, J], I32)
        m.group_table = sb("group_table", [1, GP], I32)
        m.degree = sb("degree", [R, T])
        m.degree_s = sb("degree_s", [R, 2, T])
        m.inv_sqrt_degree = sb("inv_sqrt_degree", [R, T])
        m.x = sb("x_rows", [R, T, C])
        m.colvec = sb("colvec", [128, 384])
        m.rowvec = sb("rowvec", [R, 10, C])
        m.gate = sb("gate", [R, T, X8])
        m.z = sb("z_rows", [R, T, C])
        m.ident16 = sb("ident16", [128, 128], F16)
        z_flat = sb("z_flat", [128, CB * N])
        m.z_cols = z_flat[:, :].rearrange("p (b n) -> p b n", b=CB)
        m.zc = z_flat[:, :].bitcast(F16).rearrange("p (k b n) -> p k b n", k=2, b=CB)
        m.gather_q = nc.dram_tensor("gather_q", [N, 2 * C], F16).ap()
        m.gather_kv = nc.dram_tensor("gather_kv", [N, 2 * C], F32).ap()
        m.gather0 = nc.dram_tensor("gather0", [N, 2 * C], F16).ap()
        y_stack = ExitStack()

        def take_y(turn):
            m.y = y_stack.enter_context(nc.sbuf_tensor(f"y_rows{turn}", [R, T, C], F32))

        def free_y():
            y_stack.close()

        take_y(0)
        with nc.semaphore("x_in") as s_x:
            with nc.Block() as block:

                @block.sync
                def _(sp):
                    sp.dma_start(m.x[:, :, :], a["x"].rearrange("(t p) n -> p t n", p=R)).then_inc(s_x, 16)

                @block.gpsimd
                def _(pool):
                    pool.memset(m.edge_src[:, :, :], 0)

            constants(nc, m)
            edge_tables(nc, m, a["src"], a["dst"])
            with nc.Block() as block:

                @block.sync
                def _(sp):
                    sp.wait_ge(s_x, 16)
        layernorm(nc, m, "ln0", m.x, m.z)
        scaled_rows(nc, m, a["L0_gnn_W"])
        load_vectors(nc, m, a)
        message_sum(nc, m, a)
        col = m.col
        layernorm_cols(nc, m, "ln1", m.z, None, [(m.z_cols, col["L0_mix_ln1_g"], col["L0_mix_ln1_b"])])
        mixer0(nc, m, a)
        layernorm(nc, m, "ln2", m.y)
        feed_forward(nc, m, "ff0", 1, lambda e: a["L0_mix_W1"], col["L0_mix_b1"], lambda e: a["L0_mix_W2"],
                     gain=col["L0_mix_ln2_g"], bias_in=col["L0_mix_ln2_b"])
        layernorm(nc, m, "ln3", m.x)
        router(nc, m, "ro0", a["L0_ffn_Wr"], m.row["L0_ffn_br"], False, a["L0_ffn_bo"])
        experts0(nc, m, a)
        layernorm(nc, m, "ln4", m.x, m.z)
        query_rows(nc, m, a)
        ball_log_rows(nc, m)
        free_y()
        ball_mixer(nc, m, a)
        take_y(1)
        attention_sum(nc, m, a["dst"])
        attention_out(nc, m)
        layernorm(nc, m, "ln5", m.y)
        feed_forward(nc, m, "ff1", 1, lambda e: m.turned["w1"], col["L1_gnn_b1"], lambda e: m.turned["w2"],
                     gain=col["L1_gnn_ln_g"], bias_in=col["L1_gnn_ln_b"])
        free_y()
        layernorm(nc, m, "ln6", m.x)
        router(nc, m, "ro1", a["L1_ffn_Wr"], None, True, a["L1_ffn_b2p"], m.row["L1_ffn_b2s"])
        feed_forward(nc, m, "ff2", 1, lambda e: a["L1_ffn_W1s"], col["L1_ffn_b1s"], lambda e: a["L1_ffn_W2s"])
        expert = lambda W: lambda e: W[bass.ds(e, 1), :, :].rearrange("e k n -> (e k) n")
        feed_forward(nc, m, "ff3", X8, expert(a["L1_ffn_W1p"]), col["L1_ffn_b1p"], expert(a["L1_ffn_W2p"]), m.gate)
        with nc.semaphore("out") as s_out, nc.Block() as block:

            @block.sync
            def _(sp):
                sp.dma_start(out.rearrange("(t p) n -> p t n", p=R), m.x[:, :, :]).then_inc(s_out, 16)
                sp.wait_ge(s_out, 16)


def kernel(**inputs):
    import numpy as np
    from concourse import bacc
    from concourse.bass_utils import run_bass_kernel_spmd

    nc = bacc.Bacc("TRN2", target_bir_lowering=False, num_devices=1)
    arrays, a = {}, {}
    for name, given in inputs.items():
        array = np.ascontiguousarray(given)
        arrays[f"in_{name}"] = array
        a[name] = nc.dram_tensor(f"in_{name}", array.shape, mybir.dt.from_np(array.dtype),
                                          kind="ExternalInput").ap()
    out = nc.dram_tensor("out", (N, C), F32, kind="ExternalOutput").ap()
    graph_layers(nc, a, out)
    return run_bass_kernel_spmd(nc, [arrays], core_ids=[0]).results[0]["out"]
```
